# Optimizing a Trainium2 kernel written in Bass

```python
import numpy as np
import jax
import jax.numpy as jnp

def _softmax(x, axis=-1):
    return jax.nn.softmax(x, axis=axis)

def _gelu(x):
    return jax.nn.gelu(x, approximate=True)

def _silu(x):
    return jax.nn.silu(x)

def _sigmoid(x):
    return jax.nn.sigmoid(x)

def _layernorm(x, axis=-1, eps=1e-05):
    m = jnp.mean(x, axis=axis, keepdims=True)
    v = jnp.var(x, axis=axis, keepdims=True)
    return (x - m) / jnp.sqrt(v + eps)

def _scatter_add(tgt, idx, src, axis=0):
    return tgt.at[idx].add(src)

def _segment_sum(src, seg, n):
    return jax.ops.segment_sum(src, seg, n)
kernel_name = 'mk_xattn_ffn_d4_seqx_r8_676742'

def setup_inputs(seed: int=0):
    np.random.seed(seed)
    _w = jnp.asarray

    def _rec_inputs():
        import jax
        import jax.numpy as jnp
        _rk = jax.random.key(seed)
        x = 7.22e-05 + 1 * jax.random.normal(jax.random.fold_in(_rk, 1), (16, 128, 256), jnp.float32)
        _lenS = 128 - jax.random.randint(jax.random.fold_in(_rk, 7), (16,), 0, max(1, 128 // 4) + 1, jnp.int32)
        _lenS2 = 128 - jax.random.randint(jax.random.fold_in(_rk, 8), (16,), 0, max(1, 128 // 4) + 1, jnp.int32)
        _ctx_1024P = jax.random.normal(jax.random.fold_in(_rk, 11), (16, 16, 128), jnp.float32)
        _ctx_1024c = jax.random.dirichlet(jax.random.fold_in(_rk, 511), 0.3 * jnp.ones((16,), jnp.float32), (16, 128))
        _ctx_1024t = jnp.einsum('bsk,bkd->bsd', _ctx_1024c, _ctx_1024P)
        _ctx_1024t = _ctx_1024t * jax.lax.rsqrt(jnp.mean(jnp.square(_ctx_1024t)) + 1e-12) * 0.953939
        ctx_1024 = -1.39393e-06 + 0.999914 * (_ctx_1024t + 0.3 * jax.random.normal(jax.random.fold_in(_rk, 611), (16, 128, 128), jnp.float32))
        fside_BxSx2_0 = jax.random.uniform(jax.random.fold_in(_rk, 12), (16, 128, 2), jnp.float32, 0.0, 0.999707)
        _validS = jnp.arange(128)[None, :] < _lenS[:, None]
        _validS2 = jnp.arange(128)[None, :] < _lenS2[:, None]
        _causal = jnp.tril(jnp.ones((128, 128), dtype=bool))
        mask_BxS2_bf1 = jnp.ones((16, 128), dtype=bool)
        return (x, ctx_1024, fside_BxSx2_0, mask_BxS2_bf1)
    x, ctx_1024, fside_BxSx2_0, mask_BxS2_bf1 = _rec_inputs()

    def _L0_xattn_setup():
        import jax, jax.numpy as jnp
        import numpy as np
        DIM = 256
        CTX_DIM = 128
        N_HEADS = 32
        HEAD_DIM = DIM // N_HEADS
        POS_DIM = 2
        B, N, CTXN = (2, 256, 256)
        ROPE_BASE = 10000.0

        def apply_axial_rope(x, pos):
            b, n, h, d = x.shape
            p = pos.shape[-1]
            dpa = d // p
            half = dpa // 2
            freqs = ROPE_BASE ** (-jnp.arange(half, dtype=x.dtype) / half)
            ang = pos[..., :, None] * freqs
            cos = jnp.cos(ang)[:, :, None, :, :]
            sin = jnp.sin(ang)[:, :, None, :, :]
            xr = x.reshape(b, n, h, p, half, 2)
            x1, x2 = (xr[..., 0], xr[..., 1])
            out = jnp.stack([x1 * cos - x2 * sin, x1 * sin + x2 * cos], axis=-1)
            return out.reshape(b, n, h, d)
        key = jax.random.key(seed)
        ks = jax.random.split(key, 8)
        x = jax.random.normal(ks[0], (B, N, DIM), jnp.float32)
        ctx = jax.random.normal(ks[1], (B, CTXN, CTX_DIM), jnp.float32)
        pos_map = jax.random.uniform(ks[2], (B, N, POS_DIM), jnp.float32)
        ctx_pos_map = jax.random.uniform(ks[3], (B, CTXN, POS_DIM), jnp.float32)
        Wq = jax.random.normal(ks[4], (DIM, DIM), jnp.float32) / np.sqrt(DIM)
        Wkv = jax.random.normal(ks[5], (CTX_DIM, 2 * DIM), jnp.float32) / np.sqrt(CTX_DIM)
        Wout = jax.random.normal(ks[6], (DIM, DIM), jnp.float32) / np.sqrt(DIM)
        bout = jnp.zeros((DIM,), jnp.float32)
        return {'x': x, 'ctx': ctx, 'pos_map': pos_map, 'ctx_pos_map': ctx_pos_map, 'Wq': Wq, 'Wkv': Wkv, 'Wout': Wout, 'bout': bout}
    _L0_xattn_all = _L0_xattn_setup()
    _L0_xattn_in = {k: v for k, v in _L0_xattn_all.items() if k in ('Wq', 'Wkv', 'Wout', 'bout')}
    del _L0_xattn_all

    def _L0_ffn_setup():
        import jax, jax.numpy as jnp
        import numpy as np
        B, T, D = (2, 128, 256)
        H, K, DK = (4, 8, 64)
        E = 2048
        NK = 128
        key = jax.random.key(seed)
        k1, k2, k3, k4, k5 = jax.random.split(key, 5)
        x = jax.random.normal(k1, (B, T, D), dtype=jnp.float32)
        Wq = jax.random.normal(k2, (D, 2 * H * DK), dtype=jnp.float32) * 0.02
        keys = jax.random.normal(k3, (H, NK, 2, DK), dtype=jnp.float32) * 0.02
        e_down = jax.random.normal(k4, (E, D), dtype=jnp.float32) * 0.01
        e_up = jax.random.normal(k5, (E, D), dtype=jnp.float32) * 0.01
        return {'x': x, 'Wq': Wq, 'keys': keys, 'e_down': e_down, 'e_up': e_up}
    _L0_ffn_all = _L0_ffn_setup()
    _L0_ffn_in = {k: v for k, v in _L0_ffn_all.items() if k in ('Wq', 'keys', 'e_down', 'e_up')}
    del _L0_ffn_all

    def _L1_xattn_setup():
        import jax, jax.numpy as jnp
        import numpy as np
        N_HEADS = 16
        N_KV_HEADS = 8
        HEAD_DIM = 128
        D_TEXT = 256
        D_VISION = 128
        GROUPS = N_HEADS // N_KV_HEADS
        key = jax.random.key(seed)
        ks = jax.random.split(key, 6)
        B, T_text, T_vis = (4, 256, 72)
        text_hidden = jax.random.normal(ks[0], (B, T_text, D_TEXT), dtype=jnp.float32)
        vision_tokens = jax.random.normal(ks[1], (B, T_vis, D_VISION), dtype=jnp.float32)
        vision_mask = jnp.ones((B, T_vis), dtype=bool)
        s = 0.02
        Wq = jax.random.normal(ks[2], (D_TEXT, N_HEADS * HEAD_DIM), dtype=jnp.float32) * s
        Wk = jax.random.normal(ks[3], (D_VISION, N_KV_HEADS * HEAD_DIM), dtype=jnp.float32) * s
        Wv = jax.random.normal(ks[4], (D_VISION, N_KV_HEADS * HEAD_DIM), dtype=jnp.float32) * s
        Wo = jax.random.normal(ks[5], (N_HEADS * HEAD_DIM, D_TEXT), dtype=jnp.float32) * s
        return {'text_hidden': text_hidden, 'vision_tokens': vision_tokens, 'vision_mask': vision_mask, 'Wq': Wq, 'Wk': Wk, 'Wv': Wv, 'Wo': Wo}
    _L1_xattn_all = _L1_xattn_setup()
    _L1_xattn_in = {k: v for k, v in _L1_xattn_all.items() if k in ('Wq', 'Wk', 'Wv', 'Wo')}
    del _L1_xattn_all

    def _L1_ffn_setup():
        import jax, jax.numpy as jnp
        import numpy as np
        H = 256
        I = 256
        E_ROUTED = 7
        NS = 1
        TOPK = 2
        TEMP = 1.0

        def _moe_forward(x, Wr, br, gate_bias, Wup, bup, Wgate, bgate, Wdown, bdown, Wsu, bsu, Wsg, bsg, Wsd, bsd):
            B, S, _ = x.shape
            xt = x.reshape(-1, H)
            N = xt.shape[0]
            gate = (xt @ Wr + br) / TEMP
            bias_gate = gate + gate_bias
            _, ids = jax.lax.top_k(bias_gate, TOPK)
            sel_logits = jnp.take_along_axis(gate, ids, axis=-1)
            masked = jnp.full_like(gate, -jnp.inf)
            masked = masked.at[jnp.arange(N)[:, None], ids].set(sel_logits)
            probs = jax.nn.softmax(masked, axis=-1)
            u = jnp.einsum('nh,ehi->eni', xt, Wup) + bup[:, None, :]
            g = jax.nn.silu(jnp.einsum('eni,eij->enj', u, Wgate) + bgate[:, None, :]) * u
            eo = jnp.einsum('enj,ejh->enh', g, Wdown) + bdown[:, None, :]
            out = jnp.einsum('ne,enh->nh', probs, eo)
            su = (xt @ Wsu + bsu).reshape(N, NS, I)
            sg = jax.nn.silu(su @ Wsg + bsg) * su
            so = (sg @ Wsd + bsd).sum(axis=1)
            out = out + so
            return out.reshape(B, S, H)
        key = jax.random.key(seed)
        ks = jax.random.split(key, 20)
        s = lambda fan_in: 1.0 / np.sqrt(fan_in)
        inp = {'x': jax.random.normal(ks[0], (4, 128, H), dtype=jnp.float32), 'Wr': jax.random.normal(ks[1], (H, E_ROUTED), jnp.float32) * s(H), 'br': jax.random.normal(ks[2], (E_ROUTED,), jnp.float32) * s(H), 'gate_bias': jnp.zeros((E_ROUTED,), jnp.float32), 'Wup': jax.random.normal(ks[3], (E_ROUTED, H, I), jnp.float32) * s(H), 'bup': jax.random.normal(ks[4], (E_ROUTED, I), jnp.float32) * s(H), 'Wgate': jax.random.normal(ks[5], (E_ROUTED, I, I), jnp.float32) * s(I), 'bgate': jax.random.normal(ks[6], (E_ROUTED, I), jnp.float32) * s(I), 'Wdown': jax.random.normal(ks[7], (E_ROUTED, I, H), jnp.float32) * s(I), 'bdown': jax.random.normal(ks[8], (E_ROUTED, H), jnp.float32) * s(I), 'Wsu': jax.random.normal(ks[9], (H, NS * I), jnp.float32) * s(H), 'bsu': jax.random.normal(ks[10], (NS * I,), jnp.float32) * s(H), 'Wsg': jax.random.normal(ks[11], (I, I), jnp.float32) * s(I), 'bsg': jax.random.normal(ks[12], (I,), jnp.float32) * s(I), 'Wsd': jax.random.normal(ks[13], (I, H), jnp.float32) * s(I), 'bsd': jax.random.normal(ks[14], (H,), jnp.float32) * s(I)}
        return inp
    _L1_ffn_all = _L1_ffn_setup()
    _L1_ffn_in = {k: v for k, v in _L1_ffn_all.items() if k in ('Wr', 'br', 'gate_bias', 'Wup', 'bup', 'Wgate', 'bgate', 'Wdown', 'bdown', 'Wsu', 'bsu', 'Wsg', 'bsg', 'Wsd', 'bsd')}
    del _L1_ffn_all

    def _L2_xattn_setup():
        import jax, jax.numpy as jnp
        import numpy as np
        B, S1, S2, DCA = (2, 256, 128, 16)
        QDIM, KDIM, H = (256, 128, 16)
        HD = QDIM // H
        SCALE = HD ** (-0.5)
        EPS = 1e-06
        DCA_WEIGHT = 1.0

        def _ln(t, w, b):
            m = jnp.mean(t, axis=-1, keepdims=True)
            v = jnp.var(t, axis=-1, keepdims=True)
            return (t - m) * jax.lax.rsqrt(v + EPS) * w + b

        def _attn(q, k, v):
            s = jnp.einsum('bhqd,bhkd->bhqk', q, k) * SCALE
            p = jax.nn.softmax(s, axis=-1)
            return jnp.einsum('bhqk,bhkd->bhqd', p, v)
        key = jax.random.key(seed)
        ks = jax.random.split(key, 8)
        w = lambda k, shape: jax.random.normal(k, shape, jnp.float32) * 0.02
        return {'x': jax.random.normal(ks[0], (B, S1, QDIM), jnp.float32), 'y': jax.random.normal(ks[1], (B, S2 + DCA, KDIM), jnp.float32), 'Wq': w(ks[2], (QDIM, QDIM)), 'bq': jnp.zeros((QDIM,), jnp.float32), 'Wk': w(ks[3], (KDIM, QDIM)), 'bk': jnp.zeros((QDIM,), jnp.float32), 'Wv': w(ks[4], (KDIM, QDIM)), 'bv': jnp.zeros((QDIM,), jnp.float32), 'Wkv_dca': w(ks[5], (KDIM, 2 * QDIM)), 'bkv_dca': jnp.zeros((2 * QDIM,), jnp.float32), 'qn_w': jnp.ones((HD,), jnp.float32), 'qn_b': jnp.zeros((HD,), jnp.float32), 'kn_w': jnp.ones((HD,), jnp.float32), 'kn_b': jnp.zeros((HD,), jnp.float32), 'kn_dca_w': jnp.ones((HD,), jnp.float32), 'kn_dca_b': jnp.zeros((HD,), jnp.float32), 'Wo': w(ks[6], (QDIM, QDIM)), 'bo': jnp.zeros((QDIM,), jnp.float32)}
    _L2_xattn_all = _L2_xattn_setup()
    _L2_xattn_in = {k: v for k, v in _L2_xattn_all.items() if k in ('Wq', 'bq', 'Wk', 'bk', 'Wv', 'bv', 'Wkv_dca', 'bkv_dca', 'qn_w', 'qn_b', 'kn_w', 'kn_b', 'kn_dca_w', 'kn_dca_b', 'Wo', 'bo')}
    del _L2_xattn_all

    def _L2_ffn_setup():
        import jax, jax.numpy as jnp
        import numpy as np
        D_MODEL = 256
        HIDDEN = int(2 * D_MODEL * 4 / 3)

        def ternary_quant(w):
            s = jnp.mean(jnp.abs(w))
            q = jnp.clip(jnp.round(w / s), -1.0, 1.0) * s
            return w + jax.lax.stop_gradient(q - w)
        key = jax.random.key(seed)
        k0, k1, k2, k3 = jax.random.split(key, 4)
        x = jax.random.normal(k0, (4, 512, D_MODEL), dtype=jnp.float32)
        std_in = 1.0 / np.sqrt(D_MODEL)
        std_h = 1.0 / np.sqrt(HIDDEN)
        w1 = jax.random.uniform(k1, (HIDDEN, D_MODEL), jnp.float32, -std_in, std_in)
        w3 = jax.random.uniform(k2, (HIDDEN, D_MODEL), jnp.float32, -std_in, std_in)
        w2 = jax.random.uniform(k3, (D_MODEL, HIDDEN), jnp.float32, -std_h, std_h)
        return {'x': x, 'w1': w1, 'w3': w3, 'w2': w2}
    _L2_ffn_all = _L2_ffn_setup()
    _L2_ffn_in = {k: v for k, v in _L2_ffn_all.items() if k in ('w1', 'w3', 'w2')}
    del _L2_ffn_all

    def _L3_xattn_setup():
        import jax, jax.numpy as jnp
        import numpy as np
        EPS = 1e-05

        def rmsnorm(x, g, eps=EPS):
            var = jnp.mean(jnp.square(x), axis=-1, keepdims=True)
            return x * jax.lax.rsqrt(var + eps) * g
        key = jax.random.key(seed)
        ks = jax.random.split(key, 8)
        B, Sq, Skv = (2, 512, 64)
        dim, cdim, H, D = (256, 128, 16, 128)
        inner = H * D
        s = lambda f: 1.0 / np.sqrt(f)
        return {'hidden_states': jax.random.normal(ks[0], (B, Sq, dim), jnp.float32), 'encoder_hidden_states': jax.random.normal(ks[1], (B, Skv, cdim), jnp.float32), 'Wq': jax.random.normal(ks[2], (dim, inner), jnp.float32) * s(dim), 'Wk': jax.random.normal(ks[3], (cdim, inner), jnp.float32) * s(cdim), 'Wv': jax.random.normal(ks[4], (cdim, inner), jnp.float32) * s(cdim), 'Wo': jax.random.normal(ks[5], (inner, dim), jnp.float32) * s(inner), 'gq': jnp.ones((D,), jnp.float32), 'gk': jnp.ones((D,), jnp.float32)}
    _L3_xattn_all = _L3_xattn_setup()
    _L3_xattn_in = {k: v for k, v in _L3_xattn_all.items() if k in ('Wq', 'Wk', 'Wv', 'Wo', 'gq', 'gk')}
    del _L3_xattn_all

    def _L3_ffn_setup():
        import jax, jax.numpy as jnp
        import numpy as np
        _FP8_MAX = 448.0
        _BLOCK = 32
        _EPS = 1e-30

        def _mx_dequant(t):
            rows, feat = t.shape
            blocks = t.reshape(rows, feat // _BLOCK, _BLOCK)
            max_abs = jnp.max(jnp.abs(blocks), axis=-1)
            scales = jnp.maximum(max_abs / _FP8_MAX, _EPS)
            q = (blocks / scales[..., None]).astype(jnp.float8_e4m3fn).astype(jnp.float32)
            return (q * scales[..., None]).reshape(rows, feat)

        def _mx_linear(x2d, w):
            return _mx_dequant(x2d) @ _mx_dequant(w).T
        key = jax.random.key(seed)
        k1, k2, k3, k4 = jax.random.split(key, 4)
        B, S, H, I = (2, 128, 256, 1024)
        return {'x': jax.random.normal(k1, (B, S, H), dtype=jnp.float32), 'gate_w': jax.random.normal(k2, (I, H), dtype=jnp.float32) * 0.02, 'up_w': jax.random.normal(k3, (I, H), dtype=jnp.float32) * 0.02, 'down_w': jax.random.normal(k4, (H, I), dtype=jnp.float32) * 0.02}
    _L3_ffn_all = _L3_ffn_setup()
    _L3_ffn_in = {k: v for k, v in _L3_ffn_all.items() if k in ('gate_w', 'up_w', 'down_w')}
    del _L3_ffn_all
    return {'x': x, 'ctx_1024': ctx_1024, 'fside_BxSx2_0': fside_BxSx2_0, 'mask_BxS2_bf1': mask_BxS2_bf1, 'L0_xattn_Wq': _L0_xattn_in['Wq'], 'L0_xattn_Wkv': _L0_xattn_in['Wkv'], 'L0_xattn_Wout': _L0_xattn_in['Wout'], 'L0_xattn_bout': _L0_xattn_in['bout'], 'L0_ffn_Wq': _L0_ffn_in['Wq'], 'L0_ffn_keys': _L0_ffn_in['keys'], 'L0_ffn_e_down': _L0_ffn_in['e_down'], 'L0_ffn_e_up': _L0_ffn_in['e_up'], 'L1_xattn_Wq': _L1_xattn_in['Wq'], 'L1_xattn_Wk': _L1_xattn_in['Wk'], 'L1_xattn_Wv': _L1_xattn_in['Wv'], 'L1_xattn_Wo': _L1_xattn_in['Wo'], 'L1_ffn_Wr': _L1_ffn_in['Wr'], 'L1_ffn_br': _L1_ffn_in['br'], 'L1_ffn_gate_bias': _L1_ffn_in['gate_bias'], 'L1_ffn_Wup': _L1_ffn_in['Wup'], 'L1_ffn_bup': _L1_ffn_in['bup'], 'L1_ffn_Wgate': _L1_ffn_in['Wgate'], 'L1_ffn_bgate': _L1_ffn_in['bgate'], 'L1_ffn_Wdown': _L1_ffn_in['Wdown'], 'L1_ffn_bdown': _L1_ffn_in['bdown'], 'L1_ffn_Wsu': _L1_ffn_in['Wsu'], 'L1_ffn_bsu': _L1_ffn_in['bsu'], 'L1_ffn_Wsg': _L1_ffn_in['Wsg'], 'L1_ffn_bsg': _L1_ffn_in['bsg'], 'L1_ffn_Wsd': _L1_ffn_in['Wsd'], 'L1_ffn_bsd': _L1_ffn_in['bsd'], 'L2_xattn_Wq': _L2_xattn_in['Wq'], 'L2_xattn_bq': _L2_xattn_in['bq'], 'L2_xattn_Wk': _L2_xattn_in['Wk'], 'L2_xattn_bk': _L2_xattn_in['bk'], 'L2_xattn_Wv': _L2_xattn_in['Wv'], 'L2_xattn_bv': _L2_xattn_in['bv'], 'L2_xattn_Wkv_dca': _L2_xattn_in['Wkv_dca'], 'L2_xattn_bkv_dca': _L2_xattn_in['bkv_dca'], 'L2_xattn_qn_w': _L2_xattn_in['qn_w'], 'L2_xattn_qn_b': _L2_xattn_in['qn_b'], 'L2_xattn_kn_w': _L2_xattn_in['kn_w'], 'L2_xattn_kn_b': _L2_xattn_in['kn_b'], 'L2_xattn_kn_dca_w': _L2_xattn_in['kn_dca_w'], 'L2_xattn_kn_dca_b': _L2_xattn_in['kn_dca_b'], 'L2_xattn_Wo': _L2_xattn_in['Wo'], 'L2_xattn_bo': _L2_xattn_in['bo'], 'L2_ffn_w1': _L2_ffn_in['w1'], 'L2_ffn_w3': _L2_ffn_in['w3'], 'L2_ffn_w2': _L2_ffn_in['w2'], 'L3_xattn_Wq': _L3_xattn_in['Wq'], 'L3_xattn_Wk': _L3_xattn_in['Wk'], 'L3_xattn_Wv': _L3_xattn_in['Wv'], 'L3_xattn_Wo': _L3_xattn_in['Wo'], 'L3_xattn_gq': _L3_xattn_in['gq'], 'L3_xattn_gk': _L3_xattn_in['gk'], 'L3_ffn_gate_w': _L3_ffn_in['gate_w'], 'L3_ffn_up_w': _L3_ffn_in['up_w'], 'L3_ffn_down_w': _L3_ffn_in['down_w']}

def reference(x, ctx_1024, fside_BxSx2_0, mask_BxS2_bf1, L0_xattn_Wq, L0_xattn_Wkv, L0_xattn_Wout, L0_xattn_bout, L0_ffn_Wq, L0_ffn_keys, L0_ffn_e_down, L0_ffn_e_up, L1_xattn_Wq, L1_xattn_Wk, L1_xattn_Wv, L1_xattn_Wo, L1_ffn_Wr, L1_ffn_br, L1_ffn_gate_bias, L1_ffn_Wup, L1_ffn_bup, L1_ffn_Wgate, L1_ffn_bgate, L1_ffn_Wdown, L1_ffn_bdown, L1_ffn_Wsu, L1_ffn_bsu, L1_ffn_Wsg, L1_ffn_bsg, L1_ffn_Wsd, L1_ffn_bsd, L2_xattn_Wq, L2_xattn_bq, L2_xattn_Wk, L2_xattn_bk, L2_xattn_Wv, L2_xattn_bv, L2_xattn_Wkv_dca, L2_xattn_bkv_dca, L2_xattn_qn_w, L2_xattn_qn_b, L2_xattn_kn_w, L2_xattn_kn_b, L2_xattn_kn_dca_w, L2_xattn_kn_dca_b, L2_xattn_Wo, L2_xattn_bo, L2_ffn_w1, L2_ffn_w3, L2_ffn_w2, L3_xattn_Wq, L3_xattn_Wk, L3_xattn_Wv, L3_xattn_Wo, L3_xattn_gq, L3_xattn_gk, L3_ffn_gate_w, L3_ffn_up_w, L3_ffn_down_w):
    import jax
    import jax.numpy as jnp

    def _L0_xattn_ref(x, ctx, pos_map, ctx_pos_map, Wq, Wkv, Wout, bout):
        import jax, jax.numpy as jnp
        import numpy as np
        DIM = 256
        CTX_DIM = 128
        N_HEADS = 32
        HEAD_DIM = DIM // N_HEADS
        POS_DIM = 2
        B, N, CTXN = (2, 256, 256)
        ROPE_BASE = 10000.0

        def apply_axial_rope(x, pos):
            b, n, h, d = x.shape
            p = pos.shape[-1]
            dpa = d // p
            half = dpa // 2
            freqs = ROPE_BASE ** (-jnp.arange(half, dtype=x.dtype) / half)
            ang = pos[..., :, None] * freqs
            cos = jnp.cos(ang)[:, :, None, :, :]
            sin = jnp.sin(ang)[:, :, None, :, :]
            xr = x.reshape(b, n, h, p, half, 2)
            x1, x2 = (xr[..., 0], xr[..., 1])
            out = jnp.stack([x1 * cos - x2 * sin, x1 * sin + x2 * cos], axis=-1)
            return out.reshape(b, n, h, d)
        b, n, _ = x.shape
        ctx_n = ctx.shape[1]
        q = (x @ Wq).reshape(b, n, N_HEADS, HEAD_DIM)
        k, v = jnp.split(ctx @ Wkv, 2, axis=-1)
        k = k.reshape(b, ctx_n, N_HEADS, HEAD_DIM)
        v = v.reshape(b, ctx_n, N_HEADS, HEAD_DIM)
        q = apply_axial_rope(q, pos_map)
        k = apply_axial_rope(k, ctx_pos_map)
        scale = 1.0 / np.sqrt(HEAD_DIM).astype(np.float32)
        logits = jnp.einsum('bqhd,bkhd->bhqk', q, k) * scale
        w = jax.nn.softmax(logits, axis=-1)
        attn = jnp.einsum('bhqk,bkhd->bqhd', w, v)
        attn = attn.reshape(b, n, N_HEADS * HEAD_DIM)
        return attn @ Wout + bout

    def _L0_ffn_ref(x, Wq, keys, e_down, e_up):
        import jax, jax.numpy as jnp
        import numpy as np
        B, T, D = (2, 128, 256)
        H, K, DK = (4, 8, 64)
        E = 2048
        NK = 128
        b, t, d = x.shape
        q = (x @ Wq).reshape(b, t, H, 2, DK)
        q1, q2 = (q[..., 0, :], q[..., 1, :])
        sim1 = jnp.einsum('bthd,hkd->bthk', q1, keys[:, :, 0, :])
        sim2 = jnp.einsum('bthd,hkd->bthk', q2, keys[:, :, 1, :])
        s1, i1 = jax.lax.top_k(sim1, K)
        s2, i2 = jax.lax.top_k(sim2, K)
        all_scores = (s1[..., :, None] + s2[..., None, :]).reshape(b, t, H, K * K)
        all_indices = (i1[..., :, None] * NK + i2[..., None, :]).reshape(b, t, H, K * K)
        final_scores, pk_idx = jax.lax.top_k(all_scores, K)
        final_indices = jnp.take_along_axis(all_indices, pk_idx, axis=-1)
        w_down = e_down[final_indices]
        w_up = e_up[final_indices]
        hidden = jnp.einsum('btd,bthkd->bthk', x, w_down)
        hidden = jax.nn.silu(hidden)
        hidden = hidden * jax.nn.relu(final_scores)
        out = jnp.einsum('bthk,bthkd->btd', hidden, w_up)
        return out

    def _L1_xattn_ref(text_hidden, vision_tokens, vision_mask, Wq, Wk, Wv, Wo):
        import jax, jax.numpy as jnp
        import numpy as np
        N_HEADS = 16
        N_KV_HEADS = 8
        HEAD_DIM = 128
        D_TEXT = 256
        D_VISION = 128
        GROUPS = N_HEADS // N_KV_HEADS
        B, T_text, _ = text_hidden.shape
        T_vis = vision_tokens.shape[1]
        scale = jnp.float32(np.sqrt(HEAD_DIM))
        q = (text_hidden @ Wq).reshape(B, T_text, N_HEADS, HEAD_DIM).transpose(0, 2, 1, 3)
        k = (vision_tokens @ Wk).reshape(B, T_vis, N_KV_HEADS, HEAD_DIM).transpose(0, 2, 1, 3)
        v = (vision_tokens @ Wv).reshape(B, T_vis, N_KV_HEADS, HEAD_DIM).transpose(0, 2, 1, 3)
        k = jnp.repeat(k, GROUPS, axis=1)
        v = jnp.repeat(v, GROUPS, axis=1)
        scores = jnp.einsum('bhtd,bhsd->bhts', q, k) / scale
        mask = vision_mask[:, None, None, :]
        scores = jnp.where(mask, scores, -jnp.inf)
        attn = jax.nn.softmax(scores, axis=-1)
        attn = jnp.nan_to_num(attn, nan=0.0)
        out = jnp.einsum('bhts,bhsd->bhtd', attn, v)
        out = out.transpose(0, 2, 1, 3).reshape(B, T_text, N_HEADS * HEAD_DIM)
        return out @ Wo

    def _L1_ffn_ref(x, Wr, br, gate_bias, Wup, bup, Wgate, bgate, Wdown, bdown, Wsu, bsu, Wsg, bsg, Wsd, bsd):
        import jax, jax.numpy as jnp
        import numpy as np
        H = 256
        I = 256
        E_ROUTED = 7
        NS = 1
        TOPK = 2
        TEMP = 1.0

        def _moe_forward(x, Wr, br, gate_bias, Wup, bup, Wgate, bgate, Wdown, bdown, Wsu, bsu, Wsg, bsg, Wsd, bsd):
            B, S, _ = x.shape
            xt = x.reshape(-1, H)
            N = xt.shape[0]
            gate = (xt @ Wr + br) / TEMP
            bias_gate = gate + gate_bias
            _, ids = jax.lax.top_k(bias_gate, TOPK)
            sel_logits = jnp.take_along_axis(gate, ids, axis=-1)
            masked = jnp.full_like(gate, -jnp.inf)
            masked = masked.at[jnp.arange(N)[:, None], ids].set(sel_logits)
            probs = jax.nn.softmax(masked, axis=-1)
            u = jnp.einsum('nh,ehi->eni', xt, Wup) + bup[:, None, :]
            g = jax.nn.silu(jnp.einsum('eni,eij->enj', u, Wgate) + bgate[:, None, :]) * u
            eo = jnp.einsum('enj,ejh->enh', g, Wdown) + bdown[:, None, :]
            out = jnp.einsum('ne,enh->nh', probs, eo)
            su = (xt @ Wsu + bsu).reshape(N, NS, I)
            sg = jax.nn.silu(su @ Wsg + bsg) * su
            so = (sg @ Wsd + bsd).sum(axis=1)
            out = out + so
            return out.reshape(B, S, H)
        return _moe_forward(x, Wr, br, gate_bias, Wup, bup, Wgate, bgate, Wdown, bdown, Wsu, bsu, Wsg, bsg, Wsd, bsd)

    def _L2_xattn_ref(x, y, Wq, bq, Wk, bk, Wv, bv, Wkv_dca, bkv_dca, qn_w, qn_b, kn_w, kn_b, kn_dca_w, kn_dca_b, Wo, bo):
        import jax, jax.numpy as jnp
        import numpy as np
        B, S1, S2, DCA = (2, 256, 128, 16)
        QDIM, KDIM, H = (256, 128, 16)
        HD = QDIM // H
        SCALE = HD ** (-0.5)
        EPS = 1e-06
        DCA_WEIGHT = 1.0

        def _ln(t, w, b):
            m = jnp.mean(t, axis=-1, keepdims=True)
            v = jnp.var(t, axis=-1, keepdims=True)
            return (t - m) * jax.lax.rsqrt(v + EPS) * w + b

        def _attn(q, k, v):
            s = jnp.einsum('bhqd,bhkd->bhqk', q, k) * SCALE
            p = jax.nn.softmax(s, axis=-1)
            return jnp.einsum('bhqk,bhkd->bhqd', p, v)
        b, s1, _ = x.shape
        y_dca = y[:, -DCA:, :]
        y_main = y[:, :-DCA, :]
        kv_dca = (y_dca @ Wkv_dca + bkv_dca).reshape(b, DCA, 2, H, HD)
        k_dca = _ln(kv_dca[:, :, 0], kn_dca_w, kn_dca_b)
        v_dca = kv_dca[:, :, 1]
        s2 = y_main.shape[1]
        q = _ln((x @ Wq + bq).reshape(b, s1, H, HD), qn_w, qn_b)
        kv = jnp.concatenate([y_main @ Wk + bk, y_main @ Wv + bv], axis=-1)
        kv = kv.reshape(b, s2, H, 2 * HD)
        k = _ln(kv[..., :HD], kn_w, kn_b)
        v = kv[..., HD:]
        qT = q.transpose(0, 2, 1, 3)
        ctx = _attn(qT, k.transpose(0, 2, 1, 3), v.transpose(0, 2, 1, 3))
        ctx = ctx.transpose(0, 2, 1, 3).reshape(b, s1, QDIM)
        ctx_dca = _attn(qT, k_dca.transpose(0, 2, 1, 3), v_dca.transpose(0, 2, 1, 3))
        ctx_dca = ctx_dca.transpose(0, 2, 1, 3).reshape(b, s1, QDIM)
        ctx = ctx + DCA_WEIGHT * ctx_dca
        return ctx @ Wo + bo

    def _L2_ffn_ref(x, w1, w3, w2):
        import jax, jax.numpy as jnp
        import numpy as np
        D_MODEL = 256
        HIDDEN = int(2 * D_MODEL * 4 / 3)

        def ternary_quant(w):
            s = jnp.mean(jnp.abs(w))
            q = jnp.clip(jnp.round(w / s), -1.0, 1.0) * s
            return w + jax.lax.stop_gradient(q - w)
        w1q = ternary_quant(w1)
        w3q = ternary_quant(w3)
        w2q = ternary_quant(w2)
        h1 = jnp.einsum('bsd,hd->bsh', x, w1q)
        h3 = jnp.einsum('bsd,hd->bsh', x, w3q)
        g = jax.nn.silu(h1) * h3
        return jnp.einsum('bsh,dh->bsd', g, w2q)

    def _L3_xattn_ref(hidden_states, encoder_hidden_states, Wq, Wk, Wv, Wo, gq, gk):
        import jax, jax.numpy as jnp
        import numpy as np
        EPS = 1e-05

        def rmsnorm(x, g, eps=EPS):
            var = jnp.mean(jnp.square(x), axis=-1, keepdims=True)
            return x * jax.lax.rsqrt(var + eps) * g
        B, Sq, _ = hidden_states.shape
        Skv = encoder_hidden_states.shape[1]
        D = gq.shape[0]
        H = Wq.shape[1] // D
        scale = 1.0 / np.sqrt(D)
        q = (hidden_states @ Wq).reshape(B, Sq, H, D)
        k = (encoder_hidden_states @ Wk).reshape(B, Skv, H, D)
        v = (encoder_hidden_states @ Wv).reshape(B, Skv, H, D)
        q = rmsnorm(q, gq)
        k = rmsnorm(k, gk)
        scores = jnp.einsum('bqhd,bkhd->bhqk', q, k) * scale
        attn = jax.nn.softmax(scores, axis=-1)
        out = jnp.einsum('bhqk,bkhd->bqhd', attn, v)
        out = out.reshape(B, Sq, H * D)
        return out @ Wo

    def _L3_ffn_ref(x, gate_w, up_w, down_w):
        import jax, jax.numpy as jnp
        import numpy as np
        _FP8_MAX = 448.0
        _BLOCK = 32
        _EPS = 1e-30

        def _mx_dequant(t):
            rows, feat = t.shape
            blocks = t.reshape(rows, feat // _BLOCK, _BLOCK)
            max_abs = jnp.max(jnp.abs(blocks), axis=-1)
            scales = jnp.maximum(max_abs / _FP8_MAX, _EPS)
            q = (blocks / scales[..., None]).astype(jnp.float8_e4m3fn).astype(jnp.float32)
            return (q * scales[..., None]).reshape(rows, feat)

        def _mx_linear(x2d, w):
            return _mx_dequant(x2d) @ _mx_dequant(w).T
        B, S, H = x.shape
        x2d = x.reshape(B * S, H)
        gate = _mx_linear(x2d, gate_w)
        up = _mx_linear(x2d, up_w)
        h = jax.nn.silu(gate) * up
        out = _mx_linear(h, down_w)
        return out.reshape(B, S, H)
    x = x + _L0_xattn_ref(_layernorm(x, axis=-1), ctx_1024, fside_BxSx2_0, fside_BxSx2_0, L0_xattn_Wq, L0_xattn_Wkv, L0_xattn_Wout, L0_xattn_bout)
    x = x + _L0_ffn_ref(_layernorm(x, axis=-1), L0_ffn_Wq, L0_ffn_keys, L0_ffn_e_down, L0_ffn_e_up)
    x = x + _L1_xattn_ref(_layernorm(x, axis=-1), ctx_1024, mask_BxS2_bf1, L1_xattn_Wq, L1_xattn_Wk, L1_xattn_Wv, L1_xattn_Wo)
    x = x + _L1_ffn_ref(_layernorm(x, axis=-1), L1_ffn_Wr, L1_ffn_br, L1_ffn_gate_bias, L1_ffn_Wup, L1_ffn_bup, L1_ffn_Wgate, L1_ffn_bgate, L1_ffn_Wdown, L1_ffn_bdown, L1_ffn_Wsu, L1_ffn_bsu, L1_ffn_Wsg, L1_ffn_bsg, L1_ffn_Wsd, L1_ffn_bsd)
    x = x + _L2_xattn_ref(_layernorm(x, axis=-1), ctx_1024, L2_xattn_Wq, L2_xattn_bq, L2_xattn_Wk, L2_xattn_bk, L2_xattn_Wv, L2_xattn_bv, L2_xattn_Wkv_dca, L2_xattn_bkv_dca, L2_xattn_qn_w, L2_xattn_qn_b, L2_xattn_kn_w, L2_xattn_kn_b, L2_xattn_kn_dca_w, L2_xattn_kn_dca_b, L2_xattn_Wo, L2_xattn_bo)
    x = x + _L2_ffn_ref(_layernorm(x, axis=-1), L2_ffn_w1, L2_ffn_w3, L2_ffn_w2)
    x = x + _L3_xattn_ref(_layernorm(x, axis=-1), ctx_1024, L3_xattn_Wq, L3_xattn_Wk, L3_xattn_Wv, L3_xattn_Wo, L3_xattn_gq, L3_xattn_gk)
    x = x + _L3_ffn_ref(_layernorm(x, axis=-1), L3_ffn_gate_w, L3_ffn_up_w, L3_ffn_down_w)
    return x

_drawn_inputs = setup_inputs


def setup_inputs(seed=0):
    import zlib

    import numpy as np

    out = dict(_drawn_inputs(seed))
    spreads = {'L0_xattn_bout': (0.0, 0.1),
     'L1_ffn_gate_bias': (0.0, 0.8),
     'L2_xattn_bq': (0.0, 2.0),
     'L2_xattn_bk': (0.0, 2.0),
     'L2_xattn_bv': (0.0, 2.0),
     'L2_xattn_bkv_dca': (0.0, 1.684),
     'L2_xattn_qn_w': (1.0, 0.6),
     'L2_xattn_qn_b': (0.0, 2.0),
     'L2_xattn_kn_w': (1.0, 0.6),
     'L2_xattn_kn_b': (0.0, 2.0),
     'L2_xattn_kn_dca_w': (1.0, 0.6),
     'L2_xattn_kn_dca_b': (0.0, 2.0),
     'L2_xattn_bo': (0.0, 0.552),
     'L3_xattn_gq': (1.0, 0.6),
     'L3_xattn_gk': (1.0, 0.6)}
    factors = {'L0_ffn_Wq': 8.0,
     'L0_ffn_keys': 8.0,
     'L0_ffn_e_down': 3.887,
     'L0_ffn_e_up': 4.328,
     'L1_xattn_Wq': 19.011,
     'L1_xattn_Wk': 17.35,
     'L1_ffn_bgate': 13.731,
     'L2_xattn_Wq': 20.258,
     'L2_xattn_Wk': 12.138,
     'L2_xattn_Wv': 11.687,
     'L1_ffn_br': 8.0,
     'L1_ffn_bup': 8.0,
     'L1_ffn_bdown': 8.0,
     'L1_ffn_bsu': 7.622,
     'L1_ffn_bsg': 8.0,
     'L1_ffn_bsd': 6.502,
     'L2_xattn_Wkv_dca': 8.0,
     'L2_ffn_w1': 8.0,
     'L2_ffn_w3': 8.0,
     'L2_ffn_w2': 8.0,
     'L3_ffn_gate_w': 8.0,
     'L3_ffn_up_w': 8.0,
     'L3_ffn_down_w': 8.0}
    for name, (base, spread) in spreads.items():
        noise = np.random.default_rng([zlib.crc32(name.encode()), seed]).standard_normal(out[name].shape)
        drawn = base * np.exp(spread * noise) if base else spread * noise
        out[name] = jnp.asarray(drawn.astype(out[name].dtype))
    for name, factor in factors.items():
        out[name] = (out[name] * factor).astype(out[name].dtype)
    return out
```

```python
import math
from contextlib import ExitStack

import numpy as np
import concourse.bass as bass
from concourse import mybir

SUBS = (0, 1, 2, 3, 4, 5, 6, 7)

F32 = mybir.dt.float32
BF16 = mybir.dt.bfloat16
F16 = mybir.dt.float16
U32 = mybir.dt.uint32
U8 = mybir.dt.uint8
ALU = mybir.AluOpType
ACT = mybir.ActivationFunctionType
AX = mybir.AxisListType

NB = 16
C_ID, C_I128, C_I64, C_I8, C_MM, C_MD, C_PC, C_Z, C_ONE, C_N = 0, 128, 256, 320, 328, 329, 330, 331, 459, 587


class Queue:

    def __init__(self, sem):
        self.sem, self.n, self.ops, self.seen = sem, 0, [], {}

    def __call__(self, waits, f, *args, inc=1, sem=None, step=1, **kw):
        need = []
        for sem_, n in flat(waits):
            if self.seen.get(sem_.name, 0) < n:
                self.seen[sem_.name] = n
                need = [(s, k) for s, k in need if s.name != sem_.name] + [(sem_, n)]
        if sem is None:
            self.ops.append((need, f, args, kw, self.sem if inc else None, 1))
            if inc:
                self.n += 1
            return (self.sem, self.n)
        self.ops.append((need, f, args, kw, sem, step))
        return None

    def run(self, eng):
        for need, f, args, kw, sem, step in self.ops:
            for s, n in need:
                eng.wait_ge(s, n)
            ins = f(*args, **kw)
            if sem is not None:
                ins.then_inc(sem, step)


def flat(waits):
    if waits is None:
        return []
    if isinstance(waits, tuple) and len(waits) == 2 and isinstance(waits[1], int):
        return [waits]
    return [t for w in waits for t in flat(w)]


class Load:

    def __init__(self, q, dma, sem):
        self.q, self.dma, self.sem, self.n = q, dma, sem, 0

    def __call__(self, waits, dst, src):
        self.q(waits, self.dma, dst, src, sem=self.sem, step=16)
        self.n += 16
        return (self.sem, self.n)


class Slot:
    pass


def bc(ap, axis, shape):
    return ap.unsqueeze(axis).to_broadcast(shape)


def program(nc, A, out):
    ctx = ExitStack()
    with ctx:
        def sb(name, shape, dt=F32):
            return ctx.enter_context(nc.sbuf_tensor(name, shape, dt))

        def sem(name):
            return ctx.enter_context(nc.semaphore(name))

        x = sb("x", [128, NB, 256])
        ctxT = sb("ctxT", [128, NB * 128])
        area = [sb("areaA", [128, 12288]), sb("areaB", [128, 12288])]
        cst = sb("cst", [128, C_N])
        idb = sb("idb", [128, 128], BF16)
        zb = sb("zb", [128, 4, 128], BF16)
        i128h = sb("i128h", [128, 128], F16)
        i64h = sb("i64h", [128, 64], F16)
        neghalf = sb("neghalf", [128, 32])
        cs = sb("cs", [128, 2, NB * 4])
        mbias = sb("mbias", [128, NB])
        mkey = sb("mkey", [128, NB])

        slots = []
        for i in range(2):
            s = Slot()
            s.i = i
            s.xn = sb(f"xn{i}", [128, 2, 256])
            s.xT = sb(f"xT{i}", [128, 2, 256])
            s.ar = sb(f"ar{i}", [128, 8704])
            s.sm = sb(f"sm{i}", [128, 192])
            s.bk = [ctx.enter_context(nc.psum_tensor(f"pb{i}_{j}", [128, 512], F32)) for j in range(4)]
            s.bf = [None] * 4
            s.done = None
            slots.append(s)

        V = Queue(sem("s_dve"))
        S = Queue(sem("s_act"))
        T = Queue(sem("s_pe"))
        P = Queue(sem("s_pool"))
        D = Queue(sem("s_sp"))
        ve, se, te, pe_ = nc.vector, nc.scalar, nc.tensor, nc.gpsimd

        ld_c = Load(D, nc.sync.dma_start, sem("d_c"))
        ld_x = Load(D, nc.sync.dma_start, sem("d_x"))
        ld_w = [Load(D, nc.sync.dma_start, sem(f"d_w{k}")) for k in range(8)]
        st_o = Load(D, nc.sync.dma_start, sem("d_o"))

        ident = cst[:, C_ID:C_ID + 128]
        ones_row = cst[0:1, C_ONE:C_ONE + 128]
        ones_sq = cst[:, C_ONE:C_ONE + 128]
        iota8 = cst[:, C_I8:C_I8 + 8]

        ld_c(None, cst[:, :], A["consts"])
        t_c = ld_c(None, cs[:, 0, :].rearrange("p (b k) -> p b k", k=4)[:, :, 0:2],
                   A["fside"].rearrange("b t p -> t b p"))
        t_x0 = ld_x(None, x[:, :, :], A["x"].rearrange("b t d -> t b d"))
        t_ctx = ld_x(None, ctxT[:, :], A["ctxT"])
        m8 = slots[1].ar[:, 0:4].bitcast(U8)
        t_m8 = ld_x(None, m8, A["maskT"])

        t_k = V(t_c, ve.tensor_copy, idb[:, :], ident)
        for t_ in range(4):
            t_k = V(t_c, ve.tensor_copy, zb[:, t_, :].rearrange("p (g e) -> p g e", e=16),
                    bc(cst[:, C_Z + 8 * t_:C_Z + 8 * t_ + 8], 2, [128, 8, 16]))
        t_k = V(t_c, ve.tensor_copy, i128h[:, :], cst[:, C_I128:C_I128 + 128])
        t_k = V(t_c, ve.tensor_copy, i64h[:, :], cst[:, C_I64:C_I64 + 64])
        t_k = V(None, ve.memset, neghalf[:, :], -0.5)
        t_m = V(t_m8, ve.tensor_copy, mkey[:, :], m8)
        t_k = V(t_m, ve.tensor_scalar, mbias[:, :], mkey[:, :], -1.0, 1e30, ALU.add, ALU.mult)

        ang = slots[0].ar[:, 0:64].rearrange("p (b q j) -> p b q j", q=2, j=2)
        pos = cs[:, 0, :].rearrange("p (b k) -> p b k", k=4)[:, :, 0:2]
        t = V(t_c, ve.tensor_copy, ang[:, :, :, 0], pos)
        t = V(t_c, ve.tensor_scalar, ang[:, :, :, 1], pos, float(np.float32(0.01)), None, ALU.mult)
        af = slots[0].ar[:, 0:64]
        MAGIC = 12582912.0
        for which, off in ((1, 0.0), (0, math.pi / 2)):
            a0 = slots[0].ar[:, 64:128]
            n0 = slots[0].ar[:, 128:192]
            t = V(t, ve.tensor_scalar, a0, af, off, None, ALU.add)
            t = V(t, ve.tensor_scalar, n0, a0, 1.0 / (2 * math.pi), MAGIC, ALU.mult, ALU.add)
            t = V(t, ve.tensor_scalar, n0, n0, MAGIC, None, ALU.subtract)
            t = V(t, ve.scalar_tensor_tensor, a0, n0, -6.28125, a0, ALU.mult, ALU.add)
            t = V(t, ve.scalar_tensor_tensor, a0, n0, -(2 * math.pi - 6.28125), a0, ALU.mult, ALU.add)
            t = V(t, ve.tensor_scalar, a0, a0, 3.1415925, -3.1415925, ALU.min, ALU.max)
            t = S(t, se.activation, cs[:, which, :], a0, ACT.Sin)
        t_cs = t
        slots[0].done = [t_cs, t_k]
        slots[1].done = [t_k]
        t_const = [t_k, t_c]

        def put(k, off, dims, src, waits, rows=128):
            n = int(np.prod(dims))
            v = area[k % 2][0:rows, off:off + n]
            if len(dims) == 2:
                v = v.rearrange("p (a b) -> p a b", a=dims[0])
            if len(dims) == 3:
                v = v.rearrange("p (a b c) -> p a b c", a=dims[0], b=dims[1])
            if src is not None:
                ld_w[k](waits, v, src)
            return v

        W = [None] * 8

        def kp(ap, k):
            return ap.rearrange("(k p) n -> p k n", k=k)

        def load_weights(k, w):
            d = {}
            if k == 0:
                d["wq"] = put(k, 0, [2, 256], kp(A["L0_xattn_Wq"], 2), w)
                d["wkv"] = put(k, 512, [512], A["L0_xattn_Wkv"], w)
                d["wo"] = put(k, 1024, [2, 256], kp(A["L0_xattn_Wout"], 2), w)
                d["bo"] = put(k, 1536, [256], A["L0_xattn_bout"].unsqueeze(0), w, rows=1)
            if k == 1:
                d["ed"] = put(k, 0, [2, 2048], kp(A["edT"], 2), w)
                d["eu"] = put(k, 4096, [16, 256], kp(A["L0_ffn_e_up"], 16), w)
                d["wq"] = put(k, 8192, [2, 512], kp(A["L0_ffn_Wq"], 2), w)
                d["keys"] = put(k, 9216, [4, 128], A["keysT"], w)
            if k == 2:
                d["wq"] = put(k, 0, [2, 2048], kp(A["L1_xattn_Wq"], 2), w)
                d["wk"] = put(k, 4096, [1024], A["L1_xattn_Wk"], w)
                d["wv"] = put(k, 5120, [1024], A["L1_xattn_Wv"], w)
                d["wo"] = put(k, 6144, [16, 256], kp(A["L1_xattn_Wo"], 16), w)
            if k == 3:
                for j, (n, m) in enumerate((("Wup", "Wsu"), ("Wgate", "Wsg"), ("Wdown", "Wsd"))):
                    v = area[1][:, 4096 * j:4096 * (j + 1)].rearrange("p (e k n) -> p e k n", e=8, k=2)
                    d[n] = v
                    for e in range(7):
                        ld_w[k](w, v[:, e], kp(A["L1_ffn_" + n][e], 2))
                    ld_w[k](w, v[:, 7], kp(A["L1_ffn_" + m], 2))
            if k == 4:
                d["wq"] = put(k, 0, [2, 256], kp(A["L2_xattn_Wq"], 2), w)
                d["wk"] = put(k, 512, [256], A["L2_xattn_Wk"], w)
                d["wv"] = put(k, 768, [256], A["L2_xattn_Wv"], w)
                d["wd"] = put(k, 1024, [512], A["L2_xattn_Wkv_dca"], w)
                d["wo"] = put(k, 1536, [2, 256], kp(A["L2_xattn_Wo"], 2), w)
                for j, n in enumerate(("bq", "bk", "bv", "bo")):
                    d[n] = put(k, 2048 + 256 * j, [256], A["L2_xattn_" + n].unsqueeze(0), w, rows=1)
                d["bd"] = put(k, 3072, [512], A["L2_xattn_bkv_dca"].unsqueeze(0), w, rows=1)
                ww = area[0][:, 3584:3648].rearrange("p (a b c) -> p a b c", a=2, b=2)
                d["nw"] = ww
                for c, sfx in ((0, "w"), (1, "b")):
                    ld_w[k](w, ww[:, c, 0], A["L2_xattn_qn_" + sfx].partition_broadcast(128))
                    ld_w[k](w, ww[0:112, c, 1], A["L2_xattn_kn_" + sfx].partition_broadcast(112))
                    ld_w[k](w, ww[112:128, c, 1], A["L2_xattn_kn_dca_" + sfx].partition_broadcast(16))
                d["mrow"] = put(k, 3648, [2, 128], A["mrow"].unsqueeze(0), w, rows=1)
            if k == 5:
                d["w1"] = put(k, 0, [2, 682], kp(A["w1T"], 2), w)
                d["w3"] = put(k, 1364, [2, 682], kp(A["w3T"], 2), w)
                v = put(k, 2728, [6, 256], None, w)
                d["w2"] = v
                ld_w[k](w, v[:, 0:5], kp(A["w2T"][0:640], 5))
                ld_w[k](w, v[0:42, 5], A["w2T"][640:682])
                d["tmp"] = area[1][:, 4264:8528]
            if k == 6:
                d["wq"] = put(k, 0, [2, 2048], kp(A["L3_xattn_Wq"], 2), w)
                d["wk"] = put(k, 4096, [2048], A["L3_xattn_Wk"], w)
                d["wv"] = put(k, 6144, [2048], A["L3_xattn_Wv"], w)
                d["wo"] = put(k, 8192, [16, 256], kp(A["L3_xattn_Wo"], 16), w)
            if k == 7:
                d["raw"] = put(k, 0, [24, 256], None, w)
                ld_w[k](w, d["raw"][:, 0:8], kp(A["L3_ffn_gate_w"], 8))
                ld_w[k](w, d["raw"][:, 8:16], kp(A["L3_ffn_up_w"], 8))
                ld_w[k](w, d["raw"][:, 16:24].rearrange("p (k c) n -> p k (c n)", k=2), kp(A["L3_ffn_down_w"], 2))
                d["g"] = put(k, 6144, [2, 1024], None, w)
                d["u"] = put(k, 8192, [2, 1024], None, w)
                d["d"] = put(k, 10240, [8, 256], None, w)
            d["t"] = (ld_w[k].sem, ld_w[k].n)
            W[k] = d

        wr = sb("wr", [128, 2, 7])
        rb = sb("rb", [1, 16])
        bu = sb("bu", [128, 2, 16])
        bdn = sb("bdn", [8, 256])
        gqk = sb("gqk", [128, 2])
        gp = sb("gp", [128, 1])
        ld_s = Load(D, nc.sync.dma_start, sem("d_s"))

        def load_small():
            ld_s(None, wr[:, :, :], kp(A["L1_ffn_Wr"], 2))
            ld_s(None, rb[0:1, 0:7], A["L1_ffn_br"].unsqueeze(0))
            ld_s(None, rb[0:1, 8:15], A["L1_ffn_gate_bias"].unsqueeze(0))
            ld_s(None, bu[:, :, :], A["bugT"])
            ld_s(None, bdn[:, :], A["bdown"])
            t = ld_s(None, gqk[:, :], A["gqk"])
            return t

        def ln(s, u, eps=1e-5):
            w = [s.done, s.x_t[u]]
            st = s.sm[:, 0:12].rearrange("p (b k) -> p b k", b=2)
            mv = s.sm[:, 12:16].rearrange("p (b k) -> p b k", b=2)
            rs = s.sm[:, 16:18]
            for bb in range(2):
                t = V(w, ve.bn_stats, st[:, bb, :], x[:, 2 * u + bb, :])
                t = V(t, ve.bn_aggr, mv[:, bb, :], st[:, bb, :])
            t = P(t, pe_.tensor_scalar, rs, mv[:, :, 1], eps, None, ALU.add)
            t = P([t, t_const], pe_.tensor_tensor, rs, rs, neghalf[:, 0:2], ALU.pow)
            for bb in range(2):
                tv = V([t, w], ve.tensor_scalar, s.xn[:, bb, :], x[:, 2 * u + bb, :],
                       mv[:, bb, 0:1], rs[:, bb:bb + 1], ALU.subtract, ALU.mult)
            s.t_xn = tv
            return tv

        def xpose(s, t_in, j=0):
            b4 = s.bk[j][:, :].rearrange("p (k n) -> p k n", k=2)
            for k in range(2):
                for bb in range(2):
                    t = T([t_in, s.bf[j], t_const], te.transpose, b4[:, k, bb * 128:(bb + 1) * 128],
                          s.xn[:, bb, k * 128:(k + 1) * 128], ident, inc=(k + bb == 2))
            t = S([t, s.done], se.copy, s.xT[:, :, :], b4)
            s.bf[j] = t
            return t

        def add_x(s, b, src, waits):
            return V(waits, ve.tensor_tensor, x[:, b, :], x[:, b, :], src, ALU.add)

        def small_init(s, L):
            H = 32 if L == 0 else 16
            qp = s.ar[:, 0:2048]
            t = V(s.done, ve.memset, qp, 0.0)
            t = V(s.done, ve.memset, s.ar[:, 8492:8620], 0.0)
            if L == 0:
                vt = s.ar[:, 6144:6144 + 288].rearrange("p (h e) -> p h e", e=9)
                t = V(s.done, ve.memset, vt[:, :, 8:9], 1.0)
            else:
                t = V(s.done, ve.memset, s.ar[:, 6700:6956], 0.0)
            s.t_init = t
            return
            yield

        def small_attn(s, u, L):
            w = W[0 if L == 0 else 4]
            H = 32 if L == 0 else 16
            hd = 256 // H
            E = 9 if L == 0 else 34
            scale = 1.0 / math.sqrt(hd)
            bk = s.bk
            t_ln = ln(s, u)
            yield
            t_xT = xpose(s, t_ln)
            yield
            qp = s.ar[:, 0:64 * H].rearrange("p (a h e) -> p a h e", a=2, h=H)
            qT = s.ar[:, 2048:2048 + 32 * H].rearrange("p (t n) -> p t n", n=128)
            kT = s.ar[:, 3072:3072 + 32 * H].rearrange("p (t n) -> p t n", n=128)
            Pm = s.ar[:, 4096:6144].rearrange("p (i n) -> p i n", i=4)
            vt = s.ar[:, 6144:6144 + H * E].rearrange("p (h e) -> p h e", e=E)
            cm = s.ar[:, 6700:6828]
            cd = s.ar[:, 6828:6956]
            tmp = s.ar[:, 6956:7980]
            O = s.ar[:, 7980:8236].rearrange("p (h e) -> p h e", h=H)
            OT = s.ar[:, 8236:8492].rearrange("p (k n) -> p k n", k=2)
            nm = s.ar[:, 8492:8620].rearrange("p (i n) -> p i n", i=4)
            rec = s.sm[:, 64:96]
            nmT = s.ar[:, 8620:8684].bitcast(BF16)
            t_b = [s.done, t_xT]
            for bb in range(2):
                b = 2 * u + bb
                cx = ctxT[:, b * 128:(b + 1) * 128]
                tok = slice(bb * 128, (bb + 1) * 128)
                wq = [w["t"], t_xT, s.bf[0], t_const, t_ctx]
                if L == 0:
                    T(wq, te.matmul, bk[0][:, 0:256], s.xT[:, 0, tok], w["wq"][:, 0], start=True, stop=False, inc=0)
                    T(None, te.matmul, bk[0][:, 0:256], s.xT[:, 1, tok], w["wq"][:, 1], start=False, stop=True, inc=0)
                    T(None, te.matmul, bk[0][:, 256:512], cx, w["wkv"][:, 0:256], start=True, stop=True, inc=0)
                    t_p = T(s.bf[1], te.matmul, bk[1][:, 0:256], cx, w["wkv"][:, 256:512], start=True, stop=True)
                    yield
                    src = bk[0][:, :].rearrange("p (h f two) -> p h f two", f=4, two=2)
                    co = bc(cs[:, 0, 4 * b:4 * b + 4], 1, [128, 64, 4])
                    si = bc(cs[:, 1, 4 * b:4 * b + 4], 1, [128, 64, 4])
                    tt = [tmp[:, 256 * k:256 * (k + 1)].rearrange("p (h f) -> p h f", f=4) for k in range(4)]
                    t1 = V([t_p, t_cs, t_b], ve.tensor_tensor, tt[0], src[:, :, :, 0], co, ALU.mult)
                    t1 = V(None, ve.tensor_tensor, tt[1], src[:, :, :, 1], si, ALU.mult)
                    t1 = V(None, ve.tensor_tensor, tt[2], src[:, :, :, 0], si, ALU.mult)
                    t1 = V(None, ve.tensor_tensor, tt[3], src[:, :, :, 1], co, ALU.mult)
                    s.bf[0] = t1
                    dst = s.ar[:, 0:2048].rearrange("p (h e) -> p h e", e=32)[:, :, 0:8] \
                        .rearrange("p h (f two) -> p h f two", two=2)
                    V([t1, s.t_init], ve.tensor_tensor, dst[:, :, :, 0], tt[0], tt[1], ALU.subtract)
                    t_q = V(None, ve.tensor_tensor, dst[:, :, :, 1], tt[2], tt[3], ALU.add)
                    t_v = S([t_p, t_b, s.t_init], se.copy, vt[:, :, 0:8],
                            bk[1][:, 0:256].rearrange("p (h e) -> p h e", e=8))
                    s.bf[1] = t_v
                else:
                    P([t_ctx, t_b, s.t_init], pe_.tensor_copy, cm[:, 0:112], cx[:, 0:112])
                    t_cm = P(None, pe_.tensor_copy, cd[:, 112:128], cx[:, 112:128])
                    mr = w["mrow"]
                    T(wq, te.matmul, bk[0][:, 0:256], s.xT[:, 0, tok], w["wq"][:, 0], start=True, stop=False, inc=0)
                    T(None, te.matmul, bk[0][:, 0:256], s.xT[:, 1, tok], w["wq"][:, 1], start=False, stop=False, inc=0)
                    T(None, te.matmul, bk[0][:, 0:256], ones_row, w["bq"][0:1, :], start=False, stop=True, inc=0)
                    t_p = None
                    for dst, wm, wd, bm, bd, wt in (
                            (bk[0][:, 256:512], w["wk"], w["wd"][:, 0:256], w["bk"], w["bd"][0:1, 0:256], None),
                            (bk[1][:, 0:256], w["wv"], w["wd"][:, 256:512], w["bv"], w["bd"][0:1, 256:512], s.bf[1])):
                        T([t_cm, wt], te.matmul, dst, cm, wm, start=True, stop=False, inc=0)
                        T(None, te.matmul, dst, cd, wd, start=False, stop=False, inc=0)
                        T(None, te.matmul, dst, mr[0:1, 0], bm[0:1, :], start=False, stop=False, inc=0)
                        t_p = T(None, te.matmul, dst, mr[0:1, 1], bd, start=False, stop=True)
                    yield
                    src = bk[0][:, :].rearrange("p (h e) -> p h e", e=16)
                    y = tmp[:, 0:512].rearrange("p (h e) -> p h e", e=16)
                    sq = tmp[:, 512:1024].rearrange("p (h e) -> p h e", e=16)
                    mu = s.sm[:, 96:128]
                    va = s.sm[:, 128:160]
                    t1 = V([t_p, t_b], ve.tensor_reduce, mu, src, AX.X, ALU.add)
                    t1 = V(t1, ve.tensor_scalar, mu, mu, 1.0 / 16, None, ALU.mult)
                    t1 = V(t1, ve.tensor_tensor, y, src, bc(mu, 2, [128, 32, 16]), ALU.subtract)
                    s.bf[0] = t1
                    t2 = S(t1, se.activation, sq, y, ACT.Square)
                    t2 = V(t2, ve.tensor_reduce, va, sq, AX.X, ALU.add)
                    t2 = P(t2, pe_.tensor_scalar, va, va, 1.0 / 16, 1e-6, ALU.mult, ALU.add)
                    t2 = P(t2, pe_.tensor_tensor, va, va, neghalf[:, 0:32], ALU.pow)
                    t2 = V(t2, ve.tensor_tensor, y, y, bc(va, 2, [128, 32, 16]), ALU.mult)
                    y4 = tmp[:, 0:512].rearrange("p (a h e) -> p a h e", a=2, h=16)
                    for a in range(2):
                        t3 = V([t2, w["t"]], ve.tensor_tensor, y4[:, a], y4[:, a],
                               bc(w["nw"][:, 0, a], 1, [128, 16, 16]), ALU.mult)
                    for a in range(2):
                        t_q = V([t3, s.t_init], ve.tensor_tensor, qp[:, a, :, 0:16], y4[:, a],
                                bc(w["nw"][:, 1, a], 1, [128, 16, 16]), ALU.add)
                    vs = bk[1][:, 0:256].rearrange("p (h e) -> p h e", e=16)
                    t_v = None
                    for c in range(2):
                        m = cst[:, C_MM + c:C_MM + c + 1]
                        V([t_p, t_b], ve.tensor_scalar, vt[:, :, 17 * c:17 * c + 16], vs, m, None, ALU.mult)
                        t_v = V(None, ve.tensor_scalar, vt[:, :, 17 * c + 16:17 * c + 17],
                                ones_sq[:, 0:16].unsqueeze(2), m, None, ALU.mult)
                    s.bf[1] = t_v
                yield
                nt = H // 4
                kb = (0, 1) if L == 0 else (3,)
                qb = (2, 3) if L == 0 else (2,)
                t_e = []
                for a, banks, dstT in ((0, qb, qT), (1, kb, kT)):
                    for t_ in range(nt):
                        j = banks[t_ // 4]
                        t = T([t_q, s.bf[j]], te.transpose, bk[j][:, (t_ % 4) * 128:(t_ % 4 + 1) * 128],
                              qp[:, a, 4 * t_:4 * t_ + 4, :].rearrange("p h e -> p (h e)"), ident,
                              inc=(t_ % 4 == 3))
                        if t_ % 4 == 3:
                            o = dstT[:, t_ - 3:t_ + 1, :]
                            i_ = bk[j][:, :].rearrange("p (t n) -> p t n", t=4)
                            if a == 0:
                                t = S([t, t_b], se.copy, o, i_)
                            else:
                                t = V([t, t_b], ve.tensor_copy, o, i_)
                            s.bf[j] = t
                            t_e.append(t)
                yield
                nh = H // 16
                t_m = None
                for half in range(nh):
                    t = None
                    for i in range(4):
                        for j in range(4):
                            h = half * 16 + j * 4 + i
                            t_ = h // 4
                            t = T([t_e, s.bf[i]], te.matmul, bk[i][:, j * 128:(j + 1) * 128],
                                  qT[32 * i:32 * i + 32, t_, :], kT[32 * i:32 * i + 32, t_, :],
                                  start=True, stop=True, inc=(j == 3))
                        bv = bk[i][:, :].rearrange("p (j n) -> p j n", j=4)
                        if L == 0:
                            t_m = V([t, t_b, s.t_init], ve.tensor_reduce, nm[:, i, 4 * half:4 * half + 4], bv, AX.X, ALU.max)
                        else:
                            V([t, t_b, s.t_init], ve.tensor_reduce, nm[:, i, 0:4], bv[:, :, 0:112], AX.X, ALU.max)
                            t_m = V(None, ve.tensor_reduce, nm[:, i, 4:8], bv[:, :, 112:128], AX.X, ALU.max)
                        s.bf[i] = t_m
                    yield
                t = T([t_m, s.bf[0]], te.transpose, bk[0][:, 0:128],
                      nm[:, :, :].rearrange("p i n -> p (i n)"), ident)
                t_n = S([t, t_b], se.mul, nmT, bk[0][:, 0:128], -1.0)
                s.bf[0] = t_n
                yield
                for half in range(nh):
                    t_x = []
                    for i in range(4):
                        for j in range(4):
                            h = half * 16 + j * 4 + i
                            t_ = h // 4
                            o = bk[i][:, j * 128:(j + 1) * 128]
                            T([t_n, s.bf[i]], te.matmul, o, kT[32 * i:32 * i + 32, t_, :], qT[32 * i:32 * i + 32, t_, :],
                              start=True, stop=False, inc=0)
                            if L == 0:
                                sel = idb[32 * i:32 * i + 32, 32 * i + t_:32 * i + t_ + 1].to_broadcast([32, 128])
                            else:
                                sel = zb[32 * i:32 * i + 32, t_, :]
                            t = T(None, te.matmul, o, sel, nmT[32 * i:32 * i + 32, :], start=False, stop=True, inc=(j == 3))
                        t = S([t, t_b, s.t_o if half else None], se.activation, Pm[:, i, :], bk[i][:, :], ACT.Exp, scale=scale)
                        s.bf[i] = t
                        t_x.append(t)
                    yield
                    nbk = 1 if L == 0 else 2
                    per = 16 // nbk
                    for q in range(nbk):
                        for hh in range(per):
                            h16 = q * per + hh
                            h = half * 16 + h16
                            t = T([t_x, t_v, s.bf[q]], te.matmul, bk[q][:, hh * E:(hh + 1) * E],
                                  Pm[:, h16 % 4, (h16 // 4) * 128:(h16 // 4 + 1) * 128], vt[:, h, :],
                                  start=True, stop=True, inc=(hh == per - 1))
                        ov = bk[q][:, 0:per * E].rearrange("p (h e) -> p h e", e=E)
                        hs = slice(half * 16 + q * per, half * 16 + (q + 1) * per)
                        if L == 0:
                            t1 = V([t, t_b], ve.reciprocal, rec[:, 0:16].unsqueeze(2), ov[:, :, 8:9])
                            t1 = V(t1, ve.tensor_tensor, O[:, hs, :], ov[:, :, 0:8],
                                   bc(rec[:, 0:16], 2, [128, 16, 8]), ALU.mult)
                        else:
                            tA = tmp[:, 0:128].rearrange("p (h e) -> p h e", e=16)
                            t1 = V([t, t_b], ve.reciprocal, rec[:, 0:8].unsqueeze(2), ov[:, :, 16:17])
                            t1 = V(t1, ve.reciprocal, rec[:, 8:16].unsqueeze(2), ov[:, :, 33:34])
                            t2 = V(t1, ve.tensor_tensor, O[:, hs, :], ov[:, :, 0:16],
                                   bc(rec[:, 0:8], 2, [128, 8, 16]), ALU.mult)
                            t2 = V(t1, ve.tensor_tensor, tA, ov[:, :, 17:33],
                                   bc(rec[:, 8:16], 2, [128, 8, 16]), ALU.mult)
                            t1 = V(t2, ve.tensor_tensor, O[:, hs, :], O[:, hs, :], tA, ALU.add)
                        s.bf[q] = t1
                        s.t_o = t1
                    yield
                for k in range(2):
                    t = T([s.t_o, s.bf[2]], te.transpose, bk[2][:, k * 128:(k + 1) * 128],
                          O[:, :, :].rearrange("p h e -> p (h e)")[:, k * 128:(k + 1) * 128], ident, inc=(k == 1))
                t = S([t, t_b], se.copy, OT, bk[2][:, 0:256].rearrange("p (k n) -> p k n", k=2))
                s.bf[2] = t
                yield
                T([t, s.bf[3]], te.matmul, bk[3][:, 0:256], OT[:, 0], w["wo"][:, 0], start=True, stop=False, inc=0)
                T(None, te.matmul, bk[3][:, 0:256], OT[:, 1], w["wo"][:, 1], start=False, stop=False, inc=0)
                t = T(None, te.matmul, bk[3][:, 0:256], ones_row, w["bo"][0:1, :], start=False, stop=True)
                t = add_x(s, b, bk[3][:, 0:256], t)
                s.bf[3] = t
                t_b = [t]
                yield
            s.done = t
            s.x_t[u] = t

        def big_init(s, L):
            kv = 2 if L == 1 else 4
            vt = s.ar[:, 4096:4096 + kv * 129].rearrange("p (h e) -> p h e", e=129)
            s.t_init = V([s.done, ts], ve.memset, vt[:, :, 128:129], 1.0)
            return
            yield

        def big_attn(s, u, L):
            w = W[2 if L == 1 else 6]
            kv = 2 if L == 1 else 4
            scale = 1.0 / math.sqrt(128.0)
            bk = s.bk
            t_ln = ln(s, u)
            yield
            t_xT = xpose(s, t_ln)
            yield
            qn = s.ar[:, 0:512]
            kn = s.ar[:, 512:1024]
            sq = s.ar[:, 1024:2048]
            qT = s.ar[:, 2048:2560].rearrange("p (h n) -> p h n", n=128)
            kT = s.ar[:, 2560:3072].rearrange("p (h n) -> p h n", n=128)
            Pm = s.ar[:, 3072:3584].rearrange("p (h n) -> p h n", n=128)
            O = s.ar[:, 3584:4096].rearrange("p (h n) -> p h n", n=128)
            vt = s.ar[:, 4096:4096 + kv * 129].rearrange("p (h e) -> p h e", e=129)
            OT = s.ar[:, 4700:5212].rearrange("p (h n) -> p h n", n=128)
            nmT = s.ar[0:4, 5212:5276].bitcast(BF16)
            vm = s.ar[:, 5280:5280 + kv * 129].rearrange("p (h e) -> p h e", e=129)
            mrow = s.ar[0:1, 5800:5928]
            ms = s.sm[:, 32:40]
            nm = s.sm[:, 40:44]
            rec = s.sm[:, 44:48]
            zz = s.sm[:, 48:52]
            t_b = [s.done, t_xT]
            for bb in range(2):
                b = 2 * u + bb
                cx = ctxT[:, b * 128:(b + 1) * 128]
                tok = slice(bb * 128, (bb + 1) * 128)
                t_mr = None
                if L == 1:
                    t = T([s.bf[1], t_const], te.transpose, bk[1][0:1, 0:128], mbias[:, b:b + 1], ident)
                    t_mr = V([t, t_b], ve.tensor_scalar, mrow, bk[1][0:1, 0:128], -30000.0, None, ALU.max)
                    s.bf[1] = t_mr
                for c in range(4):
                    deps = [w["t"], t_xT, t_const, t_ctx]
                    if L == 1:
                        for h in range(4):
                            for k in range(2):
                                t = T([deps, s.bf[0]], te.matmul, bk[0][:, h * 128:(h + 1) * 128],
                                      w["wq"][:, k, (4 * c + h) * 128:(4 * c + h + 1) * 128], s.xT[:, k, tok],
                                      start=(k == 0), stop=(k == 1), inc=(k == 1 and h == 3))
                        for h in range(2):
                            t1 = T(s.bf[1], te.matmul, bk[1][:, h * 128:(h + 1) * 128],
                                   w["wk"][:, (2 * c + h) * 128:(2 * c + h + 1) * 128], cx,
                                   start=True, stop=True, inc=(h == 1))
                        t2 = T(s.bf[2], te.matmul, bk[2][:, 0:256], cx, w["wv"][:, c * 256:(c + 1) * 256],
                               start=True, stop=True)
                        yield
                        t_q = S([t, t_b], se.copy, qT, bk[0][:, :].rearrange("p (h n) -> p h n", h=4))
                        s.bf[0] = t_q
                        t_k = V([t1, t_b], ve.tensor_copy, kT[:, 0:2, :], bk[1][:, 0:256].rearrange("p (h n) -> p h n", h=2))
                        s.bf[1] = t_k
                        mk = mkey[:, b:b + 1]
                        t_v = V([t2, t_b, s.t_init], ve.tensor_scalar, vm[:, :, 0:128],
                                bk[2][:, 0:256].rearrange("p (h n) -> p h n", h=2), mk, None, ALU.mult)
                        s.bf[2] = t_v
                        t_v = V(None, ve.tensor_scalar, vm[:, :, 128:129], vt[:, :, 128:129], mk, None, ALU.mult)
                        va = vm
                    else:
                        for k in range(2):
                            t = T([deps, s.bf[0]], te.matmul, bk[0][:, :], s.xT[:, k, tok],
                                  w["wq"][:, k, c * 512:(c + 1) * 512], start=(k == 0), stop=(k == 1), inc=(k == 1))
                        t1 = T(s.bf[1], te.matmul, bk[1][:, :], cx, w["wk"][:, c * 512:(c + 1) * 512], start=True, stop=True)
                        t2 = T(s.bf[2], te.matmul, bk[2][:, :], cx, w["wv"][:, c * 512:(c + 1) * 512], start=True, stop=True)
                        yield
                        ta = S([t, t_b], se.activation, sq[:, 0:512], bk[0][:, :], ACT.Square)
                        tb = S(t1, se.activation, sq[:, 512:1024], bk[1][:, :], ACT.Square)
                        t_v = S([t2, s.t_init], se.copy, vt[:, :, 0:128], bk[2][:, :].rearrange("p (h n) -> p h n", h=4))
                        s.bf[2] = t_v
                        t3 = V([ta, tb, t_b], ve.tensor_reduce, ms, sq.rearrange("p (h n) -> p h n", h=8), AX.X, ALU.add)
                        t3 = P(t3, pe_.tensor_scalar, ms, ms, 1.0 / 128, 1e-5, ALU.mult, ALU.add)
                        t3 = P(t3, pe_.tensor_tensor, ms, ms, neghalf[:, 0:8], ALU.pow)
                        yield
                        t_qn = V([t3, t_b], ve.tensor_tensor, qn.rearrange("p (h n) -> p h n", h=4),
                                 bk[0][:, :].rearrange("p (h n) -> p h n", h=4), bc(ms[:, 0:4], 2, [128, 4, 128]), ALU.mult)
                        s.bf[0] = t_qn
                        t_kn = V(None, ve.tensor_tensor, kn.rearrange("p (h n) -> p h n", h=4),
                                 bk[1][:, :].rearrange("p (h n) -> p h n", h=4), bc(ms[:, 4:8], 2, [128, 4, 128]), ALU.mult)
                        s.bf[1] = t_kn
                        yield
                        for h in range(4):
                            t = T([t_qn, s.bf[2]], te.transpose, bk[2][:, h * 128:(h + 1) * 128], qn[:, h * 128:(h + 1) * 128], ident, inc=(h == 3))
                        for h in range(4):
                            t1 = T([t_kn, s.bf[0]], te.transpose, bk[0][:, h * 128:(h + 1) * 128], kn[:, h * 128:(h + 1) * 128], ident, inc=(h == 3))
                        t_q = S([t, t_b], se.copy, qT, bk[2][:, :].rearrange("p (h n) -> p h n", h=4))
                        s.bf[2] = t_q
                        t_k = V([t1, t_b, t_gp], ve.tensor_scalar, kT, bk[0][:, :].rearrange("p (h n) -> p h n", h=4),
                                gp[:, 0:1], None, ALU.mult)
                        s.bf[0] = t_k
                        va = vt
                    yield
                    for h in range(4):
                        kh = h // 2 if L == 1 else h
                        T([t_q, t_k, s.bf[0]], te.matmul, bk[0][:, h * 128:(h + 1) * 128], qT[:, h], kT[:, kh],
                          start=True, stop=(L == 3), inc=0) if L == 1 else None
                        if L == 1:
                            t = T(t_mr, te.matmul, bk[0][:, h * 128:(h + 1) * 128], ones_row, mrow, start=False, stop=True,
                                  inc=(h == 3))
                        else:
                            t = T([t_q, t_k, s.bf[0]], te.matmul, bk[0][:, h * 128:(h + 1) * 128], qT[:, h], kT[:, kh],
                                  start=True, stop=True, inc=(h == 3))
                    t_m = V([t, t_b], ve.tensor_reduce, nm, bk[0][:, :].rearrange("p (h n) -> p h n", h=4), AX.X, ALU.max)
                    s.bf[0] = t_m
                    yield
                    t = T([t_m, s.bf[1]], te.transpose, bk[1][0:4, 0:128], nm, ident)
                    t_n = S([t, t_b], se.mul, nmT, bk[1][0:4, 0:128], -1.0)
                    s.bf[1] = t_n
                    yield
                    for h in range(4):
                        kh = h // 2 if L == 1 else h
                        o = bk[2][:, h * 128:(h + 1) * 128]
                        T([t_n, s.bf[2]], te.matmul, o, kT[:, kh], qT[:, h], start=True, stop=False, inc=0)
                        t = T(None, te.matmul, o, idb[0:4, h:h + 1].to_broadcast([4, 128]), nmT, start=False, stop=True, inc=(h == 3))
                    kw = {"scale": scale}
                    if L == 1:
                        kw["bias"] = mbias[:, b:b + 1]
                    t_x = S([t, t_b], se.activation, Pm, bk[2][:, :].rearrange("p (h n) -> p h n", h=4), ACT.Exp, **kw)
                    s.bf[2] = t_x
                    yield
                    for h in range(4):
                        kh = h // 2 if L == 1 else h
                        q = h // 2
                        t = T([t_x, t_v, s.bf[q]], te.matmul, bk[q][:, (h % 2) * 129:(h % 2 + 1) * 129], Pm[:, h], va[:, kh],
                              start=True, stop=True, inc=(h % 2 == 1))
                        if h % 2:
                            ov = bk[q][:, 0:258].rearrange("p (h e) -> p h e", e=129)
                            rq = rec[:, 2 * q:2 * q + 2]
                            if L == 1:
                                zq = zz[:, 2 * q:2 * q + 2]
                                t1 = V([t, t_b], ve.tensor_scalar, zq.unsqueeze(2), ov[:, :, 128:129], 0.0, None, ALU.is_equal)
                                t1 = V(t1, ve.tensor_tensor, zq.unsqueeze(2), zq.unsqueeze(2), ov[:, :, 128:129], ALU.add)
                                t1 = V(t1, ve.reciprocal, rq, zq)
                            else:
                                t1 = V([t, t_b], ve.reciprocal, rq.unsqueeze(2), ov[:, :, 128:129])
                            t_o = V(t1, ve.tensor_tensor, O[:, 2 * q:2 * q + 2], ov[:, :, 0:128], bc(rq, 2, [128, 2, 128]), ALU.mult)
                            s.bf[q] = t_o
                    yield
                    for h in range(4):
                        t = T([t_o, s.bf[2]], te.transpose, bk[2][:, h * 128:(h + 1) * 128], O[:, h], ident, inc=(h == 3))
                    t = S([t, t_b], se.copy, OT, bk[2][:, :].rearrange("p (h n) -> p h n", h=4))
                    s.bf[2] = t
                    yield
                    for h in range(4):
                        t = T([t, s.bf[3]], te.matmul, bk[3][:, 0:256], OT[:, h], w["wo"][:, 4 * c + h],
                              start=(c == 0 and h == 0), stop=(c == 3 and h == 3), inc=(h == 3))
                    t_b = [t]
                    yield
                t = add_x(s, b, bk[3][:, 0:256], t)
                s.bf[3] = t
                t_b = [t]
                yield
            s.done = t
            s.x_t[u] = t

        def peer(s, u):
            w = W[1]
            bk = s.bk
            t_ln = ln(s, u)
            yield
            t_xT = xpose(s, t_ln)
            yield
            G = s.ar[:, 0:4096].rearrange("p (e n) -> p e n", n=256)
            B = s.ar[:, 4096:6144].bitcast(F16).rearrange("p (g n) -> p g n", n=128)
            Am = s.ar[:, 6144:8192].bitcast(F16).rearrange("p (g a n) -> p g a n", a=2, n=64)
            qT = s.ar[:, 4096:5120].rearrange("p (h n) -> p h n", n=256)
            sims = s.ar[:, 5120:6144].rearrange("p (a h n) -> p a h n", a=2, h=4)
            oh = s.ar[:, 6144:7168].bitcast(F16).rearrange("p (g n) -> p g n", n=64)
            e1 = s.ar[:, 7168:7424]
            al = s.ar[:, 7424:7680]
            s8 = s.ar[:, 7680:7744].rearrange("p (a h k) -> p a h k", a=2, h=4)
            i8 = s.ar[:, 7744:7808].bitcast(U32)
            i8f = s.ar[:, 7808:7872]
            f8 = s.ar[:, 7872:7904].rearrange("p (h k) -> p h k", h=4)
            pk = s.ar[:, 7904:7936].bitcast(U32)
            pk2 = s.ar[:, 7936:8000].bitcast(U32)
            pkf = s.ar[:, 8000:8064]
            isel = s.ar[:, 8064:8128]
            idx = s.ar[:, 8128:8160]
            iu = s.ar[:, 8160:8192].bitcast(U32)
            iv = s.ar[:, 8192:8256].bitcast(U32)
            wh = s.ar[:, 8256:8352]
            tr = s.ar[:, 8352:8448]
            trh = s.ar[:, 8448:8512].bitcast(F16)
            rest = s.ar[:, 8512:8544]
            t_b = [s.done, t_xT]
            for j in range(8):
                for e in range(2):
                    for k in range(2):
                        t = T([w["t"], t_xT, s.bf[j % 4]], te.matmul, bk[j % 4][:, e * 256:(e + 1) * 256],
                              w["ed"][:, k, (2 * j + e) * 128:(2 * j + e + 1) * 128], s.xT[:, k, :],
                              start=(k == 0), stop=(k == 1), inc=(k == 1 and e == 1))
                t = S([t, t_b], se.activation, G[:, 2 * j:2 * j + 2, :], bk[j % 4][:, :].rearrange("p (e n) -> p e n", e=2), ACT.Silu)
                s.bf[j % 4] = t
                if j % 4 == 3:
                    yield
            t_g = t
            t_prev = t_b
            for bb in range(2):
                b = 2 * u + bb
                tok = slice(bb * 128, (bb + 1) * 128)
                for h in range(4):
                    for k in range(2):
                        t = T([s.bf[0]], te.matmul, bk[0][:, h * 128:(h + 1) * 128], w["wq"][:, k, h * 128:(h + 1) * 128],
                              s.xT[:, k, tok], start=(k == 0), stop=(k == 1), inc=(h == 3 and k == 1))
                t = S([t, t_prev], se.copy, qT[:, :, 0:128], bk[0][:, :].rearrange("p (h n) -> p h n", h=4))
                s.bf[0] = t
                yield
                for a in range(2):
                    for h in range(4):
                        tt = T([t, s.bf[1 + a]], te.matmul, bk[1 + a][:, h * 128:(h + 1) * 128],
                               qT[64 * a:64 * a + 64, h, 0:128], w["keys"][64 * a:64 * a + 64, h, :],
                               start=True, stop=True, inc=(h == 3))
                    ts_ = S([tt, t_prev], se.copy, sims[:, a], bk[1 + a][:, :].rearrange("p (h n) -> p h n", h=4))
                    s.bf[1 + a] = ts_
                yield
                for a in range(2):
                    for h in range(4):
                        t = V([ts_, t_prev], ve.max, s8[:, a, h], sims[:, a, h])
                for a in range(2):
                    for h in range(4):
                        t2 = V(t, ve.max_index, i8[:, (a * 4 + h) * 8:(a * 4 + h + 1) * 8], s8[:, a, h], sims[:, a, h])
                al4 = al.rearrange("p (h i j) -> p h i j", h=4, i=8)
                t = V(t, ve.tensor_tensor, al4, bc(s8[:, 0], 3, [128, 4, 8, 8]), bc(s8[:, 1], 2, [128, 4, 8, 8]), ALU.add)
                t2 = V(t2, ve.tensor_copy, i8f, i8)
                for h in range(4):
                    t3 = V(t, ve.max, f8[:, h], al[:, h * 64:(h + 1) * 64])
                for h in range(4):
                    t3_ = V(t3, ve.max_index, pk[:, h * 8:(h + 1) * 8], f8[:, h], al[:, h * 64:(h + 1) * 64])
                t4 = V(t3_, ve.tensor_scalar, pk2[:, 0:32], pk, 3, None, ALU.logical_shift_right)
                t4 = V(t3_, ve.tensor_scalar, pk2[:, 32:64], pk, 7, None, ALU.bitwise_and)
                t4 = V(t4, ve.tensor_copy, pkf, pk2)
                yield
                for a in range(2):
                    e2 = e1.rearrange("p (m j) -> p m j", j=8)
                    t5 = V([t4, s.t_e], ve.tensor_tensor, e2, bc(iota8, 1, [128, 32, 8]),
                           bc(pkf[:, 32 * a:32 * a + 32], 2, [128, 32, 8]), ALU.is_equal)
                    e4 = e1.rearrange("p (h k j) -> p h k j", h=4, k=8)
                    iv4 = i8f[:, 32 * a:32 * a + 32].rearrange("p (h j) -> p h j", h=4)
                    t5 = V([t5, t2], ve.tensor_tensor, e4, e4, bc(iv4, 2, [128, 4, 8, 8]), ALU.mult)
                    t5 = V(t5, ve.tensor_reduce, isel[:, 32 * a:32 * a + 32], e2, AX.X, ALU.add)
                    s.t_e = t5
                t5 = V(t5, ve.scalar_tensor_tensor, idx, isel[:, 0:32], 128.0, isel[:, 32:64], ALU.mult, ALU.add)
                t5 = V(t5, ve.tensor_scalar, idx, idx, 2047.0, None, ALU.min)
                t5 = V(t5, ve.tensor_copy, iu, idx)
                V(t5, ve.tensor_scalar, iv[:, 0:32], iu, 7, None, ALU.logical_shift_right)
                t5 = V(None, ve.tensor_scalar, iv[:, 32:64], iu, 127, None, ALU.bitwise_and)
                t5 = V(t5, ve.tensor_copy, wh[:, 0:64], iv)
                t5 = V(t5, ve.tensor_scalar, wh[:, 64:96], f8.rearrange("p h k -> p (h k)"), 0.0, None, ALU.max)
                for q in range(3):
                    t6 = V(t5, ve.transpose, tr[:, 32 * q:32 * q + 32], wh[:, 32 * q:32 * q + 32])
                V(t6, ve.tensor_scalar, trh[:, 0:32], tr[:, 0:32], cst[:, C_PC:C_PC + 1], None, ALU.add)
                t7 = V(None, ve.tensor_copy, trh[:, 32:96], tr[:, 32:96])
                t7 = V(t7, ve.tensor_tensor, rest, tr[:, 64:96], trh[:, 64:96], ALU.subtract)
                t7 = V(t7, ve.tensor_copy, trh[:, 96:128], rest)
                yield
                t8 = V([t7, t_prev], ve.tensor_tensor, B, bc(i128h[:, :], 1, [128, 32, 128]),
                       bc(trh[:, 32:64], 2, [128, 32, 128]), ALU.is_equal)
                ohv = s.oh[:, :].rearrange("p (g n) -> p g n", n=64)
                t9 = V([t7, t_prev], ve.tensor_tensor, ohv, bc(i64h[:, :], 1, [128, 32, 64]),
                       bc(trh[:, 0:32], 2, [128, 32, 64]), ALU.is_equal)
                for a in range(2):
                    t10 = P(t9, pe_.tensor_tensor, Am[:, :, a], ohv, bc(trh[:, 64 + 32 * a:96 + 32 * a], 2, [128, 32, 64]), ALU.mult)
                yield
                for j in range(4):
                    for g in range(8):
                        for a in range(2):
                            t = T([t8, t10, s.bf[j]], te.matmul, bk[j][:, g * 64:(g + 1) * 64], B[:, 8 * j + g, :], Am[:, 8 * j + g, a, :],
                                  start=(a == 0), stop=(a == 1), inc=(g == 7 and a == 1))
                    src = bk[j][:, :].rearrange("p (g c e) -> p e c g", g=8, c=4)
                    dst = G[:, :, tok].rearrange("p e (c g) -> p e c g", c=4)[:, :, :, 8 * j:8 * j + 8]
                    t = V([t, t_g], ve.tensor_tensor, dst, dst, src, ALU.mult)
                    s.bf[j] = t
                t_gm = t
                yield
                for e in range(16):
                    t = T([t_gm, s.bf[0]], te.matmul, bk[0][:, 0:256], G[:, e, tok], w["eu"][:, e, :],
                          start=(e == 0), stop=(e == 15), inc=(e == 15))
                t = add_x(s, b, bk[0][:, 0:256], t)
                s.bf[0] = t
                t_prev = [t]
                yield
            s.done = t
            s.x_t[u] = t

        def moe(s, u):
            w = W[3]
            bk = s.bk
            t_ln = ln(s, u)
            yield
            t_xT = xpose(s, t_ln)
            yield
            pr = s.sm[:, 32:48].rearrange("p (b e) -> p b e", b=2)
            bg = s.sm[:, 48:56]
            s8 = s.sm[:, 56:64]
            i8 = s.sm[:, 64:72].bitcast(U32)
            i8f = s.sm[:, 72:80]
            sel = s.sm[:, 80:96]
            mk = s.sm[:, 96:104]
            mm = s.sm[:, 104:106]
            pT = s.ar[0:8, 0:256].rearrange("p (b n) -> p b n", b=2)
            uT = s.ar[:, 256:768].rearrange("p (k n) -> p k n", k=2)
            gT = s.ar[:, 768:1280].rearrange("p (k n) -> p k n", k=2)
            acc = s.ar[:, 1280:1792].rearrange("p (b n) -> p b n", b=2)
            t_b = [s.done, t_xT]
            for bb in range(2):
                tok = slice(bb * 128, (bb + 1) * 128)
                r = bk[1][:, 0:7]
                T([w["t"], ts, t_xT, s.bf[1], t_const], te.matmul, r, s.xT[:, 0, tok], wr[:, 0], start=True, stop=False, inc=0)
                T(None, te.matmul, r, s.xT[:, 1, tok], wr[:, 1], start=False, stop=False, inc=0)
                T(None, te.matmul, r, ones_row, rb[0:1, 0:7], start=False, stop=True, inc=0)
                T(None, te.matmul, bk[1][:, 8:15], s.xT[:, 0, tok], wr[:, 0], start=True, stop=False, inc=0)
                T(None, te.matmul, bk[1][:, 8:15], s.xT[:, 1, tok], wr[:, 1], start=False, stop=False, inc=0)
                T(None, te.matmul, bk[1][:, 8:15], ones_row, rb[0:1, 0:7], start=False, stop=False, inc=0)
                t = T(None, te.matmul, bk[1][:, 8:15], ones_row, rb[0:1, 8:15], start=False, stop=True)
                t1 = V([t_b, s.done], ve.memset, bg, -3e38)
                t1 = V([t, t1], ve.tensor_copy, bg[:, 0:7], bk[1][:, 8:15])
                t1 = V(t1, ve.max, s8, bg)
                t1 = V(t1, ve.max_index, i8, s8, bg)
                t1 = V(t1, ve.tensor_copy, i8f, i8)
                t2 = V(t1, ve.tensor_scalar, sel[:, 0:8], iota8, i8f[:, 0:1], None, ALU.is_equal)
                t2 = V(t1, ve.tensor_scalar, sel[:, 8:16], iota8, i8f[:, 1:2], None, ALU.is_equal)
                t2 = V(t2, ve.tensor_tensor, sel[:, 0:8], sel[:, 0:8], sel[:, 8:16], ALU.add)
                t2 = V(t2, ve.tensor_scalar, mk, sel[:, 0:8], -1.0, 1e30, ALU.add, ALU.mult)
                t2 = V(t2, ve.tensor_tensor, mk[:, 0:7], mk[:, 0:7], bk[1][:, 0:7], ALU.add)
                s.bf[1] = t2
                t2 = V(t2, ve.tensor_reduce, mm[:, 0:1], mk[:, 0:7], AX.X, ALU.max)
                t2 = V(t2, ve.tensor_scalar, mk[:, 0:7], mk[:, 0:7], mm[:, 0:1], None, ALU.subtract)
                t2 = S(t2, se.activation, mk[:, 0:7], mk[:, 0:7], ACT.Exp)
                t2 = V(t2, ve.tensor_reduce, mm[:, 1:2], mk[:, 0:7], AX.X, ALU.add)
                t2 = V(t2, ve.reciprocal, mm[:, 1:2], mm[:, 1:2])
                V(None, ve.memset, pr[:, bb, 7:8], 1.0)
                t2 = V(t2, ve.tensor_scalar, pr[:, bb, 0:7], mk[:, 0:7], mm[:, 1:2], None, ALU.mult)
                t_b = [t_b, t2]
                yield
                t = T([t2, s.bf[0]], te.transpose, bk[0][0:8, bb * 128:(bb + 1) * 128], pr[:, bb, :], ident)
            t_p = t2
            t = V([t, t_b], ve.tensor_copy, pT, bk[0][0:8, 0:256].rearrange("p (b n) -> p b n", b=2))
            s.bf[0] = t
            yield
            for bb in range(2):
                t = T([t, s.bf[1]], te.matmul, bk[1][:, bb * 256:(bb + 1) * 256], pT[:, bb], bdn[:, :], start=True, stop=True)
            t_acc = V([t, t_b], ve.tensor_tensor, acc, x[:, 2 * u:2 * u + 2, :], bk[1][:, :].rearrange("p (b n) -> p b n", b=2), ALU.add)
            s.bf[1] = t_acc
            t_u_rd = None
            t_g_rd = None
            for e in range(8):
                for m in range(2):
                    for k in range(2):
                        t = T([t_xT, s.bf[0]], te.matmul, bk[0][:, m * 256:(m + 1) * 256], w["Wup"][:, e, k, m * 128:(m + 1) * 128],
                              s.xT[:, k, :], start=(k == 0), stop=(k == 1), inc=(k == 1 and m == 1))
                b0 = bk[0][:, :].rearrange("p (m n) -> p m n", m=2)
                b2 = bk[2][:, :].rearrange("p (m n) -> p m n", m=2)
                for m in range(2):
                    t_u = V([t, t_b, t_g_rd], ve.tensor_scalar, uT[:, m], b0[:, m], bu[:, 0, 2 * e + m:2 * e + m + 1], None, ALU.add)
                s.bf[0] = t_u
                yield
                for m in range(2):
                    for k in range(2):
                        t = T([t_u, s.bf[2]], te.matmul, bk[2][:, m * 256:(m + 1) * 256], w["Wgate"][:, e, k, m * 128:(m + 1) * 128],
                              uT[:, k], start=(k == 0), stop=(k == 1), inc=(k == 1 and m == 1))
                for m in range(2):
                    t_s = S([t, t_b, t_g_rd], se.activation, gT[:, m], b2[:, m], ACT.Silu, bias=bu[:, 1, 2 * e + m:2 * e + m + 1])
                s.bf[2] = t_s
                t_g = V([t_s, t_g_rd], ve.tensor_tensor, gT, gT, uT, ALU.mult)
                yield
                for bb in range(2):
                    for k in range(2):
                        t = T([t_g, s.bf[3]], te.matmul, bk[3][:, bb * 256:(bb + 1) * 256], gT[:, k, bb * 128:(bb + 1) * 128],
                              w["Wdown"][:, e, k, :], start=(k == 0), stop=(k == 1), inc=(k == 1 and bb == 1))
                t_g_rd = t
                for bb in range(2):
                    dst = acc[:, bb] if e < 7 else x[:, 2 * u + bb]
                    t_acc = V([t, t_acc, t_p], ve.scalar_tensor_tensor, dst, bk[3][:, bb * 256:(bb + 1) * 256],
                              pr[:, bb, e:e + 1], acc[:, bb], ALU.mult, ALU.add)
                s.bf[3] = t_acc
                yield
            s.done = t_acc
            s.x_t[u] = t_acc

        def tern_prep():
            w = W[5]
            s = slots[0]
            tmp = w["tmp"]
            sm = s.sm
            t0 = [slots[0].done, slots[1].done, w["t"]]
            raw = area[1]
            t = V(t0, ve.tensor_reduce, sm[:, 0:1], raw[:, 0:1364], AX.X, ALU.add, apply_absolute_value=True)
            t = V(t0, ve.tensor_reduce, sm[:, 1:2], raw[:, 1364:2728], AX.X, ALU.add, apply_absolute_value=True)
            t = V(t0, ve.tensor_reduce, sm[:, 2:3], raw[:, 2728:2728 + 1280], AX.X, ALU.add, apply_absolute_value=True)
            t = V(t0, ve.tensor_reduce, sm[0:42, 3:4], raw[0:42, 4008:4264], AX.X, ALU.add, apply_absolute_value=True)
            t = V(t, ve.tensor_tensor, sm[0:42, 2:3], sm[0:42, 2:3], sm[0:42, 3:4], ALU.add)
            t = T([t, s.bf[0]], te.matmul, s.bk[0][:, 0:3], ones_sq, sm[:, 0:3], start=True, stop=True)
            t = V(t, ve.tensor_scalar, sm[:, 4:7], s.bk[0][:, 0:3], 1.0 / (682 * 256), None, ALU.mult)
            s.bf[0] = t
            t = V(t, ve.tensor_scalar, sm[:, 8:11], sm[:, 4:7], 0.5, None, ALU.mult)
            t = V(t, ve.tensor_scalar, sm[:, 12:15], sm[:, 4:7], -0.5, None, ALU.mult)
            for j, (lo, hi, rows) in enumerate(((0, 1364, 128), (1364, 2728, 128), (2728, 4008, 128), (4008, 4264, 42))):
                q = min(j, 2)
                r = raw[0:rows, lo:hi]
                m = tmp[0:rows, lo:hi]
                t1 = V(t, ve.tensor_scalar, m, r, sm[0:rows, 8 + q:9 + q], None, ALU.is_gt)
                t2 = V(t, ve.tensor_scalar, s.ar[0:rows, 0:hi - lo], r, sm[0:rows, 12 + q:13 + q], None, ALU.is_lt)
                t2 = V([t1, t2], ve.tensor_tensor, m, m, s.ar[0:rows, 0:hi - lo], ALU.subtract)
                t2 = V(t2, ve.scalar_tensor_tensor, m, m, sm[0:rows, 4 + q:5 + q], r, ALU.mult, ALU.subtract)
                t = V(t2, ve.tensor_tensor, r, r, m, ALU.add)
            w["tq"] = t
            slots[0].done = [slots[0].done, t]
            slots[1].done = [slots[1].done, t]

        def tern(s, u):
            w = W[5]
            bk = s.bk
            t_ln = ln(s, u)
            yield
            t_xT = xpose(s, t_ln)
            yield
            a = s.ar[:, 0:1024].rearrange("p (c n) -> p c n", c=2)
            g = s.ar[:, 1024:2560].rearrange("p (k n) -> p k n", k=6)
            t_b = [s.done, t_xT]
            for c in range(3):
                j = 2 * (c % 2)
                ca = a[:, c % 2]
                for q, wm in ((0, w["w1"]), (1, w["w3"])):
                    for m in range(2):
                        mt = 2 * c + m
                        M = 42 if mt == 5 else 128
                        for k in range(2):
                            t = T([t_xT, w["tq"], s.bf[j + q]], te.matmul, bk[j + q][0:M, m * 256:(m + 1) * 256],
                                  wm[:, k, mt * 128:mt * 128 + M], s.xT[:, k, :], start=(k == 0), stop=(k == 1),
                                  inc=(k == 1 and m == 1))
                parts = ((0, 2, 128),) if c < 2 else ((0, 1, 128), (1, 2, 42))
                for lo, hi, M in parts:
                    cs_ = slice(lo * 256, hi * 256)
                    t1 = S([t, t_b, s.t_a.get(c % 2)], se.activation, ca[0:M, cs_], bk[j][0:M, cs_], ACT.Silu)
                    t2 = V([t1, t], ve.tensor_tensor, g[0:M, 2 * c + lo:2 * c + hi, :].rearrange("p k n -> p (k n)"),
                           ca[0:M, cs_], bk[j + 1][0:M, cs_], ALU.mult)
                s.bf[j] = t1
                s.bf[j + 1] = t2
                s.t_a[c % 2] = t2
                yield
            for bb in range(2):
                for k in range(6):
                    M = 42 if k == 5 else 128
                    t = T([t2, s.bf[0]], te.matmul, bk[0][:, bb * 256:(bb + 1) * 256], g[0:M, k, bb * 128:(bb + 1) * 128],
                          w["w2"][0:M, k, :], start=(k == 0), stop=(k == 5), inc=(k == 5))
            t = V(t, ve.tensor_tensor, x[:, 2 * u:2 * u + 2, :], x[:, 2 * u:2 * u + 2, :],
                  bk[0][:, :].rearrange("p (b n) -> p b n", b=2), ALU.add)
            s.bf[0] = t
            s.done = t
            s.x_t[u] = t
            yield

        def quant(s_, src, dst, n, sc, tm, waits):
            nb = n // 32
            s3 = src.rearrange("p (b k) -> p b k", k=32)
            d3 = dst.rearrange("p (b k) -> p b k", k=32)
            am, iv = sc[:, 0:nb], sc[:, 32:32 + nb]
            t = V(waits, ve.tensor_reduce, am, s3, AX.X, ALU.max, apply_absolute_value=True)
            t = V(t, ve.tensor_scalar, am, am, 1.0 / 448.0, 1e-30, ALU.mult, ALU.max)
            t = V(t, ve.reciprocal, iv, am)
            t = V(t, ve.tensor_tensor, d3, s3, bc(iv, 2, [128, nb, 32]), ALU.mult)
            yield
            t = V(t, ve.tensor_scalar, tm.bitcast(U32), dst.bitcast(U32), 0x7f800000, None, ALU.bitwise_and)
            t = V(t, ve.tensor_scalar, tm, tm, 1572864.0, 24576.0, ALU.mult, ALU.max)
            t = V(t, ve.tensor_tensor, dst, dst, tm, ALU.add)
            t = V(t, ve.tensor_tensor, dst, dst, tm, ALU.subtract)
            yield
            t = V(t, ve.tensor_tensor, d3, d3, bc(am, 2, [128, nb, 32]), ALU.mult)
            s_.t_q = t
            return t

        def mx_prep(s):
            w = W[7]
            raw = w["raw"].rearrange("p a n -> p (a n)")
            bk = s.bk
            t = s.done
            jj = 0
            for blk in range(s.i, 6, 2):
                q = s.ar[:, 0:1024]
                t = yield from quant(s, raw[:, blk * 1024:(blk + 1) * 1024], q, 1024, s.sm[:, 0:64], s.ar[:, 1024:2048],
                                     [s.done, w["t"], t])
                for i in range(4):
                    for k in range(2):
                        c = 2 * i + k
                        j = jj % 4
                        tt = T([t, s.bf[j], t_const], te.transpose, bk[j][:, 0:128], q[:, c * 128:(c + 1) * 128], ident)
                        if blk < 4:
                            r = 4 * (blk % 2) + i
                            dst = (w["g"], w["u"])[blk // 2][:, k, r * 128:(r + 1) * 128]
                        else:
                            dst = w["d"][:, c, (blk - 4) * 128:(blk - 3) * 128]
                        s.bf[j] = S(tt, se.copy, dst, bk[j][:, 0:128])
                        jj += 1
                t = [tt, s.bf[(jj - 1) % 4]]
                yield
            w.setdefault("tp", []).append(t)
            s.done = [s.done, t, s.t_q]

        def mx(s, u):
            w = W[7]
            bk = s.bk
            t_ln = ln(s, u)
            yield
            xf = s.xn[:, :, :].rearrange("p b n -> p (b n)")
            t = yield from quant(s, xf, xf, 512, s.sm[:, 32:96], s.ar[:, 0:512], [t_ln, s.done])
            t_xT = xpose(s, t)
            yield
            g = s.ar[:, 0:1024]
            h = s.ar[:, 1024:2048]
            tm = s.ar[:, 2048:3072]
            hT = s.ar[:, 3072:4096].rearrange("p (k n) -> p k n", k=8)
            t_b = [t_xT, s.done]
            for bb in range(2):
                b = 2 * u + bb
                tok = slice(bb * 128, (bb + 1) * 128)
                for c in range(2):
                    for q, wm in ((0, w["g"]), (2, w["u"])):
                        for k in range(2):
                            t = T([t_xT, w["tp"], s.bf[q + c]], te.matmul, bk[q + c][:, :], s.xT[:, k, tok],
                                  wm[:, k, c * 512:(c + 1) * 512], start=(k == 0), stop=(k == 1), inc=(k == 1))
                    t1 = S([t, t_b], se.activation, g[:, c * 512:(c + 1) * 512], bk[c][:, :], ACT.Silu)
                    s.bf[c] = t1
                    t2 = V([t1, t_b, t], ve.tensor_tensor, h[:, c * 512:(c + 1) * 512], g[:, c * 512:(c + 1) * 512],
                           bk[2 + c][:, :], ALU.mult)
                    s.bf[2 + c] = t2
                yield
                t = yield from quant(s, h, h, 1024, s.sm[:, 32:96], tm, t2)
                yield
                for c in range(2):
                    for k in range(4):
                        tt = T([t, s.bf[c]], te.transpose, bk[c][:, k * 128:(k + 1) * 128], h[:, (4 * c + k) * 128:(4 * c + k + 1) * 128],
                               ident, inc=(k == 3))
                    s.bf[c] = S([tt, t_b], se.copy, hT[:, 4 * c:4 * c + 4, :], bk[c][:, :].rearrange("p (k n) -> p k n", k=4))
                t = s.bf[1]
                yield
                for k in range(8):
                    t = T([t, s.bf[2]], te.matmul, bk[2][:, 0:256], hT[:, k, :], w["d"][:, k, :], start=(k == 0), stop=(k == 7),
                          inc=(k == 7))
                t = add_x(s, b, bk[2][:, 0:256], t)
                s.bf[2] = t
                t_b = [t]
                yield
            s.done = t
            s.x_t[u] = t

        for s in slots:
            s.oh = area[1][:, 9728 + 1024 * s.i:10752 + 1024 * s.i].bitcast(F16)

        def interleave(gens):
            gens = list(gens)
            while gens:
                for g in list(gens):
                    try:
                        next(g)
                    except StopIteration:
                        gens.remove(g)

        x_t = {u: [t_x0] for u in range(8)}
        for s in slots:
            s.x_t, s.t_e, s.t_a, s.t_o = x_t, None, {}, None
        ends = {}
        first, second = SUBS[0], (SUBS + (None,))[1]
        load_weights(first, None)
        ts = load_small()
        t_gp = V([ts], ve.tensor_tensor, gp[:, :], gqk[:, 0:1], gqk[:, 1:2], ALU.mult)
        if second is not None:
            load_weights(second, [] if second % 2 != first % 2 else None)
        for n, k in enumerate(SUBS):
            for s in slots:
                s.t_a, s.t_e = {}, None
            if k in (0, 4):
                interleave(small_init(s, 0 if k == 0 else 2) for s in slots)
            if k in (2, 6):
                interleave(big_init(s, 1 if k == 2 else 3) for s in slots)
            if k == 5:
                tern_prep()
            if k == 7:
                interleave(mx_prep(s) for s in slots)

            def units(s):
                for u in range(s.i, 8, 2):
                    if k in (0, 4):
                        yield from small_attn(s, u, 0 if k == 0 else 2)
                    if k in (2, 6):
                        yield from big_attn(s, u, 1 if k == 2 else 3)
                    if k == 1:
                        yield from peer(s, u)
                    if k == 3:
                        yield from moe(s, u)
                    if k == 5:
                        yield from tern(s, u)
                    if k == 7:
                        yield from mx(s, u)

            interleave(units(s) for s in slots)
            if n + 2 < len(SUBS):
                load_weights(SUBS[n + 2], [slots[0].done, slots[1].done])

        for u in range(8):
            t = st_o([x_t[u]], out[2 * u:2 * u + 2].rearrange("b t d -> t b d"), x[:, 2 * u:2 * u + 2, :])
        D([t], nc.sync.nop, inc=0)

        block = ctx.enter_context(nc.Block())

        @block.sync
        def _(eng):
            D.run(eng)

        @block.vector
        def _(eng):
            V.run(eng)

        @block.scalar
        def _(eng):
            S.run(eng)

        @block.tensor
        def _(eng):
            T.run(eng)

        @block.gpsimd
        def _(eng):
            P.run(eng)


_PLAIN = ["L0_xattn_Wq", "L0_xattn_Wkv", "L0_xattn_Wout", "L0_xattn_bout", "L0_ffn_Wq", "L0_ffn_e_up",
          "L1_xattn_Wq", "L1_xattn_Wk", "L1_xattn_Wv", "L1_xattn_Wo", "L1_ffn_Wr", "L1_ffn_br",
          "L1_ffn_gate_bias", "L1_ffn_Wup", "L1_ffn_Wgate", "L1_ffn_Wdown", "L1_ffn_Wsu", "L1_ffn_Wsg",
          "L1_ffn_Wsd", "L2_xattn_Wq", "L2_xattn_bq", "L2_xattn_Wk", "L2_xattn_bk", "L2_xattn_Wv",
          "L2_xattn_bv", "L2_xattn_Wkv_dca", "L2_xattn_bkv_dca", "L2_xattn_qn_w", "L2_xattn_qn_b",
          "L2_xattn_kn_w", "L2_xattn_kn_b", "L2_xattn_kn_dca_w", "L2_xattn_kn_dca_b", "L2_xattn_Wo",
          "L2_xattn_bo", "L3_xattn_Wq", "L3_xattn_Wk", "L3_xattn_Wv", "L3_xattn_Wo", "L3_ffn_gate_w",
          "L3_ffn_up_w", "L3_ffn_down_w"]


def _constants():
    c = np.zeros((128, C_N), np.float32)
    c[:, C_ID:C_ID + 128] = np.eye(128)
    c[:, C_I128:C_I128 + 128] = np.arange(128)
    c[:, C_I64:C_I64 + 64] = np.arange(64)
    c[:, C_I8:C_I8 + 8] = np.arange(8)
    p = np.arange(128)
    c[:, C_MM] = p < 112
    c[:, C_MD] = p >= 112
    c[:, C_PC] = 16 * (p // 32)
    z = np.zeros((4, 32, 16, 8), np.float32)
    for j in range(4):
        z[:, j, j, 0:7] = 1
        z[:, 4 + j, j, 7] = 1
    c[:, C_Z:C_Z + 128] = z.reshape(128, 128)
    c[:, C_ONE:C_ONE + 128] = 1
    return c


def kernel(**inputs):
    import concourse.bacc as _bacc
    from concourse.bass_utils import run_bass_kernel_spmd as _run

    I = {k: np.asarray(v) for k, v in inputs.items()}
    a = {n: I[n] for n in _PLAIN}
    a["x"] = I["x"]
    a["fside"] = I["fside_BxSx2_0"]
    a["ctxT"] = I["ctx_1024"].reshape(2048, 128).T
    a["maskT"] = I["mask_BxS2_bf1"].T.view(np.uint8) if I["mask_BxS2_bf1"].dtype == np.bool_ else I["mask_BxS2_bf1"].T
    a["edT"] = I["L0_ffn_e_down"].T
    a["keysT"] = I["L0_ffn_keys"].transpose(2, 3, 0, 1).reshape(128, 4, 128)
    bup = np.concatenate([I["L1_ffn_bup"], I["L1_ffn_bsu"][None]], 0)
    bga = np.concatenate([I["L1_ffn_bgate"], I["L1_ffn_bsg"][None]], 0)
    a["bugT"] = np.stack([bup.reshape(16, 128).T, bga.reshape(16, 128).T], 1)
    a["bdown"] = np.concatenate([I["L1_ffn_bdown"], I["L1_ffn_bsd"][None]], 0)
    a["w1T"], a["w3T"], a["w2T"] = I["L2_ffn_w1"].T, I["L2_ffn_w3"].T, I["L2_ffn_w2"].T
    kv = np.concatenate([I["L2_xattn_Wk"], I["L2_xattn_Wv"]], 1).reshape(128, 16, 2, 16)
    a["L2_xattn_Wk"], a["L2_xattn_Wv"] = kv[:, :, 0].reshape(128, 256), kv[:, :, 1].reshape(128, 256)
    bkv = np.concatenate([I["L2_xattn_bk"], I["L2_xattn_bv"]]).reshape(16, 2, 16)
    a["L2_xattn_bk"], a["L2_xattn_bv"] = bkv[:, 0].reshape(256), bkv[:, 1].reshape(256)
    a["gqk"] = np.stack([I["L3_xattn_gq"], I["L3_xattn_gk"]], 1)
    a["consts"] = _constants()
    r = np.arange(128)
    a["mrow"] = np.stack([r < 112, r >= 112]).astype(np.float32)

    nc = _bacc.Bacc("TRN2", target_bir_lowering=False, num_devices=1)
    arrays, aps = {}, {}
    for name, v in a.items():
        v = np.ascontiguousarray(v)
        arrays[f"in_{name}"] = v
        aps[name] = nc.dram_tensor(f"in_{name}", v.shape, mybir.dt.from_np(v.dtype), kind="ExternalInput").ap()
    o = nc.dram_tensor("out_0", (16, 128, 256), F32, kind="ExternalOutput").ap()
    program(nc, aps, o)
    return _run(nc, [arrays], core_ids=[0]).results[0]["out_0"]
```

```python
import math
from contextlib import ExitStack

import numpy as np
import concourse.bass as bass
from concourse import mybir

SUBS = (0, 1, 2, 3, 4, 5, 6, 7)

F32 = mybir.dt.float32
BF16 = mybir.dt.bfloat16
F16 = mybir.dt.float16
U32 = mybir.dt.uint32
U8 = mybir.dt.uint8
ALU = mybir.AluOpType
ACT = mybir.ActivationFunctionType
AX = mybir.AxisListType

NB = 16
NS = 4
AR = 4684
C_ID, C_I128, C_I64, C_I8, C_MM, C_MD, C_PC, C_ONE, C_N = 0, 128, 256, 320, 328, 329, 330, 332, 460


class Queue:

    def __init__(self, sem, cost, clock):
        self.sem, self.n, self.ops, self.seen = sem, 0, [], {}
        self.cost, self.at, self.clock = cost, 0.0, clock

    def __call__(self, waits, f, *args, inc=1, sem=None, step=1, **kw):
        need = []
        start = self.at
        for sem_, n in flat(waits):
            start = max(start, self.clock.get((sem_.name, n), 0.0) + 60.0)
            if self.seen.get(sem_.name, 0) < n:
                self.seen[sem_.name] = n
                need = [(s, k) for s, k in need if s.name != sem_.name] + [(sem_, n)]
        if sem is None:
            self.at = start + self.cost(args, kw)
            self.ops.append((need, f, args, kw, self.sem if inc else None, 1))
            if inc:
                self.n += 1
                self.clock[(self.sem.name, self.n)] = self.at
                self.clock["last"] = max(self.clock.get("last", 0.0), self.at)
            return (self.sem, self.n)
        self.at = start + self.cost(args, kw)
        self.ops.append((need, f, args, kw, sem, step))
        return None

    def run(self, eng):
        for need, f, args, kw, sem, step in self.ops:
            for s, n in need:
                eng.wait_ge(s, n)
            ins = f(*args, **kw)
            if sem is not None:
                ins.then_inc(sem, step)


def flat(waits):
    if waits is None:
        return []
    if isinstance(waits, tuple) and len(waits) == 2 and isinstance(waits[1], int):
        return [waits]
    return [t for w in waits for t in flat(w)]


class Load:

    def __init__(self, q, dma, sem):
        self.q, self.dma, self.sem, self.n = q, dma, sem, 0

    def __call__(self, waits, dst, src):
        self.q(waits, self.dma, dst, src, sem=self.sem, step=16)
        self.n += 16
        self.q.at += 4.0 * int(np.prod(dst.shape)) / 180.0
        self.q.clock[(self.sem.name, self.n)] = self.q.at + 2500.0
        return (self.sem, self.n)


class Slot:
    pass


def width(ap):
    return int(np.prod(ap.shape[1:]))


def pe_cost(args, kw):
    out, w = args[0], args[1]
    n = max(width(out), 32)
    if len(args) > 2 and "start" not in kw:
        return n * (4 if w.dtype == F32 else 1) / 2.4
    c = n * (4 if w.dtype == F32 else 1) / 2.4
    c = c * 2 if w.shape[0] <= 64 else c
    return max(c, 426.0) if w.dtype == F32 else c


def dve_cost(args, kw):
    big = max((width(a) for a in args if isinstance(a, bass.AP)), default=1)
    return (big + 62) / 0.96


def act_cost(args, kw):
    return 190.0 + width(args[0]) / 1.2


def pool_cost(args, kw):
    return 120.0 + 1.9 * width(args[0])


def no_cost(args, kw):
    return 50.0


def bc(ap, axis, shape):
    return ap.unsqueeze(axis).to_broadcast(shape)


def program(nc, A, out):
    ctx = ExitStack()
    with ctx:
        def sb(name, shape, dt=F32):
            return ctx.enter_context(nc.sbuf_tensor(name, shape, dt))

        def sem(name):
            return ctx.enter_context(nc.semaphore(name))

        x = sb("x", [128, NB, 256])
        ctxT = sb("ctxT", [128, NB * 128])
        area = [sb("areaA", [128, 12288]), sb("areaB", [128, 12288])]
        cst = sb("cst", [128, C_N])
        idh = sb("idh", [128, 128], F16)
        i128h = sb("i128h", [128, 128], F16)
        i64h = sb("i64h", [128, 64], F16)
        neghalf = sb("neghalf", [128, 32])
        cs = sb("cs", [128, 2, NB * 4])
        mbias = sb("mbias", [128, NB])
        mkey = sb("mkey", [128, NB])

        slots = []
        for i in range(NS):
            s = Slot()
            s.i = i
            s.xn = sb(f"xn{i}", [128, 256])
            s.xT = sb(f"xT{i}", [128, 2, 128])
            s.ar = sb(f"ar{i}", [128, AR])
            s.sm = sb(f"sm{i}", [128, 128])
            s.bk = [ctx.enter_context(nc.psum_tensor(f"pb{i}_{j}", [128, 512], F32)) for j in range(2)]
            s.bf = [None] * 2
            s.done = None
            slots.append(s)

        clock = {}
        V = Queue(sem("s_dve"), dve_cost, clock)
        S = Queue(sem("s_act"), act_cost, clock)
        T = Queue(sem("s_pe"), pe_cost, clock)
        P = Queue(sem("s_pool"), pool_cost, clock)
        D = Queue(sem("s_sp"), no_cost, clock)
        ve, se, te, pe_ = nc.vector, nc.scalar, nc.tensor, nc.gpsimd

        ld_c = Load(D, nc.sync.dma_start, sem("d_c"))
        ld_x = Load(D, nc.sync.dma_start, sem("d_x"))
        ld_w = [Load(D, nc.sync.dma_start, sem(f"d_w{k}")) for k in range(8)]
        st_o = Load(D, nc.sync.dma_start, sem("d_o"))

        ident = cst[:, C_ID:C_ID + 128]
        ones_row = cst[0:1, C_ONE:C_ONE + 128]
        ones_sq = cst[:, C_ONE:C_ONE + 128]
        iota8 = cst[:, C_I8:C_I8 + 8]

        ld_c(None, cst[:, :], A["consts"])
        t_c = ld_c(None, cs[:, 0, :].rearrange("p (b k) -> p b k", k=4)[:, :, 0:2],
                   A["fside"].rearrange("b t p -> t b p"))
        t_x0 = ld_x(None, x[:, :, :], A["x"].rearrange("b t d -> t b d"))
        t_ctx = ld_x(None, ctxT[:, :], A["ctxT"])
        m8 = slots[1].ar[:, 0:4].bitcast(U8)
        t_m8 = ld_x(None, m8, A["maskT"])

        t_k = V(t_c, ve.tensor_copy, idh[:, :], ident)
        t_k = V(t_c, ve.tensor_copy, i128h[:, :], cst[:, C_I128:C_I128 + 128])
        t_k = V(t_c, ve.tensor_copy, i64h[:, :], cst[:, C_I64:C_I64 + 64])
        t_k = V(None, ve.memset, neghalf[:, :], -0.5)
        t_m = V(t_m8, ve.tensor_copy, mkey[:, :], m8)
        t_k = V(t_m, ve.tensor_scalar, mbias[:, :], mkey[:, :], -1.0, 1e30, ALU.add, ALU.mult)

        ang = slots[0].ar[:, 0:64].rearrange("p (b q j) -> p b q j", q=2, j=2)
        pos = cs[:, 0, :].rearrange("p (b k) -> p b k", k=4)[:, :, 0:2]
        t = V(t_c, ve.tensor_copy, ang[:, :, :, 0], pos)
        t = V(t_c, ve.tensor_scalar, ang[:, :, :, 1], pos, float(np.float32(0.01)), None, ALU.mult)
        af = slots[0].ar[:, 0:64]
        MAGIC = 12582912.0
        for which, off in ((1, 0.0), (0, math.pi / 2)):
            a0 = slots[0].ar[:, 64:128]
            n0 = slots[0].ar[:, 128:192]
            t = V(t, ve.tensor_scalar, a0, af, off, None, ALU.add)
            t = V(t, ve.tensor_scalar, n0, a0, 1.0 / (2 * math.pi), MAGIC, ALU.mult, ALU.add)
            t = V(t, ve.tensor_scalar, n0, n0, MAGIC, None, ALU.subtract)
            t = V(t, ve.scalar_tensor_tensor, a0, n0, -6.28125, a0, ALU.mult, ALU.add)
            t = V(t, ve.scalar_tensor_tensor, a0, n0, -(2 * math.pi - 6.28125), a0, ALU.mult, ALU.add)
            t = V(t, ve.tensor_scalar, a0, a0, 3.1415925, -3.1415925, ALU.min, ALU.max)
            t = S(t, se.activation, cs[:, which, :], a0, ACT.Sin)
        t_cs = t
        slots[0].done = [t_cs, t_k]
        for s in slots[1:]:
            s.done = [t_k, t_m]
        t_const = [t_k, t_c]

        def put(k, off, dims, src, waits, rows=128):
            n = int(np.prod(dims))
            v = area[k % 2][0:rows, off:off + n]
            if len(dims) == 2:
                v = v.rearrange("p (a b) -> p a b", a=dims[0])
            if len(dims) == 3:
                v = v.rearrange("p (a b c) -> p a b c", a=dims[0], b=dims[1])
            if src is not None:
                ld_w[k](waits, v, src)
            return v

        W = [None] * 8

        def kp(ap, k):
            return ap.rearrange("(k p) n -> p k n", k=k)

        def load_weights(k, w):
            d = {}
            if k == 0:
                d["wq"] = put(k, 0, [2, 256], kp(A["L0_xattn_Wq"], 2), w)
                d["wkv"] = put(k, 512, [512], A["L0_xattn_Wkv"], w)
                d["wo"] = put(k, 1024, [2, 256], kp(A["L0_xattn_Wout"], 2), w)
                d["bo"] = put(k, 1536, [256], A["L0_xattn_bout"].partition_broadcast(128), w)
            if k == 1:
                d["ed"] = put(k, 0, [2, 2048], kp(A["edT"], 2), w)
                d["eu"] = put(k, 4096, [16, 256], kp(A["L0_ffn_e_up"], 16), w)
                d["wq"] = put(k, 8192, [2, 512], kp(A["L0_ffn_Wq"], 2), w)
                d["keys"] = put(k, 9216, [4, 128], A["keysT"], w)
            if k == 2:
                d["wq"] = put(k, 0, [2, 2048], kp(A["L1_xattn_Wq"], 2), w)
                d["wk"] = put(k, 4096, [1024], A["L1_xattn_Wk"], w)
                d["wv"] = put(k, 5120, [1024], A["L1_xattn_Wv"], w)
                d["wo"] = put(k, 6144, [16, 256], kp(A["L1_xattn_Wo"], 16), w)
            if k == 3:
                for j, (n, m) in enumerate((("Wup", "Wsu"), ("Wgate", "Wsg"), ("Wdown", "Wsd"))):
                    v = area[1][:, 4096 * j:4096 * (j + 1)].rearrange("p (e k n) -> p e k n", e=8, k=2)
                    d[n] = v
                    for e in range(7):
                        ld_w[k](w, v[:, e], kp(A["L1_ffn_" + n][e], 2))
                    ld_w[k](w, v[:, 7], kp(A["L1_ffn_" + m], 2))
            if k == 4:
                d["wq"] = put(k, 0, [2, 256], kp(A["L2_xattn_Wq"], 2), w)
                d["wk"] = put(k, 512, [256], A["L2_xattn_Wk"], w)
                d["wv"] = put(k, 768, [256], A["L2_xattn_Wv"], w)
                d["wd"] = put(k, 1024, [512], A["L2_xattn_Wkv_dca"], w)
                d["wo"] = put(k, 1536, [2, 256], kp(A["L2_xattn_Wo"], 2), w)
                d["bo"] = put(k, 2048, [256], A["L2_xattn_bo"].partition_broadcast(128), w)
                d["bqk"] = area[0][:, 2304:2816]
                d["bv"] = area[0][:, 2816:3072]
                ld_w[k](w, area[0][:, 2304:2560], A["L2_xattn_bq"].partition_broadcast(128))
                ld_w[k](w, area[0][0:112, 2560:2816], A["L2_xattn_bk"].partition_broadcast(112))
                ld_w[k](w, area[0][0:112, 2816:3072], A["L2_xattn_bv"].partition_broadcast(112))
                ld_w[k](w, area[0][112:128, 2560:3072], A["L2_xattn_bkv_dca"].partition_broadcast(16))
                ww = area[0][:, 3584:3648].rearrange("p (a b c) -> p a b c", a=2, b=2)
                d["nw"] = ww
                for c, sfx in ((0, "w"), (1, "b")):
                    ld_w[k](w, ww[:, c, 0], A["L2_xattn_qn_" + sfx].partition_broadcast(128))
                    ld_w[k](w, ww[0:112, c, 1], A["L2_xattn_kn_" + sfx].partition_broadcast(112))
                    ld_w[k](w, ww[112:128, c, 1], A["L2_xattn_kn_dca_" + sfx].partition_broadcast(16))
            if k == 5:
                d["w1"] = put(k, 0, [2, 682], kp(A["w1T"], 2), w)
                d["w3"] = put(k, 1364, [2, 682], kp(A["w3T"], 2), w)
                v = put(k, 2728, [6, 256], None, w)
                d["w2"] = v
                ld_w[k](w, v[:, 0:5], kp(A["w2T"][0:640], 5))
                ld_w[k](w, v[0:42, 5], A["w2T"][640:682])
                d["tmp"] = area[1][:, 4264:8528]
            if k == 6:
                d["wq"] = put(k, 0, [2, 2048], kp(A["L3_xattn_Wq"], 2), w)
                d["wk"] = put(k, 4096, [2048], A["L3_xattn_Wk"], w)
                d["wv"] = put(k, 6144, [2048], A["L3_xattn_Wv"], w)
                d["wo"] = put(k, 8192, [16, 256], kp(A["L3_xattn_Wo"], 16), w)
            if k == 7:
                d["raw"] = put(k, 0, [24, 256], None, w)
                ld_w[k](w, d["raw"][:, 0:8], kp(A["L3_ffn_gate_w"], 8))
                ld_w[k](w, d["raw"][:, 8:16], kp(A["L3_ffn_up_w"], 8))
                ld_w[k](w, d["raw"][:, 16:24].rearrange("p (k c) n -> p k (c n)", k=2), kp(A["L3_ffn_down_w"], 2))
                d["g"] = put(k, 6144, [2, 1024], None, w)
                d["u"] = put(k, 8192, [2, 1024], None, w)
                d["d"] = put(k, 10240, [8, 256], None, w)
            d["t"] = (ld_w[k].sem, ld_w[k].n)
            W[k] = d

        wr = sb("wr", [128, 2, 7])
        rb = sb("rb", [1, 16])
        bu = sb("bu", [128, 2, 16])
        bdn = sb("bdn", [8, 256])
        gqk = sb("gqk", [128, 2])
        gp = sb("gp", [128, 1])
        ld_s = Load(D, nc.sync.dma_start, sem("d_s"))

        def load_small():
            ld_s(None, wr[:, :, :], kp(A["L1_ffn_Wr"], 2))
            ld_s(None, rb[0:1, 0:7], A["L1_ffn_br"].unsqueeze(0))
            ld_s(None, rb[0:1, 8:15], A["L1_ffn_gate_bias"].unsqueeze(0))
            ld_s(None, bu[:, :, :], A["bugT"])
            ld_s(None, bdn[:, :], A["bdown"])
            t = ld_s(None, gqk[:, :], A["gqk"])
            return t

        def ln(s, b, eps=1e-5):
            w = [s.done, s.x_t[b]]
            st, mv, rs = s.sm[:, 0:6], s.sm[:, 6:8], s.sm[:, 8:9]
            t = V(w, ve.bn_stats, st, x[:, b, :])
            t = V(t, ve.bn_aggr, mv, st)
            t = V(t, ve.tensor_scalar, rs, mv[:, 1:2], eps, None, ALU.add)
            t = P([t, t_const], pe_.tensor_tensor, rs, rs, neghalf[:, 0:1], ALU.pow)
            return V([t, w], ve.tensor_scalar, s.xn[:, :], x[:, b, :], mv[:, 0:1], rs, ALU.subtract, ALU.mult)

        def xpose(s, t_in, j=0):
            for k in range(2):
                t = T([t_in, s.bf[j], t_const], te.transpose, s.bk[j][:, k * 128:(k + 1) * 128],
                      s.xn[:, k * 128:(k + 1) * 128], ident, inc=(k == 1))
            t = S([t, s.done], se.copy, s.xT[:, :, :], s.bk[j][:, 0:256].rearrange("p (k n) -> p k n", k=2))
            s.bf[j] = t
            return t

        def add_x(s, b, src, waits):
            return V(waits, ve.tensor_tensor, x[:, b, :], x[:, b, :], src, ALU.add)

        def small_init(s, L):
            H, SW, hd = (32, 32, 8) if L == 0 else (16, 64, 16)
            d = Slot()
            d.qp = s.ar[:, 0:1024].bitcast(F16).rearrange("p (a h e) -> p a h e", a=2, h=H)
            t = V(s.done, ve.memset, s.ar[:, 0:3072], 0.0)
            if L == 0:
                t = V(t, ve.memset, d.qp[:, 1, :, 24:25], 1.0)
                vt = s.ar[:, 4096:4096 + 288].bitcast(F16).rearrange("p (a h e) -> p a h e", a=2, e=9)
                t = V(s.done, ve.memset, s.ar[:, 4096:4096 + 288], 0.0)
                t = V(t, ve.memset, vt[:, 0, :, 8:9], 1.0)
            else:
                for c in range(2):
                    t = V([t, t_const], ve.tensor_scalar, d.qp[:, 1, :, 48 + c:49 + c], ones_sq[:, 0:16].unsqueeze(2),
                          cst[:, C_MM + c:C_MM + c + 1], None, ALU.mult)
                t = V([t, s.done], ve.memset, s.ar[:, 4096:4640], 0.0)
                vt = s.ar[:, 4096:4640].bitcast(F16).rearrange("p (a h e) -> p a h e", a=2, e=34)
                for c in range(2):
                    t = V(t, ve.tensor_scalar, vt[:, 0, :, 17 * c + 16:17 * c + 17], ones_sq[:, 0:16].unsqueeze(2),
                          cst[:, C_MM + c:C_MM + c + 1], None, ALU.mult)
                t = V(t, ve.memset, s.ar[:, 2048:2304], 0.0)
            s.done = t
            s.PQ = area[0][:, 4096 + 1024 * s.i:5120 + 1024 * s.i].bitcast(F16).rearrange("p (x a n) -> p x a n", x=2, a=2)
            return
            yield

        def small_attn(s, b, L):
            w = W[0 if L == 0 else 4]
            H, SW, hd, R, E = (32, 32, 8, 4, 9) if L == 0 else (16, 64, 16, 2, 34)
            scale = 1.0 / math.sqrt(hd)
            bk = s.bk
            cx = ctxT[:, b * 128:(b + 1) * 128]
            qp = s.ar[:, 0:1024].bitcast(F16).rearrange("p (a h e) -> p a h e", a=2, h=H)
            qpf = s.ar[:, 0:1024].bitcast(F16).rearrange("p (a n) -> p a n", a=2)
            bd = s.ar[:, 1024:1024 + 512 * R].bitcast(F16).rearrange("p (t i n) -> p t i n", i=R, n=128)
            cm = s.ar[:, 2048:2176]
            cd = s.ar[:, 2176:2304]
            if L == 0:
                tmp = s.ar[:, 1024:2048]
                y = s.ar[:, 3072:3584]
            else:
                tmp = s.ar[:, 2304:2816]
                y = s.ar[:, 3072:3584]
            qT = s.ar[:, 3072:3584].bitcast(F16).rearrange("p (t n) -> p t n", n=128)
            kT = s.ar[:, 3584:4096].bitcast(F16).rearrange("p (t n) -> p t n", n=128)
            vt = s.ar[:, 4096:4096 + H * E].bitcast(F16).rearrange("p (a h e) -> p a h e", a=2, e=E)
            t_ln = ln(s, b)
            yield
            t_xT = xpose(s, t_ln)
            t_in = [w["t"], t_xT, t_const, t_ctx]
            t_xb = P([t_ln, w["t"]], pe_.tensor_tensor, x[:, b, :], x[:, b, :], w["bo"], ALU.add)
            yield
            q0 = bk[0][:, 0:256]
            T([t_in, s.bf[0]], te.matmul, q0, s.xT[:, 0], w["wq"][:, 0], start=True, stop=False, inc=0)
            if L == 0:
                T(None, te.matmul, q0, s.xT[:, 1], w["wq"][:, 1], start=False, stop=True, inc=0)
                T(None, te.matmul, bk[0][:, 256:512], cx, w["wkv"][:, 0:256], start=True, stop=True, inc=0)
                t_p = T(s.bf[1], te.matmul, bk[1][:, 0:256], cx, w["wkv"][:, 256:512], start=True, stop=True)
                yield
                src = bk[0][:, :].rearrange("p (h f two) -> p h f two", f=4, two=2)
                co = bc(cs[:, 0, 4 * b:4 * b + 4], 1, [128, 64, 4])
                si = bc(cs[:, 1, 4 * b:4 * b + 4], 1, [128, 64, 4])
                tt = [sl.rearrange("p (h f) -> p h f", f=4) for sl in
                      (s.ar[:, 3584:3840], s.ar[:, 3840:4096], s.xn[:, :], s.ar[:, 4384:4640])]
                V([t_p, t_cs, s.done], ve.tensor_tensor, tt[0], src[:, :, :, 0], co, ALU.mult)
                V(None, ve.tensor_tensor, tt[1], src[:, :, :, 1], si, ALU.mult)
                V(None, ve.tensor_tensor, tt[2], src[:, :, :, 0], si, ALU.mult)
                t1 = V(None, ve.tensor_tensor, tt[3], src[:, :, :, 1], co, ALU.mult)
                s.bf[0] = t1
                y8 = y.rearrange("p (h f two) -> p h f two", f=4, two=2)
                V(t1, ve.tensor_tensor, y8[:, :, :, 0], tt[0], tt[1], ALU.subtract)
                t_y = V(None, ve.tensor_tensor, y8[:, :, :, 1], tt[2], tt[3], ALU.add)
                v0 = bk[1][:, 0:256].rearrange("p (h e) -> p h e", e=8)
                t_v = S([t_p, s.done], se.copy, vt[:, 0, :, 0:8], v0)
                t_v = V(t_v, ve.tensor_tensor, vt[:, 1, :, 0:8], v0, vt[:, 0, :, 0:8], ALU.subtract)
                s.bf[1] = t_v
            else:
                P([t_ctx, s.done], pe_.tensor_copy, cm[:, 0:112], cx[:, 0:112])
                t_cm = P(None, pe_.tensor_copy, cd[:, 112:128], cx[:, 112:128])
                T(None, te.matmul, q0, s.xT[:, 1], w["wq"][:, 1], start=False, stop=True, inc=0)
                for dst, wm, wd, wt in ((bk[0][:, 256:512], w["wk"], w["wd"][:, 0:256], None),
                                        (bk[1][:, 0:256], w["wv"], w["wd"][:, 256:512], s.bf[1])):
                    T([t_cm, wt], te.matmul, dst, cm, wm, start=True, stop=False, inc=0)
                    t_p = T(None, te.matmul, dst, cd, wd, start=False, stop=True)
                yield
                src = bk[0][:, :].rearrange("p (h e) -> p h e", e=16)
                y3 = y.rearrange("p (h e) -> p h e", e=16)
                sq = tmp.rearrange("p (h e) -> p h e", e=16)
                mu = s.sm[:, 64:96]
                va = s.sm[:, 96:128]
                t1 = s.bf[0] = V([t_p, s.done], ve.tensor_tensor, y, bk[0][:, :], w["bqk"], ALU.add)
                t_vb = s.bf[1] = V(t_p, ve.tensor_tensor, s.xn[:, :], bk[1][:, 0:256], w["bv"], ALU.add)
                t1 = V(t1, ve.tensor_reduce, mu, y3, AX.X, ALU.add)
                t1 = V(t1, ve.tensor_scalar, mu, mu, 1.0 / 16, None, ALU.mult)
                t1 = V(t1, ve.tensor_tensor, y3, y3, bc(mu, 2, [128, 32, 16]), ALU.subtract)
                t2 = S(t1, se.activation, sq, y3, ACT.Square)
                vs = s.xn[:, :].rearrange("p (h e) -> p h e", e=16)
                for c in range(2):
                    m = cst[:, C_MM + c:C_MM + c + 1]
                    vh = vt[:, 0, :, 17 * c:17 * c + 16]
                    t_v = V([t_vb, s.done], ve.tensor_scalar, vh, vs, m, None, ALU.mult)
                    t_v = V(t_v, ve.scalar_tensor_tensor, vt[:, 1, :, 17 * c:17 * c + 16], vs, m, vh, ALU.mult, ALU.subtract)
                yield
                t2 = V(t2, ve.tensor_reduce, va, sq, AX.X, ALU.add)
                t2 = V(t2, ve.tensor_scalar, va, va, 1.0 / 16, 1e-6, ALU.mult, ALU.add)
                t2 = P(t2, pe_.tensor_tensor, va, va, neghalf[:, 0:32], ALU.pow)
                yield
                t2 = V(t2, ve.tensor_tensor, y3, y3, bc(va, 2, [128, 32, 16]), ALU.mult)
                y4 = y.rearrange("p (a h e) -> p a h e", a=2, h=16)
                for a in range(2):
                    t3 = V([t2, w["t"]], ve.tensor_tensor, y4[:, a], y4[:, a],
                           bc(w["nw"][:, 0, a], 1, [128, 16, 16]), ALU.mult)
                for a in range(2):
                    t_y = V(t3, ve.tensor_tensor, y4[:, a], y4[:, a],
                            bc(w["nw"][:, 1, a], 1, [128, 16, 16]), ALU.add)
            y4 = y.rearrange("p (a h e) -> p a h e", a=2, h=H)
            qpa = s.ar[:, 0:1024].bitcast(F16).rearrange("p (ah e) -> p ah e", e=SW)
            t_h = S([t_y, s.done], se.copy, qpa[:, :, 0:hd], y.rearrange("p (ah e) -> p ah e", e=hd))
            V([t_h, s.done], ve.tensor_tensor, qp[:, 0, :, hd:2 * hd], y4[:, 0], qp[:, 0, :, 0:hd], ALU.subtract)
            t_q1 = V(None, ve.tensor_tensor, qp[:, 1, :, 2 * hd:3 * hd], y4[:, 1], qp[:, 1, :, 0:hd], ALU.subtract)
            nmx = 1 if L == 0 else 2
            V([t_h, s.done], ve.tensor_copy, qp[:, 0, :, 2 * hd:3 * hd], qp[:, 0, :, 0:hd])
            V(None, ve.tensor_copy, qp[:, 1, :, hd:2 * hd], qp[:, 1, :, 0:hd])
            t_q2 = V(None, ve.memset, qp[:, 0, :, 3 * hd:3 * hd + nmx], 0.0)
            yield
            bh = [bk[j][:, :].bitcast(F16) for j in range(2)]
            for j in range(2):
                for t_ in range(8):
                    t = T([t_q1, t_q2, s.bf[j]], te.transpose, bh[j][:, t_ * 128:(t_ + 1) * 128],
                          qpf[:, j, t_ * 128:(t_ + 1) * 128], idh[:, :], inc=(t_ == 7))
                if j == 0:
                    t_qe = s.bf[0] = S([t, t_q1], se.copy, qT, bh[0].rearrange("p (t n) -> p t n", n=128))
                else:
                    t_ke = s.bf[1] = V([t, t_q1], ve.tensor_copy, kT, bh[1].rearrange("p (t n) -> p t n", n=128))
            yield
            for i in range(R):
                r = slice(SW * i, SW * i + SW)
                t_bd = V([t_ke, t_y], ve.tensor_copy, bd[r, :, i, :], kT[r, :, :])
            yield
            ng = H // 4
            per = 4 // R
            for g in range(ng):
                j = g % 2
                for c in range(per):
                    t_ = g * per + c
                    t = T([t_qe, t_bd, s.bf[j]], te.matmul, bk[j][:, c * R * 128:(c + 1) * R * 128], qT[:, t_, :],
                          bd[:, t_], start=True, stop=True, inc=(c == per - 1))
                bv = bk[j][:, :].rearrange("p (h n) -> p h n", h=4)
                o = qp[:, 0, 4 * g:4 * g + 4, 3 * hd:3 * hd + nmx]
                if L == 0:
                    t_m = V([t, t_q2], ve.tensor_reduce, o, bv, AX.X, ALU.max, negate=True)
                else:
                    V([t, t_q2], ve.tensor_reduce, o[:, :, 0:1], bv[:, :, 0:112], AX.X, ALU.max, negate=True)
                    t_m = V(None, ve.tensor_reduce, o[:, :, 1:2], bv[:, :, 112:128], AX.X, ALU.max, negate=True)
                s.bf[j] = t_m
                if g % 2:
                    yield
            t_s = t
            for t_ in range(8):
                t = T([t_m, s.bf[0]], te.transpose, bh[0][:, t_ * 128:(t_ + 1) * 128],
                      qpf[:, 0, t_ * 128:(t_ + 1) * 128], idh[:, :], inc=(t_ == 7))
            t_qe = s.bf[0] = S([t, t_s], se.copy, qT, bh[0].rearrange("p (t n) -> p t n", n=128))
            yield
            for i in range(R):
                r = slice(SW * i, SW * i + SW)
                t_bd = V([t_qe, t_s], ve.tensor_copy, bd[r, :, i, :], qT[r, :, :])
            yield
            Pm = s.ar[:, 3072:3584]
            Pq = s.PQ
            O = s.xn[:, :].rearrange("p (h e) -> p h e", h=H)
            rec = s.sm[:, 16:48]
            t_o = None
            t_l = [None, None]
            t_pp = None
            half = 8 if L == 0 else 2
            for g in range(ng):
                xx = g % 2
                for c in range(per):
                    t_ = g * per + c
                    t = T([t_bd, s.bf[0]], te.matmul, bk[0][:, c * R * 128:(c + 1) * R * 128], kT[:, t_, :],
                          bd[:, t_], start=True, stop=True, inc=(c == per - 1))
                t = S([t, t_pp, t_bd], se.activation, Pm, bk[0][:, :], ACT.Exp, scale=scale)
                s.bf[0] = t
                t_hi = V([t, t_l[xx], s.done], ve.tensor_copy, Pq[:, xx, 0], Pm)
                t_pp = P([t_hi, t_l[xx]], pe_.tensor_tensor, Pq[:, xx, 1], Pm, Pq[:, xx, 0], ALU.subtract)
                yield
                for c in range(4):
                    h = 4 * g + c
                    o = bk[1][:, (h % (4 * half)) * E:(h % (4 * half) + 1) * E]
                    ph = Pq[:, xx, 0, c * 128:(c + 1) * 128]
                    pl = Pq[:, xx, 1, c * 128:(c + 1) * 128]
                    T([t_hi, t_v, s.bf[1]], te.matmul, o, ph, vt[:, 0, h, :], start=True, stop=False, inc=0)
                    T(None, te.matmul, o, ph, vt[:, 1, h, :], start=False, stop=False, inc=0)
                    t = T(t_pp, te.matmul, o, pl, vt[:, 0, h, :], start=False, stop=True, inc=(c == 3))
                t_l[xx] = t
                if g % half == half - 1:
                    n = 4 * half
                    ov = bk[1][:, 0:n * E].rearrange("p (h e) -> p h e", e=E)
                    hs = slice((g // half) * n, (g // half + 1) * n)
                    if L == 0:
                        t1 = V([t, t_q1], ve.reciprocal, rec[:, 0:32].unsqueeze(2), ov[:, :, 8:9])
                        t_o = V(t1, ve.tensor_tensor, O, ov[:, :, 0:8], bc(rec[:, 0:32], 2, [128, 32, 8]), ALU.mult)
                    else:
                        tA = tmp[:, 0:128].rearrange("p (h e) -> p h e", e=16)
                        V([t, t_o], ve.reciprocal, rec[:, 0:8].unsqueeze(2), ov[:, :, 16:17])
                        t1 = V(None, ve.reciprocal, rec[:, 8:16].unsqueeze(2), ov[:, :, 33:34])
                        V(t1, ve.tensor_tensor, O[:, hs, :], ov[:, :, 0:16], bc(rec[:, 0:8], 2, [128, 8, 16]), ALU.mult)
                        t2 = V(None, ve.tensor_tensor, tA, ov[:, :, 17:33], bc(rec[:, 8:16], 2, [128, 8, 16]), ALU.mult)
                        t_o = V(t2, ve.tensor_tensor, O[:, hs, :], O[:, hs, :], tA, ALU.add)
                    s.bf[1] = t_o
                    yield
            for k in range(2):
                t = T([t_o, s.bf[0]], te.transpose, bk[0][:, k * 128:(k + 1) * 128], s.xn[:, k * 128:(k + 1) * 128], ident,
                      inc=(k == 1))
            OT = s.xT
            t = S([t, t_o], se.copy, OT[:, :, :], bk[0][:, 0:256].rearrange("p (k n) -> p k n", k=2))
            s.bf[0] = t
            yield
            T([t, s.bf[1]], te.matmul, bk[1][:, 0:256], OT[:, 0], w["wo"][:, 0], start=True, stop=False, inc=0)
            t = T(None, te.matmul, bk[1][:, 0:256], OT[:, 1], w["wo"][:, 1], start=False, stop=True)
            t = add_x(s, b, bk[1][:, 0:256], [t, t_xb])
            s.bf[1] = t
            s.done = [t, t_pp]
            s.x_t[b] = t
            yield

        def big_attn(s, b, L):
            w = W[2 if L == 1 else 6]
            kv = 2 if L == 1 else 4
            scale = 1.0 / math.sqrt(128.0)
            bk = s.bk
            cx = ctxT[:, b * 128:(b + 1) * 128]
            t_ln = ln(s, b)
            yield
            t_xT = xpose(s, t_ln)
            yield
            qn = s.ar[:, 0:512]
            kn = s.ar[:, 512:1024]
            qT = s.ar[:, 1024:1536].rearrange("p (h n) -> p h n", n=128)
            kT = s.ar[:, 1536:2048].rearrange("p (h n) -> p h n", n=128)
            sq = s.ar[:, 1024:2048]
            Pm = s.ar[:, 0:512].rearrange("p (h n) -> p h n", n=128)
            O = s.ar[:, 512:1024].rearrange("p (h n) -> p h n", n=128)
            va = s.ar[:, 2048:2048 + kv * 129].rearrange("p (h e) -> p h e", e=129)
            OT = s.ar[:, 2568:4616].rearrange("p (h n) -> p h n", n=128)
            nmT = s.ar[0:4, 4616:4680].bitcast(F16)
            mrow = s.xn[0:1, 0:64].bitcast(F16)
            ms = s.sm[:, 16:24]
            nm = s.sm[:, 24:28]
            rec = s.sm[:, 28:32]
            zz = s.sm[:, 32:36]
            den = s.sm[:, 36:40]
            deps = [w["t"], t_xT, t_const, t_ctx]
            t_b = [s.done, t_xT]
            b0 = bk[0][:, :].rearrange("p (h n) -> p h n", h=4)
            b1 = bk[1][:, :].rearrange("p (h n) -> p h n", h=4)
            t_mr = t_one = None
            if L == 1:
                t = T([s.bf[1], t_const], te.transpose, bk[1][0:1, 0:128], mbias[:, b:b + 1], ident)
                t_mr = V([t, t_b, t_ln], ve.tensor_scalar, mrow, bk[1][0:1, 0:128], -30000.0, None, ALU.max)
                s.bf[1] = t_mr
                mk = mkey[:, b:b + 1]
                t_one = V(t_b, ve.tensor_scalar, va[:, :, 128:129], ones_sq[:, 0:kv].unsqueeze(2), mk, None, ALU.mult)
            else:
                t_one = V(t_b, ve.memset, va[:, :, 128:129], 1.0)
            for c in range(4):
                if L == 1:
                    for h in range(4):
                        for k in range(2):
                            t = T([deps, s.bf[0]], te.matmul, bk[0][:, h * 128:(h + 1) * 128],
                                  w["wq"][:, k, (4 * c + h) * 128:(4 * c + h + 1) * 128], s.xT[:, k, :],
                                  start=(k == 0), stop=(k == 1), inc=(k == 1 and h == 3))
                    for h in range(2):
                        T(s.bf[1], te.matmul, bk[1][:, h * 128:(h + 1) * 128],
                          w["wk"][:, (2 * c + h) * 128:(2 * c + h + 1) * 128], cx, start=True, stop=True, inc=0)
                    t1 = T(None, te.matmul, bk[1][:, 256:512], cx, w["wv"][:, c * 256:(c + 1) * 256], start=True, stop=True)
                    yield
                    t_q = s.bf[0] = S([t, t_b], se.copy, qT, b0)
                    t_k = V([t1, t_b], ve.tensor_copy, kT[:, 0:2, :], b1[:, 0:2])
                    t_v = s.bf[1] = V([t_one, t_b], ve.tensor_scalar, va[:, :, 0:128], b1[:, 2:4], mk, None, ALU.mult)
                else:
                    for k in range(2):
                        t = T([deps, s.bf[0]], te.matmul, bk[0][:, :], s.xT[:, k, :],
                              w["wq"][:, k, c * 512:(c + 1) * 512], start=(k == 0), stop=(k == 1), inc=(k == 1))
                    t1 = T(s.bf[1], te.matmul, bk[1][:, :], cx, w["wk"][:, c * 512:(c + 1) * 512], start=True, stop=True)
                    yield
                    ta = S([t, t_b], se.activation, sq[:, 0:512], bk[0][:, :], ACT.Square)
                    tb = S(t1, se.activation, sq[:, 512:1024], bk[1][:, :], ACT.Square)
                    t3 = V([ta, tb, t_b], ve.tensor_reduce, ms, sq.rearrange("p (h n) -> p h n", h=8), AX.X, ALU.add)
                    t3 = V(t3, ve.tensor_scalar, ms, ms, 1.0 / 128, 1e-5, ALU.mult, ALU.add)
                    t3 = P(t3, pe_.tensor_tensor, ms, ms, neghalf[:, 0:8], ALU.pow)
                    yield
                    t_qn = s.bf[0] = V([t3, t_b], ve.tensor_tensor, qn.rearrange("p (h n) -> p h n", h=4), b0,
                                       bc(ms[:, 0:4], 2, [128, 4, 128]), ALU.mult)
                    t_kn = s.bf[1] = V(None, ve.tensor_tensor, kn.rearrange("p (h n) -> p h n", h=4), b1,
                                       bc(ms[:, 4:8], 2, [128, 4, 128]), ALU.mult)
                    yield
                    for h in range(4):
                        t = T([t_qn, s.bf[0]], te.transpose, b0[:, h], qn[:, h * 128:(h + 1) * 128], ident, inc=(h == 3))
                    t_q = s.bf[0] = S([t, t_kn], se.copy, qT, b0)
                    for h in range(4):
                        t1 = T([t_kn, s.bf[1]], te.transpose, b1[:, h], kn[:, h * 128:(h + 1) * 128], ident, inc=(h == 3))
                    t_k = s.bf[1] = V([t1, t_gp, t_b], ve.tensor_scalar, kT, b1, gp[:, 0:1], None, ALU.mult)
                    yield
                    t2 = T(s.bf[1], te.matmul, bk[1][:, :], cx, w["wv"][:, c * 512:(c + 1) * 512], start=True, stop=True)
                    t_v = s.bf[1] = S([t2, t_one, t_b], se.copy, va[:, :, 0:128], b1)
                yield
                if L == 1:
                    T([t_mr, s.bf[0]], te.matmul, bk[0][:, :], idh[0:1, 0:1].to_broadcast([1, 128]), bc(mrow, 1, [1, 4, 128]), start=True,
                      stop=False, inc=0)
                for h in range(4):
                    kh = h // 2 if L == 1 else h
                    t = T([t_q, t_k, s.bf[0]], te.matmul, b0[:, h], qT[:, h], kT[:, kh],
                          start=(L == 3), stop=(L == 3 or h == 3), inc=(h == 3))
                t_m = s.bf[0] = V([t, t_b], ve.tensor_reduce, nm, b0, AX.X, ALU.max, negate=True)
                yield
                t = T([t_m, s.bf[1]], te.transpose, bk[1][0:4, 0:128], nm, ident)
                t_n = s.bf[1] = S([t, t_b], se.copy, nmT, bk[1][0:4, 0:128])
                yield
                for h in range(4):
                    kh = h // 2 if L == 1 else h
                    T([t_n, s.bf[0]], te.matmul, b0[:, h], kT[:, kh], qT[:, h], start=True, stop=False, inc=0)
                    t = T(None, te.matmul, b0[:, h], idh[0:4, h:h + 1].to_broadcast([4, 128]), nmT, start=False, stop=True,
                          inc=(h == 3))
                kw = {"scale": scale}
                if L == 1:
                    kw["bias"] = mbias[:, b:b + 1]
                t_x = s.bf[0] = S([t, t_b], se.activation, Pm, b0, ACT.Exp, **kw)
                yield
                for h in range(4):
                    kh = h // 2 if L == 1 else h
                    q = 1 - h // 2
                    t = T([t_x, t_v, s.bf[q]], te.matmul, bk[q][:, (h % 2) * 129:(h % 2 + 1) * 129], Pm[:, h], va[:, kh],
                          start=True, stop=True, inc=(h % 2 == 1))
                    if h % 2:
                        ov = bk[q][:, 0:258].rearrange("p (h e) -> p h e", e=129)
                        hs = slice(h - 1, h + 1)
                        if L == 1:
                            t1 = V([t, t_b], ve.tensor_scalar, zz[:, hs].unsqueeze(2), ov[:, :, 128:129], 0.0, None, ALU.is_equal)
                            t1 = V(t1, ve.tensor_tensor, den[:, hs].unsqueeze(2), zz[:, hs].unsqueeze(2), ov[:, :, 128:129], ALU.add)
                            t1 = V(t1, ve.reciprocal, rec[:, hs], den[:, hs])
                        else:
                            t1 = V([t, t_b], ve.reciprocal, rec[:, hs].unsqueeze(2), ov[:, :, 128:129])
                        t_o = s.bf[q] = V(t1, ve.tensor_tensor, O[:, hs], ov[:, :, 0:128], bc(rec[:, hs], 2, [128, 2, 128]), ALU.mult)
                yield
                for h in range(4):
                    t = T([t_o, s.bf[1]], te.transpose, b1[:, h], O[:, h], ident, inc=(h == 3))
                t_ot = s.bf[1] = S([t, t_b], se.copy, OT[:, 4 * c:4 * c + 4], b1)
                t_b = [t]
                yield
            for h in range(16):
                t = T([t_ot, s.bf[0]], te.matmul, bk[0][:, 0:256], OT[:, h], w["wo"][:, h],
                      start=(h == 0), stop=(h == 15), inc=(h == 15))
            t = s.bf[0] = add_x(s, b, bk[0][:, 0:256], t)
            s.done = t
            s.x_t[b] = t
            yield

        def peer(s, b):
            w = W[1]
            bk = s.bk
            t_ln = ln(s, b)
            yield
            t_xT = xpose(s, t_ln)
            yield
            G = s.ar[:, 0:2048].rearrange("p (e n) -> p e n", n=128)
            wk_ = s.ar[:, 2048:4608]
            B = wk_[:, 0:1024].bitcast(F16).rearrange("p (x g n) -> p x g n", x=2, n=128)
            Am = wk_[:, 1024:2048].bitcast(F16).rearrange("p (x a g n) -> p x a g n", x=2, a=2, n=64)
            oh = wk_[:, 2048:2560].bitcast(F16).rearrange("p (x g n) -> p x g n", x=2, n=64)
            sims = wk_[:, 0:1024].rearrange("p (a h n) -> p a h n", a=2, h=4)
            qT = wk_[:, 1024:1536].rearrange("p (h n) -> p h n", n=128)
            al = wk_[:, 1536:1792]
            e1 = wk_[:, 1792:2048]
            m0 = 2048
            s8 = wk_[:, m0:m0 + 64].rearrange("p (a h k) -> p a h k", a=2, h=4)
            i8 = wk_[:, m0 + 64:m0 + 128].bitcast(U32)
            i8f = wk_[:, m0 + 128:m0 + 192]
            f8 = wk_[:, m0 + 192:m0 + 224].rearrange("p (h k) -> p h k", h=4)
            pk = wk_[:, m0 + 224:m0 + 256].bitcast(U32)
            pk2 = wk_[:, m0 + 256:m0 + 320].bitcast(U32)
            pkf = wk_[:, m0 + 320:m0 + 384]
            isel = wk_[:, m0 + 384:m0 + 448]
            idx = wk_[:, m0 + 448:m0 + 480]
            iu = wk_[:, m0 + 480:m0 + 512].bitcast(U32)
            iv = wk_[:, 1024:1088].bitcast(U32)
            wh = wk_[:, 1088:1184]
            tr = wk_[:, 1184:1280]
            rest = wk_[:, 1280:1312]
            trh = s.ar[:, 4608:4672].bitcast(F16)
            t_b = [s.done, t_xT]
            for h in range(4):
                for k in range(2):
                    t = T([w["t"], t_xT, s.bf[0]], te.matmul, bk[0][:, h * 128:(h + 1) * 128], w["wq"][:, k, h * 128:(h + 1) * 128],
                          s.xT[:, k, :], start=(k == 0), stop=(k == 1), inc=(h == 3 and k == 1))
            t = s.bf[0] = S([t, t_b], se.copy, qT, bk[0][:, :].rearrange("p (h n) -> p h n", h=4))
            yield
            for a in range(2):
                for h in range(4):
                    tt = T([t, s.bf[a]], te.matmul, bk[a][:, h * 128:(h + 1) * 128],
                           qT[64 * a:64 * a + 64, h, :], w["keys"][64 * a:64 * a + 64, h, :],
                           start=True, stop=True, inc=(h == 3))
                ts_ = s.bf[a] = S([tt, t_b], se.copy, sims[:, a], bk[a][:, :].rearrange("p (h n) -> p h n", h=4))
            yield
            for a in range(2):
                for h in range(4):
                    t = V([ts_, t_b], ve.max, s8[:, a, h], sims[:, a, h])
            for a in range(2):
                for h in range(4):
                    t2 = V(t, ve.max_index, i8[:, (a * 4 + h) * 8:(a * 4 + h + 1) * 8], s8[:, a, h], sims[:, a, h])
            for j in range(4):
                for e in range(4):
                    for k in range(2):
                        tg = T([s.bf[j % 2]], te.matmul, bk[j % 2][:, e * 128:(e + 1) * 128],
                               w["ed"][:, k, (4 * j + e) * 128:(4 * j + e + 1) * 128], s.xT[:, k, :],
                               start=(k == 0), stop=(k == 1), inc=(k == 1 and e == 3))
                t_g = s.bf[j % 2] = S([tg, t_b], se.activation, G[:, 4 * j:4 * j + 4, :],
                                      bk[j % 2][:, :].rearrange("p (e n) -> p e n", e=4), ACT.Silu)
                if j % 2:
                    yield
            al4 = al.rearrange("p (h i j) -> p h i j", h=4, i=8)
            t = V(t, ve.tensor_tensor, al4, bc(s8[:, 0], 3, [128, 4, 8, 8]), bc(s8[:, 1], 2, [128, 4, 8, 8]), ALU.add)
            t2 = V(t2, ve.tensor_copy, i8f, i8)
            for h in range(4):
                t3 = V(t, ve.max, f8[:, h], al[:, h * 64:(h + 1) * 64])
            for h in range(4):
                t3_ = V(t3, ve.max_index, pk[:, h * 8:(h + 1) * 8], f8[:, h], al[:, h * 64:(h + 1) * 64])
            V(t3_, ve.tensor_scalar, pk2[:, 0:32], pk, 3, None, ALU.logical_shift_right)
            t4 = V(t3_, ve.tensor_scalar, pk2[:, 32:64], pk, 7, None, ALU.bitwise_and)
            t4 = V(t4, ve.tensor_copy, pkf, pk2)
            yield
            t5 = None
            for a in range(2):
                e2 = e1.rearrange("p (m j) -> p m j", j=8)
                t5 = V([t4, t5], ve.tensor_tensor, e2, bc(iota8, 1, [128, 32, 8]),
                       bc(pkf[:, 32 * a:32 * a + 32], 2, [128, 32, 8]), ALU.is_equal)
                e4 = e1.rearrange("p (h k j) -> p h k j", h=4, k=8)
                iv4 = i8f[:, 32 * a:32 * a + 32].rearrange("p (h j) -> p h j", h=4)
                t5 = V([t5, t2], ve.tensor_tensor, e4, e4, bc(iv4, 2, [128, 4, 8, 8]), ALU.mult)
                t5 = V(t5, ve.tensor_reduce, isel[:, 32 * a:32 * a + 32], e2, AX.X, ALU.add)
            t5 = V(t5, ve.scalar_tensor_tensor, idx, isel[:, 0:32], 128.0, isel[:, 32:64], ALU.mult, ALU.add)
            t5 = V(t5, ve.tensor_scalar, idx, idx, 2047.0, None, ALU.min)
            t5 = V(t5, ve.tensor_copy, iu, idx)
            V(t5, ve.tensor_scalar, iv[:, 0:32], iu, 7, None, ALU.logical_shift_right)
            t5 = V(None, ve.tensor_scalar, iv[:, 32:64], iu, 127, None, ALU.bitwise_and)
            t5 = V(t5, ve.tensor_copy, wh[:, 0:64], iv)
            t5 = V(t5, ve.tensor_scalar, wh[:, 64:96], f8.rearrange("p h k -> p (h k)"), 0.0, None, ALU.max)
            for q in range(3):
                t6 = V(t5, ve.transpose, tr[:, 32 * q:32 * q + 32], wh[:, 32 * q:32 * q + 32])
            V(t6, ve.tensor_scalar, trh[:, 0:32], tr[:, 0:32], cst[:, C_PC:C_PC + 1], None, ALU.add)
            t7 = V(None, ve.tensor_copy, trh[:, 32:96], tr[:, 32:96])
            t7 = V(t7, ve.tensor_tensor, rest, tr[:, 64:96], trh[:, 64:96], ALU.subtract)
            t7 = V(t7, ve.tensor_copy, trh[:, 96:128], rest)
            yield
            rd = [t7, t7]
            for j in range(4):
                xx = j % 2
                g8 = slice(8 * j, 8 * j + 8)
                t8 = V([t7, rd[xx]], ve.tensor_tensor, B[:, xx], bc(i128h[:, :], 1, [128, 8, 128]),
                       bc(trh[:, 32:64][:, g8], 2, [128, 8, 128]), ALU.is_equal)
                t9 = V([t7, rd[xx]], ve.tensor_tensor, oh[:, xx], bc(i64h[:, :], 1, [128, 8, 64]),
                       bc(trh[:, 0:32][:, g8], 2, [128, 8, 64]), ALU.is_equal)
                for a in range(2):
                    t10 = P(t9, pe_.tensor_tensor, Am[:, xx, a], oh[:, xx],
                            bc(trh[:, 64 + 32 * a:96 + 32 * a][:, g8], 2, [128, 8, 64]), ALU.mult)
                yield
                for g in range(8):
                    for a in range(2):
                        t = T([t8, t10, s.bf[xx]], te.matmul, bk[xx][:, g * 64:(g + 1) * 64], B[:, xx, g, :], Am[:, xx, a, g, :],
                              start=(a == 0), stop=(a == 1), inc=(g == 7 and a == 1))
                rd[xx] = [t, t10]
                src = bk[xx][:, :].rearrange("p (g c e) -> p e c g", g=8, c=4)
                dst = G.rearrange("p e (c g) -> p e c g", c=4)[:, :, :, g8]
                t_gm = s.bf[xx] = V([t, t_g], ve.tensor_tensor, dst, dst, src, ALU.mult)
            yield
            for e in range(16):
                t = T([t_gm, s.bf[0]], te.matmul, bk[0][:, 0:256], G[:, e, :], w["eu"][:, e, :],
                      start=(e == 0), stop=(e == 15), inc=(e == 15))
            t = s.bf[0] = add_x(s, b, bk[0][:, 0:256], t)
            s.done = [t, t10]
            s.x_t[b] = t
            yield

        def moe(s, b):
            w = W[3]
            bk = s.bk
            t_ln = ln(s, b)
            yield
            t_xT = xpose(s, t_ln)
            yield
            pr = s.sm[:, 16:24]
            bg = s.sm[:, 24:32]
            s8 = s.sm[:, 32:40]
            i8 = s.sm[:, 40:48].bitcast(U32)
            i8f = s.sm[:, 48:56]
            sel = s.sm[:, 56:72]
            mk = s.sm[:, 72:80]
            mm = s.sm[:, 80:82]
            pT = s.ar[0:8, 0:128]
            acc = s.ar[:, 128:384]
            uT = [s.ar[:, 384 + 256 * i:640 + 256 * i].rearrange("p (k n) -> p k n", k=2) for i in range(2)]
            gT = [s.ar[:, 896 + 256 * i:1152 + 256 * i].rearrange("p (k n) -> p k n", k=2) for i in range(2)]
            t_b = [s.done, t_xT]
            for o, extra in ((0, False), (8, True)):
                r = bk[1][:, o:o + 7]
                T([w["t"], ts, t_xT, s.bf[1], t_const], te.matmul, r, s.xT[:, 0], wr[:, 0], start=True, stop=False, inc=0)
                T(None, te.matmul, r, s.xT[:, 1], wr[:, 1], start=False, stop=False, inc=0)
                t = T(None, te.matmul, r, ones_row, rb[0:1, 0:7], start=False, stop=not extra)
                if extra:
                    t = T(None, te.matmul, r, ones_row, rb[0:1, 8:15], start=False, stop=True)
            t1 = V(t_b, ve.memset, bg, -3e38)
            t1 = V([t, t1], ve.tensor_copy, bg[:, 0:7], bk[1][:, 8:15])
            t1 = V(t1, ve.max, s8, bg)
            t1 = V(t1, ve.max_index, i8, s8, bg)
            t1 = V(t1, ve.tensor_copy, i8f, i8)
            t2 = V(t1, ve.tensor_scalar, sel[:, 0:8], iota8, i8f[:, 0:1], None, ALU.is_equal)
            t2 = V(t1, ve.tensor_scalar, sel[:, 8:16], iota8, i8f[:, 1:2], None, ALU.is_equal)
            t2 = V(t2, ve.tensor_tensor, sel[:, 0:8], sel[:, 0:8], sel[:, 8:16], ALU.add)
            t2 = V(t2, ve.tensor_scalar, mk, sel[:, 0:8], -1.0, 1e30, ALU.add, ALU.mult)
            t2 = V(t2, ve.tensor_tensor, mk[:, 0:7], mk[:, 0:7], bk[1][:, 0:7], ALU.add)
            s.bf[1] = t2
            t2 = V(t2, ve.tensor_reduce, mm[:, 0:1], mk[:, 0:7], AX.X, ALU.max)
            t2 = V(t2, ve.tensor_scalar, mk[:, 0:7], mk[:, 0:7], mm[:, 0:1], None, ALU.subtract)
            t2 = S(t2, se.activation, mk[:, 0:7], mk[:, 0:7], ACT.Exp)
            yield
            t2 = V(t2, ve.tensor_reduce, mm[:, 1:2], mk[:, 0:7], AX.X, ALU.add)
            t2 = V(t2, ve.reciprocal, mm[:, 1:2], mm[:, 1:2])
            V(None, ve.memset, pr[:, 7:8], 1.0)
            t_p = V(t2, ve.tensor_scalar, pr[:, 0:7], mk[:, 0:7], mm[:, 1:2], None, ALU.mult)
            t = T([t_p, s.bf[0]], te.transpose, bk[0][0:8, 0:128], pr, ident)
            t = s.bf[0] = V([t, t_b], ve.tensor_copy, pT, bk[0][0:8, 0:128])
            yield
            t = T([t, s.bf[1]], te.matmul, bk[1][:, 0:256], pT, bdn[:, :], start=True, stop=True)
            t_acc = s.bf[1] = V([t, t_b], ve.tensor_tensor, acc, x[:, b, :], bk[1][:, 0:256], ALU.add)
            rd_u, rd_g = [None, None], [None, None]
            for e in range(8):
                i = e % 2
                for m in range(2):
                    for k in range(2):
                        t = T([t_xT, s.bf[0]], te.matmul, bk[0][:, m * 128:(m + 1) * 128], w["Wup"][:, e, k, m * 128:(m + 1) * 128],
                              s.xT[:, k, :], start=(k == 0), stop=(k == 1), inc=(k == 1 and m == 1))
                b0 = bk[0][:, 0:256].rearrange("p (m n) -> p m n", m=2)
                b1 = bk[1][:, 0:256].rearrange("p (m n) -> p m n", m=2)
                t_u = s.bf[0] = V([t, t_b, rd_u[i]], ve.tensor_tensor, uT[i], b0, bc(bu[:, 0, 2 * e:2 * e + 2], 2, [128, 2, 128]), ALU.add)
                yield
                for m in range(2):
                    for k in range(2):
                        t = T([t_u, s.bf[1]], te.matmul, bk[1][:, m * 128:(m + 1) * 128], w["Wgate"][:, e, k, m * 128:(m + 1) * 128],
                              uT[i][:, k], start=(k == 0), stop=(k == 1), inc=(k == 1 and m == 1))
                for m in range(2):
                    t_s = S([t, t_b, rd_g[i]], se.activation, gT[i][:, m], b1[:, m], ACT.Silu, bias=bu[:, 1, 2 * e + m:2 * e + m + 1])
                s.bf[1] = t_s
                t_g = rd_u[i] = V([t_s, rd_g[i]], ve.tensor_tensor, gT[i], gT[i], uT[i], ALU.mult)
                yield
                for k in range(2):
                    t = T([t_g, s.bf[1]], te.matmul, bk[1][:, 0:256], gT[i][:, k, :],
                          w["Wdown"][:, e, k, :], start=(k == 0), stop=(k == 1), inc=(k == 1))
                rd_g[i] = t
                dst = acc if e < 7 else x[:, b]
                t_acc = s.bf[1] = V([t, t_acc, t_p], ve.scalar_tensor_tensor, dst, bk[1][:, 0:256],
                                    pr[:, e:e + 1], acc, ALU.mult, ALU.add)
                yield
            s.done = t_acc
            s.x_t[b] = t_acc

        def tern_prep(s):
            w = W[5]
            tmp = w["tmp"]
            sm = s.sm
            t0 = [s.done, w["t"]]
            raw = area[1]
            t = V(t0, ve.tensor_reduce, sm[:, 0:1], raw[:, 0:1364], AX.X, ALU.add, apply_absolute_value=True)
            t = V(t0, ve.tensor_reduce, sm[:, 1:2], raw[:, 1364:2728], AX.X, ALU.add, apply_absolute_value=True)
            t = V(t0, ve.tensor_reduce, sm[:, 2:3], raw[:, 2728:2728 + 1280], AX.X, ALU.add, apply_absolute_value=True)
            t = V(t0, ve.tensor_reduce, sm[0:42, 3:4], raw[0:42, 4008:4264], AX.X, ALU.add, apply_absolute_value=True)
            t = V(t, ve.tensor_tensor, sm[0:42, 2:3], sm[0:42, 2:3], sm[0:42, 3:4], ALU.add)
            t = T([t, s.bf[0]], te.matmul, s.bk[0][:, 0:3], ones_sq, sm[:, 0:3], start=True, stop=True)
            t = V(t, ve.tensor_scalar, sm[:, 4:7], s.bk[0][:, 0:3], 1.0 / (682 * 256), None, ALU.mult)
            s.bf[0] = t
            t = V(t, ve.tensor_scalar, sm[:, 8:11], sm[:, 4:7], 0.5, None, ALU.mult)
            t = V(t, ve.tensor_scalar, sm[:, 12:15], sm[:, 4:7], -0.5, None, ALU.mult)
            for j, (lo, hi, rows) in enumerate(((0, 1364, 128), (1364, 2728, 128), (2728, 4008, 128), (4008, 4264, 42))):
                q = min(j, 2)
                r = raw[0:rows, lo:hi]
                m = tmp[0:rows, lo:hi]
                t1 = V(t, ve.tensor_scalar, m, r, sm[0:rows, 8 + q:9 + q], None, ALU.is_gt)
                t2 = V(t, ve.tensor_scalar, s.ar[0:rows, 0:hi - lo], r, sm[0:rows, 12 + q:13 + q], None, ALU.is_lt)
                t2 = V([t1, t2], ve.tensor_tensor, m, m, s.ar[0:rows, 0:hi - lo], ALU.subtract)
                t2 = V(t2, ve.scalar_tensor_tensor, m, m, sm[0:rows, 4 + q:5 + q], r, ALU.mult, ALU.subtract)
                t = V(t2, ve.tensor_tensor, r, r, m, ALU.add)
            w["tq"] = t
            s.done = [s.done, t]
            return
            yield

        def tern(s, b):
            w = W[5]
            bk = s.bk
            t_ln = ln(s, b)
            yield
            t_xT = xpose(s, t_ln)
            yield
            a = s.ar[:, 0:512]
            g = s.ar[:, 512:1280].rearrange("p (k n) -> p k n", k=6)
            t_b = [s.done, t_xT]
            for c in range(2):
                nt = 4 if c == 0 else 2
                for q, wm in ((0, w["w1"]), (1, w["w3"])):
                    for m in range(nt):
                        mt = 4 * c + m
                        M = 42 if mt == 5 else 128
                        for k in range(2):
                            t = T([t_xT, w["tq"], s.bf[q]], te.matmul, bk[q][0:M, m * 128:(m + 1) * 128],
                                  wm[:, k, mt * 128:mt * 128 + M], s.xT[:, k, :], start=(k == 0), stop=(k == 1),
                                  inc=(k == 1 and m == nt - 1))
                for lo, hi, M in (((0, 4, 128),) if c == 0 else ((0, 1, 128), (1, 2, 42))):
                    cs_ = slice(lo * 128, hi * 128)
                    t1 = S([t, t_b], se.activation, a[0:M, cs_], bk[0][0:M, cs_], ACT.Silu)
                    t2 = V([t1, t], ve.tensor_tensor, g[0:M, 4 * c + lo:4 * c + hi, :].rearrange("p k n -> p (k n)"),
                           a[0:M, cs_], bk[1][0:M, cs_], ALU.mult)
                s.bf[0], s.bf[1] = t1, t2
                t_b = [t_b, t2]
                yield
            for k in range(6):
                M = 42 if k == 5 else 128
                t = T([t2, s.bf[0]], te.matmul, bk[0][:, 0:256], g[0:M, k, :],
                      w["w2"][0:M, k, :], start=(k == 0), stop=(k == 5), inc=(k == 5))
            t = s.bf[0] = add_x(s, b, bk[0][:, 0:256], t)
            s.done = t
            s.x_t[b] = t
            yield

        def quant(s_, src, dst, n, sc, tm, waits):
            nb = n // 32
            s3 = src.rearrange("p (b k) -> p b k", k=32)
            d3 = dst.rearrange("p (b k) -> p b k", k=32)
            am, iv = sc[:, 0:nb], sc[:, 32:32 + nb]
            t = V(waits, ve.tensor_reduce, am, s3, AX.X, ALU.max, apply_absolute_value=True)
            t = V(t, ve.tensor_scalar, am, am, 1.0 / 448.0, 1e-30, ALU.mult, ALU.max)
            t = V(t, ve.reciprocal, iv, am)
            t = V(t, ve.tensor_tensor, d3, s3, bc(iv, 2, [128, nb, 32]), ALU.mult)
            yield
            t = V(t, ve.tensor_scalar, tm.bitcast(U32), dst.bitcast(U32), 0x7f800000, None, ALU.bitwise_and)
            t = V(t, ve.tensor_scalar, tm, tm, 1572864.0, 24576.0, ALU.mult, ALU.max)
            t = V(t, ve.tensor_tensor, dst, dst, tm, ALU.add)
            t = V(t, ve.tensor_tensor, dst, dst, tm, ALU.subtract)
            yield
            t = V(t, ve.tensor_tensor, d3, d3, bc(am, 2, [128, nb, 32]), ALU.mult)
            s_.t_q = t
            return t

        def mx_prep(s, blk):
            w = W[7]
            raw = w["raw"].rearrange("p a n -> p (a n)")
            bk = s.bk
            q = s.ar[:, 0:1024]
            t = yield from quant(s, raw[:, blk * 1024:(blk + 1) * 1024], q, 1024, s.sm[:, 32:96], s.ar[:, 1024:2048],
                                 [s.done, w["t"]])
            for i in range(2):
                for c in range(4 * i, 4 * i + 4):
                    tt = T([t, s.bf[i], t_const], te.transpose, bk[i][:, (c % 4) * 128:(c % 4 + 1) * 128],
                           q[:, c * 128:(c + 1) * 128], ident, inc=(c % 4 == 3))
                src = bk[i][:, :].rearrange("p (r k n) -> p k r n", r=2, k=2)
                if blk < 4:
                    r = 4 * (blk % 2) + 2 * i
                    dst = (w["g"], w["u"])[blk // 2][:, :, r * 128:(r + 2) * 128].rearrange("p k (r n) -> p k r n", r=2)
                else:
                    src = bk[i][:, :].rearrange("p (c n) -> p c n", c=4)
                    dst = w["d"][:, 4 * i:4 * i + 4, (blk - 4) * 128:(blk - 3) * 128]
                s.bf[i] = S(tt, se.copy, dst, src)
            w.setdefault("tp", []).append(s.bf[1])
            s.done = [s.done, tt, s.t_q, s.bf[0], s.bf[1]]
            yield

        def mx(s, b):
            w = W[7]
            bk = s.bk
            t_ln = ln(s, b)
            yield
            t = yield from quant(s, s.xn[:, :], s.xn[:, :], 256, s.sm[:, 32:96], s.ar[:, 0:256], [t_ln, s.done])
            t_xT = xpose(s, t)
            yield
            g = s.ar[:, 0:1024]
            h = s.ar[:, 1024:2048]
            tm = s.ar[:, 2048:3072]
            hT = s.ar[:, 3072:4096].rearrange("p (k n) -> p k n", k=8)
            t_b = [t_xT, s.done]
            for c in range(2):
                for q, wm in ((0, w["g"]), (1, w["u"])):
                    for k in range(2):
                        t = T([t_xT, w["tp"], s.bf[q]], te.matmul, bk[q][:, :], s.xT[:, k, :],
                              wm[:, k, c * 512:(c + 1) * 512], start=(k == 0), stop=(k == 1), inc=(k == 1))
                t1 = s.bf[0] = S([t, t_b], se.activation, g[:, c * 512:(c + 1) * 512], bk[0][:, :], ACT.Silu)
                t2 = s.bf[1] = V([t1, t_b, t], ve.tensor_tensor, h[:, c * 512:(c + 1) * 512], g[:, c * 512:(c + 1) * 512],
                                 bk[1][:, :], ALU.mult)
                yield
            t = yield from quant(s, h, h, 1024, s.sm[:, 32:96], tm, t2)
            yield
            for c in range(2):
                for k in range(4):
                    tt = T([t, s.bf[c]], te.transpose, bk[c][:, k * 128:(k + 1) * 128], h[:, (4 * c + k) * 128:(4 * c + k + 1) * 128],
                           ident, inc=(k == 3))
                s.bf[c] = S([tt, t_b], se.copy, hT[:, 4 * c:4 * c + 4, :], bk[c][:, :].rearrange("p (k n) -> p k n", k=4))
            t = s.bf[1]
            yield
            for k in range(8):
                t = T([t, s.bf[0]], te.matmul, bk[0][:, 0:256], hT[:, k, :], w["d"][:, k, :], start=(k == 0), stop=(k == 7),
                      inc=(k == 7))
            t = s.bf[0] = add_x(s, b, bk[0][:, 0:256], t)
            s.done = t
            s.x_t[b] = t
            yield

        x_t = {b: [t_x0] for b in range(NB)}
        for s in slots:
            s.x_t = x_t
        load_weights(SUBS[0], None)
        ts = load_small()
        t_gp = V([ts], ve.tensor_tensor, gp[:, :], gqk[:, 0:1], gqk[:, 1:2], ALU.mult)
        if len(SUBS) > 1:
            load_weights(SUBS[1], None if SUBS[1] % 2 != SUBS[0] % 2 else [s.done for s in slots])
        todo = [list(range(NB)) for _ in SUBS]
        through = [0] * NB
        left = [NS] * len(SUBS)
        blocks = list(range(6))
        MORE = "more"

        def worker(s):
            for n, k in enumerate(SUBS):
                while W[k] is None:
                    yield MORE
                if k in (0, 4):
                    yield from small_init(s, 0 if k == 0 else 2)
                if k == 5:
                    if "started" not in W[5]:
                        W[5]["started"] = True
                        yield from tern_prep(s)
                    while "tq" not in W[5]:
                        yield MORE
                if k == 7:
                    while blocks:
                        yield from mx_prep(s, blocks.pop(0))
                    while len(W[7].get("tp", ())) < 6:
                        yield MORE
                while todo[n]:
                    b = next((b for b in todo[n] if through[b] == n), None)
                    if b is None:
                        yield MORE
                        continue
                    todo[n].remove(b)
                    if k in (0, 4):
                        yield from small_attn(s, b, 0 if k == 0 else 2)
                    if k in (2, 6):
                        yield from big_attn(s, b, 1 if k == 2 else 3)
                    if k == 1:
                        yield from peer(s, b)
                    if k == 3:
                        yield from moe(s, b)
                    if k == 5:
                        yield from tern(s, b)
                    if k == 7:
                        yield from mx(s, b)
                    through[b] = n + 1
                left[n] -= 1
                ends[n] = ends.get(n, []) + [s.done]
                if left[n] == 0 and n + 2 < len(SUBS):
                    load_weights(SUBS[n + 2], ends[n])

        ends = {}
        ready = [[40000.0 * 0 + s.i, worker(s)] for s in slots]
        while ready:
            r = min(ready, key=lambda e: e[0])
            clock["last"] = 0.0
            try:
                if next(r[1]) == MORE:
                    r[0] = min([e[0] for e in ready if e is not r] + [1e12]) + 1.0
                else:
                    r[0] = clock["last"]
            except StopIteration:
                ready.remove(r)

        for u in range(NB):
            t = st_o([x_t[u]], out[u], x[:, u, :])
        D([t], nc.sync.nop, inc=0)

        block = ctx.enter_context(nc.Block())

        @block.sync
        def _(eng):
            D.run(eng)

        @block.vector
        def _(eng):
            V.run(eng)

        @block.scalar
        def _(eng):
            S.run(eng)

        @block.tensor
        def _(eng):
            T.run(eng)

        @block.gpsimd
        def _(eng):
            P.run(eng)


_PLAIN = ["L0_xattn_Wq", "L0_xattn_Wkv", "L0_xattn_Wout", "L0_xattn_bout", "L0_ffn_Wq", "L0_ffn_e_up",
          "L1_xattn_Wq", "L1_xattn_Wk", "L1_xattn_Wv", "L1_xattn_Wo", "L1_ffn_Wr", "L1_ffn_br",
          "L1_ffn_gate_bias", "L1_ffn_Wup", "L1_ffn_Wgate", "L1_ffn_Wdown", "L1_ffn_Wsu", "L1_ffn_Wsg",
          "L1_ffn_Wsd", "L2_xattn_Wq", "L2_xattn_bq", "L2_xattn_Wk", "L2_xattn_bk", "L2_xattn_Wv",
          "L2_xattn_bv", "L2_xattn_Wkv_dca", "L2_xattn_bkv_dca", "L2_xattn_qn_w", "L2_xattn_qn_b",
          "L2_xattn_kn_w", "L2_xattn_kn_b", "L2_xattn_kn_dca_w", "L2_xattn_kn_dca_b", "L2_xattn_Wo",
          "L2_xattn_bo", "L3_xattn_Wq", "L3_xattn_Wk", "L3_xattn_Wv", "L3_xattn_Wo", "L3_ffn_gate_w",
          "L3_ffn_up_w", "L3_ffn_down_w"]


def _constants():
    c = np.zeros((128, C_N), np.float32)
    c[:, C_ID:C_ID + 128] = np.eye(128)
    c[:, C_I128:C_I128 + 128] = np.arange(128)
    c[:, C_I64:C_I64 + 64] = np.arange(64)
    c[:, C_I8:C_I8 + 8] = np.arange(8)
    p = np.arange(128)
    c[:, C_MM] = p < 112
    c[:, C_MD] = p >= 112
    c[:, C_PC] = 16 * (p // 32)
    c[:, C_ONE:C_ONE + 128] = 1
    return c


def kernel(**inputs):
    import concourse.bacc as _bacc
    from concourse.bass_utils import run_bass_kernel_spmd as _run

    I = {k: np.asarray(v) for k, v in inputs.items()}
    a = {n: I[n] for n in _PLAIN}
    a["x"] = I["x"]
    a["fside"] = I["fside_BxSx2_0"]
    a["ctxT"] = I["ctx_1024"].reshape(2048, 128).T
    a["maskT"] = I["mask_BxS2_bf1"].T.view(np.uint8) if I["mask_BxS2_bf1"].dtype == np.bool_ else I["mask_BxS2_bf1"].T
    a["edT"] = I["L0_ffn_e_down"].T
    a["keysT"] = I["L0_ffn_keys"].transpose(2, 3, 0, 1).reshape(128, 4, 128)
    bup = np.concatenate([I["L1_ffn_bup"], I["L1_ffn_bsu"][None]], 0)
    bga = np.concatenate([I["L1_ffn_bgate"], I["L1_ffn_bsg"][None]], 0)
    a["bugT"] = np.stack([bup.reshape(16, 128).T, bga.reshape(16, 128).T], 1)
    a["bdown"] = np.concatenate([I["L1_ffn_bdown"], I["L1_ffn_bsd"][None]], 0)
    a["w1T"], a["w3T"], a["w2T"] = I["L2_ffn_w1"].T, I["L2_ffn_w3"].T, I["L2_ffn_w2"].T
    kv = np.concatenate([I["L2_xattn_Wk"], I["L2_xattn_Wv"]], 1).reshape(128, 16, 2, 16)
    a["L2_xattn_Wk"], a["L2_xattn_Wv"] = kv[:, :, 0].reshape(128, 256), kv[:, :, 1].reshape(128, 256)
    bkv = np.concatenate([I["L2_xattn_bk"], I["L2_xattn_bv"]]).reshape(16, 2, 16)
    a["L2_xattn_bk"], a["L2_xattn_bv"] = bkv[:, 0].reshape(256), bkv[:, 1].reshape(256)
    a["gqk"] = np.stack([I["L3_xattn_gq"], I["L3_xattn_gk"]], 1)
    a["consts"] = _constants()

    nc = _bacc.Bacc("TRN2", target_bir_lowering=False, num_devices=1)
    arrays, aps = {}, {}
    for name, v in a.items():
        v = np.ascontiguousarray(v)
        arrays[f"in_{name}"] = v
        aps[name] = nc.dram_tensor(f"in_{name}", v.shape, mybir.dt.from_np(v.dtype), kind="ExternalInput").ap()
    o = nc.dram_tensor("out_0", (16, 128, 256), F32, kind="ExternalOutput").ap()
    program(nc, aps, o)
    return _run(nc, [arrays], core_ids=[0]).results[0]["out_0"]
```

```python
import math
from contextlib import ExitStack

import numpy as np
import concourse.bass as bass
from concourse import mybir

SUBS = (0, 1, 2, 3, 4, 5, 6, 7)

F32 = mybir.dt.float32
BF16 = mybir.dt.bfloat16
F16 = mybir.dt.float16
U32 = mybir.dt.uint32
U8 = mybir.dt.uint8
ALU = mybir.AluOpType
ACT = mybir.ActivationFunctionType
AX = mybir.AxisListType

NB = 16
NS = 4
AR = 4684
C_ID, C_I128, C_I64, C_I8, C_MM, C_MD, C_PC, C_ONE, C_N = 0, 128, 256, 320, 328, 329, 330, 332, 460


LAG = {"s_dve": 130.0, "s_act": 150.0, "s_pe": 190.0, "s_pool": 120.0}


class Queue:

    def __init__(self, sem, cost, clock):
        self.sem, self.n, self.ops, self.seen = sem, 0, [], {}
        self.cost, self.at, self.clock = cost, 0.0, clock

    def __call__(self, waits, f, *args, inc=1, sem=None, step=1, **kw):
        need = []
        start = self.at
        for sem_, n in flat(waits):
            start = max(start, self.clock.get((sem_.name, n), 0.0) + LAG.get(sem_.name, 0.0))
            if self.seen.get(sem_.name, 0) < n:
                self.seen[sem_.name] = n
                need = [(s, k) for s, k in need if s.name != sem_.name] + [(sem_, n)]
        if sem is None:
            self.at = start + self.cost(args, kw)
            self.ops.append((need, f, args, kw, self.sem if inc else None, 1))
            if inc:
                self.n += 1
                self.clock[(self.sem.name, self.n)] = self.at
                self.clock["last"] = max(self.clock.get("last", 0.0), self.at)
            return (self.sem, self.n)
        self.at = start + self.cost(args, kw)
        self.ops.append((need, f, args, kw, sem, step))
        return None

    def run(self, eng):
        for need, f, args, kw, sem, step in self.ops:
            for s, n in need:
                eng.wait_ge(s, n)
            ins = f(*args, **kw)
            if sem is not None:
                ins.then_inc(sem, step)


def flat(waits):
    if waits is None:
        return []
    if isinstance(waits, tuple) and len(waits) == 2 and isinstance(waits[1], int):
        return [waits]
    return [t for w in waits for t in flat(w)]


class Load:

    def __init__(self, q, dma, sem):
        self.q, self.dma, self.sem, self.n = q, dma, sem, 0

    def __call__(self, waits, dst, src):
        self.q(waits, self.dma, dst, src, sem=self.sem, step=16)
        self.n += 16
        self.q.at += 4.0 * int(np.prod(dst.shape)) / 180.0
        self.q.clock[(self.sem.name, self.n)] = self.q.at + 2500.0
        return (self.sem, self.n)


class Slot:
    pass


def width(ap):
    return int(np.prod(ap.shape[1:]))


def pe_cost(args, kw):
    n, w = max(width(args[0]), 24), args[1]
    f = 4 if w.dtype == F32 else 1
    c = n * f / 2.4
    if "start" not in kw:
        return c
    if w.shape[0] <= 64:
        c *= 2
    return max(c, 426.0 if w.dtype == F32 and n <= 64 else 0.0)


def dve_cost(args, kw):
    aps = [a for a in args if isinstance(a, bass.AP)]
    return 68.0 + 1.04 * max((width(a) for a in aps), default=1)


def act_cost(args, kw):
    return 80.0 + 0.83 * width(args[0])


def pool_cost(args, kw):
    if ALU.pow in args:
        return 200.0 + 177.0 * width(args[0])
    return 113.0 + 2.19 * width(args[0])


def no_cost(args, kw):
    return 50.0


def bc(ap, axis, shape):
    return ap.unsqueeze(axis).to_broadcast(shape)


def program(nc, A, out):
    ctx = ExitStack()
    with ctx:
        def sb(name, shape, dt=F32):
            return ctx.enter_context(nc.sbuf_tensor(name, shape, dt))

        def sem(name):
            return ctx.enter_context(nc.semaphore(name))

        x = sb("x", [128, NB, 256])
        ctxT = sb("ctxT", [128, NB * 128])
        area = [sb("areaA", [128, 12288]), sb("areaB", [128, 12288])]
        cst = sb("cst", [128, C_N])
        idh = sb("idh", [128, 128], F16)
        i128h = sb("i128h", [128, 128], F16)
        i64h = sb("i64h", [128, 64], F16)
        neghalf = sb("neghalf", [128, 32])
        cs = sb("cs", [128, 2, NB * 4])
        mbias = sb("mbias", [128, NB])
        mkey = sb("mkey", [128, NB])

        slots = []
        for i in range(NS):
            s = Slot()
            s.i = i
            s.xn = sb(f"xn{i}", [128, 256])
            s.xT = sb(f"xT{i}", [128, 2, 128])
            s.ar = sb(f"ar{i}", [128, AR])
            s.sm = sb(f"sm{i}", [128, 128])
            s.bk = [ctx.enter_context(nc.psum_tensor(f"pb{i}_{j}", [128, 512], F32)) for j in range(2)]
            s.bf = [None] * 2
            s.done = None
            slots.append(s)

        clock = {}
        V = Queue(sem("s_dve"), dve_cost, clock)
        S = Queue(sem("s_act"), act_cost, clock)
        T = Queue(sem("s_pe"), pe_cost, clock)
        P = Queue(sem("s_pool"), pool_cost, clock)
        D = Queue(sem("s_sp"), no_cost, clock)
        ve, se, te, pe_ = nc.vector, nc.scalar, nc.tensor, nc.gpsimd

        ld_c = Load(D, nc.sync.dma_start, sem("d_c"))
        ld_x = Load(D, nc.sync.dma_start, sem("d_x"))
        ld_w = [Load(D, nc.sync.dma_start, sem(f"d_w{k}")) for k in range(8)]
        st_o = Load(D, nc.sync.dma_start, sem("d_o"))

        ident = cst[:, C_ID:C_ID + 128]
        ones_row = cst[0:1, C_ONE:C_ONE + 128]
        ones_sq = cst[:, C_ONE:C_ONE + 128]
        iota8 = cst[:, C_I8:C_I8 + 8]

        ld_c(None, cst[:, :], A["consts"])
        t_c = ld_c(None, cs[:, 0, :].rearrange("p (b k) -> p b k", k=4)[:, :, 0:2],
                   A["fside"].rearrange("b t p -> t b p"))
        t_x0 = ld_x(None, x[:, :, :], A["x"].rearrange("b t d -> t b d"))
        t_ctx = ld_x(None, ctxT[:, :], A["ctxT"])
        m8 = slots[1].ar[:, 0:4].bitcast(U8)
        t_m8 = ld_x(None, m8, A["maskT"])

        t_k = V(t_c, ve.tensor_copy, idh[:, :], ident)
        t_k = V(t_c, ve.tensor_copy, i128h[:, :], cst[:, C_I128:C_I128 + 128])
        t_k = V(t_c, ve.tensor_copy, i64h[:, :], cst[:, C_I64:C_I64 + 64])
        t_k = V(None, ve.memset, neghalf[:, :], -0.5)
        t_m = V(t_m8, ve.tensor_copy, mkey[:, :], m8)
        t_k = V(t_m, ve.tensor_scalar, mbias[:, :], mkey[:, :], -1.0, 1e30, ALU.add, ALU.mult)

        ang = slots[0].ar[:, 0:64].rearrange("p (b q j) -> p b q j", q=2, j=2)
        pos = cs[:, 0, :].rearrange("p (b k) -> p b k", k=4)[:, :, 0:2]
        t = V(t_c, ve.tensor_copy, ang[:, :, :, 0], pos)
        t = V(t_c, ve.tensor_scalar, ang[:, :, :, 1], pos, float(np.float32(0.01)), None, ALU.mult)
        af = slots[0].ar[:, 0:64]
        MAGIC = 12582912.0
        for which, off in ((1, 0.0), (0, math.pi / 2)):
            a0 = slots[0].ar[:, 64:128]
            n0 = slots[0].ar[:, 128:192]
            t = V(t, ve.tensor_scalar, a0, af, off, None, ALU.add)
            t = V(t, ve.tensor_scalar, n0, a0, 1.0 / (2 * math.pi), MAGIC, ALU.mult, ALU.add)
            t = V(t, ve.tensor_scalar, n0, n0, MAGIC, None, ALU.subtract)
            t = V(t, ve.scalar_tensor_tensor, a0, n0, -6.28125, a0, ALU.mult, ALU.add)
            t = V(t, ve.scalar_tensor_tensor, a0, n0, -(2 * math.pi - 6.28125), a0, ALU.mult, ALU.add)
            t = V(t, ve.tensor_scalar, a0, a0, 3.1415925, -3.1415925, ALU.min, ALU.max)
            t = S(t, se.activation, cs[:, which, :], a0, ACT.Sin)
        t_cs = t
        slots[0].done = [t_cs, t_k]
        for s in slots[1:]:
            s.done = [t_k, t_m]
        t_const = [t_k, t_c]

        def put(k, off, dims, src, waits, rows=128):
            n = int(np.prod(dims))
            v = area[k % 2][0:rows, off:off + n]
            if len(dims) == 2:
                v = v.rearrange("p (a b) -> p a b", a=dims[0])
            if len(dims) == 3:
                v = v.rearrange("p (a b c) -> p a b c", a=dims[0], b=dims[1])
            if src is not None:
                ld_w[k](waits, v, src)
            return v

        W = [None] * 8

        def kp(ap, k):
            return ap.rearrange("(k p) n -> p k n", k=k)

        def load_weights(k, w):
            d = {}
            if k == 0:
                d["wq"] = put(k, 0, [2, 256], kp(A["L0_xattn_Wq"], 2), w)
                d["wkv"] = put(k, 512, [512], A["L0_xattn_Wkv"], w)
                d["wo"] = put(k, 1024, [2, 256], kp(A["L0_xattn_Wout"], 2), w)
                d["bo"] = put(k, 1536, [256], A["L0_xattn_bout"].partition_broadcast(128), w)
            if k == 1:
                d["ed"] = put(k, 0, [2, 2048], kp(A["edT"], 2), w)
                d["eu"] = put(k, 4096, [16, 256], kp(A["L0_ffn_e_up"], 16), w)
                d["wq"] = put(k, 8192, [2, 512], kp(A["L0_ffn_Wq"], 2), w)
                d["keys"] = put(k, 9216, [4, 128], A["keysT"], w)
            if k == 2:
                d["wq"] = put(k, 0, [2, 2048], kp(A["L1_xattn_Wq"], 2), w)
                d["wk"] = put(k, 4096, [1024], A["L1_xattn_Wk"], w)
                d["wv"] = put(k, 5120, [1024], A["L1_xattn_Wv"], w)
                d["wo"] = put(k, 6144, [16, 256], kp(A["L1_xattn_Wo"], 16), w)
            if k == 3:
                for j, (n, m) in enumerate((("Wup", "Wsu"), ("Wgate", "Wsg"), ("Wdown", "Wsd"))):
                    v = area[1][:, 4096 * j:4096 * (j + 1)].rearrange("p (e k n) -> p e k n", e=8, k=2)
                    d[n] = v
                    for e in range(7):
                        ld_w[k](w, v[:, e], kp(A["L1_ffn_" + n][e], 2))
                    ld_w[k](w, v[:, 7], kp(A["L1_ffn_" + m], 2))
            if k == 4:
                d["wq"] = put(k, 0, [2, 256], kp(A["L2_xattn_Wq"], 2), w)
                d["wk"] = put(k, 512, [256], A["L2_xattn_Wk"], w)
                d["wv"] = put(k, 768, [256], A["L2_xattn_Wv"], w)
                d["wd"] = put(k, 1024, [512], A["L2_xattn_Wkv_dca"], w)
                d["wo"] = put(k, 1536, [2, 256], kp(A["L2_xattn_Wo"], 2), w)
                d["bo"] = put(k, 2048, [256], A["L2_xattn_bo"].partition_broadcast(128), w)
                d["bqk"] = area[0][:, 2304:2816]
                d["bv"] = area[0][:, 2816:3072]
                ld_w[k](w, area[0][:, 2304:2560], A["L2_xattn_bq"].partition_broadcast(128))
                ld_w[k](w, area[0][0:112, 2560:2816], A["L2_xattn_bk"].partition_broadcast(112))
                ld_w[k](w, area[0][0:112, 2816:3072], A["L2_xattn_bv"].partition_broadcast(112))
                ld_w[k](w, area[0][112:128, 2560:3072], A["L2_xattn_bkv_dca"].partition_broadcast(16))
                ww = area[0][:, 3584:3648].rearrange("p (a b c) -> p a b c", a=2, b=2)
                d["nw"] = ww
                for c, sfx in ((0, "w"), (1, "b")):
                    ld_w[k](w, ww[:, c, 0], A["L2_xattn_qn_" + sfx].partition_broadcast(128))
                    ld_w[k](w, ww[0:112, c, 1], A["L2_xattn_kn_" + sfx].partition_broadcast(112))
                    ld_w[k](w, ww[112:128, c, 1], A["L2_xattn_kn_dca_" + sfx].partition_broadcast(16))
            if k == 5:
                d["w1"] = put(k, 0, [2, 682], kp(A["w1T"], 2), w)
                d["w3"] = put(k, 1364, [2, 682], kp(A["w3T"], 2), w)
                v = put(k, 2728, [6, 256], None, w)
                d["w2"] = v
                ld_w[k](w, v[:, 0:5], kp(A["w2T"][0:640], 5))
                ld_w[k](w, v[0:42, 5], A["w2T"][640:682])
                d["tmp"] = area[1][:, 4264:8528]
            if k == 6:
                d["wq"] = put(k, 0, [2, 2048], kp(A["L3_xattn_Wq"], 2), w)
                d["wk"] = put(k, 4096, [2048], A["L3_xattn_Wk"], w)
                d["wv"] = put(k, 6144, [2048], A["L3_xattn_Wv"], w)
                d["wo"] = put(k, 8192, [16, 256], kp(A["L3_xattn_Wo"], 16), w)
            if k == 7:
                d["raw"] = put(k, 0, [24, 256], None, w)
                ld_w[k](w, d["raw"][:, 0:8], kp(A["L3_ffn_gate_w"], 8))
                ld_w[k](w, d["raw"][:, 8:16], kp(A["L3_ffn_up_w"], 8))
                ld_w[k](w, d["raw"][:, 16:24].rearrange("p (k c) n -> p k (c n)", k=2), kp(A["L3_ffn_down_w"], 2))
                d["g"] = put(k, 6144, [2, 1024], None, w)
                d["u"] = put(k, 8192, [2, 1024], None, w)
                d["d"] = put(k, 10240, [8, 256], None, w)
            d["t"] = (ld_w[k].sem, ld_w[k].n)
            W[k] = d

        wr = sb("wr", [128, 2, 7])
        rb = sb("rb", [1, 16])
        bu = sb("bu", [128, 2, 16])
        bdn = sb("bdn", [8, 256])
        gqk = sb("gqk", [128, 2])
        gp = sb("gp", [128, 1])
        ld_s = Load(D, nc.sync.dma_start, sem("d_s"))

        def load_small():
            ld_s(None, wr[:, :, :], kp(A["L1_ffn_Wr"], 2))
            ld_s(None, rb[0:1, 0:7], A["L1_ffn_br"].unsqueeze(0))
            ld_s(None, rb[0:1, 8:15], A["L1_ffn_gate_bias"].unsqueeze(0))
            ld_s(None, bu[:, :, :], A["bugT"])
            ld_s(None, bdn[:, :], A["bdown"])
            t = ld_s(None, gqk[:, :], A["gqk"])
            return t

        def ln(s, b, eps=1e-5):
            w = [s.done, s.x_t[b]]
            st, mv, rs = s.sm[:, 0:6], s.sm[:, 6:8], s.sm[:, 8:9]
            t = V(w, ve.bn_stats, st, x[:, b, :])
            t = V(t, ve.bn_aggr, mv, st)
            t = V(t, ve.tensor_scalar, rs, mv[:, 1:2], eps, None, ALU.add)
            t = P([t, t_const], pe_.tensor_tensor, rs, rs, neghalf[:, 0:1], ALU.pow)
            return V([t, w], ve.tensor_scalar, s.xn[:, :], x[:, b, :], mv[:, 0:1], rs, ALU.subtract, ALU.mult)

        def xpose(s, t_in, j=0):
            for k in range(2):
                t = T([t_in, s.bf[j], t_const], te.transpose, s.bk[j][:, k * 128:(k + 1) * 128],
                      s.xn[:, k * 128:(k + 1) * 128], ident, inc=(k == 1))
            t = S([t, s.done], se.copy, s.xT[:, :, :], s.bk[j][:, 0:256].rearrange("p (k n) -> p k n", k=2))
            s.bf[j] = t
            return t

        def add_x(s, b, src, waits):
            return V(waits, ve.tensor_tensor, x[:, b, :], x[:, b, :], src, ALU.add)

        def small_init(s, L):
            H, SW, hd = (32, 32, 8) if L == 0 else (16, 64, 16)
            d = Slot()
            d.qp = s.ar[:, 0:1024].bitcast(F16).rearrange("p (a h e) -> p a h e", a=2, h=H)
            t = V(s.done, ve.memset, s.ar[:, 0:1024], 0.0)
            if L == 0:
                t = V(t, ve.memset, d.qp[:, 1, :, 24:25], 1.0)
                vt = s.ar[:, 4096:4096 + 288].bitcast(F16).rearrange("p (a h e) -> p a h e", a=2, e=9)
                t = V(s.done, ve.memset, s.ar[:, 4096:4096 + 288], 0.0)
                t = V(t, ve.memset, vt[:, 0, :, 8:9], 1.0)
            else:
                for c in range(2):
                    t = V([t, t_const], ve.tensor_scalar, d.qp[:, 1, :, 48 + c:49 + c], ones_sq[:, 0:16].unsqueeze(2),
                          cst[:, C_MM + c:C_MM + c + 1], None, ALU.mult)
                t = V([t, s.done], ve.memset, s.ar[:, 4096:4640], 0.0)
                vt = s.ar[:, 4096:4640].bitcast(F16).rearrange("p (a h e) -> p a h e", a=2, e=34)
                for c in range(2):
                    t = V(t, ve.tensor_scalar, vt[:, 0, :, 17 * c + 16:17 * c + 17], ones_sq[:, 0:16].unsqueeze(2),
                          cst[:, C_MM + c:C_MM + c + 1], None, ALU.mult)
                t = V(t, ve.memset, s.ar[:, 2048:2304], 0.0)
            s.done = t
            s.PQ = area[0][:, 4096 + 1024 * s.i:5120 + 1024 * s.i].bitcast(F16).rearrange("p (x a n) -> p x a n", x=2, a=2)
            return
            yield

        def small_attn(s, b, L):
            w = W[0 if L == 0 else 4]
            H, SW, hd, R, E = (32, 32, 8, 4, 9) if L == 0 else (16, 64, 16, 2, 34)
            scale = 1.0 / math.sqrt(hd)
            bk = s.bk
            cx = ctxT[:, b * 128:(b + 1) * 128]
            qp = s.ar[:, 0:1024].bitcast(F16).rearrange("p (a h e) -> p a h e", a=2, h=H)
            qpf = s.ar[:, 0:1024].bitcast(F16).rearrange("p (a n) -> p a n", a=2)
            cm = s.ar[:, 2048:2176]
            cd = s.ar[:, 2176:2304]
            if L == 0:
                y = s.ar[:, 3072:3584]
            else:
                tmp = s.ar[:, 2304:2816]
                y = s.ar[:, 3072:3584]
            qT = s.ar[:, 3072:3584].bitcast(F16).rearrange("p (t n) -> p t n", n=128)
            kT = s.ar[:, 3584:4096].bitcast(F16).rearrange("p (t n) -> p t n", n=128)
            vt = s.ar[:, 4096:4096 + H * E].bitcast(F16).rearrange("p (a h e) -> p a h e", a=2, e=E)
            t_ln = ln(s, b)
            yield
            t_xT = xpose(s, t_ln)
            t_in = [w["t"], t_xT, t_const, t_ctx]
            t_xb = P([t_ln, w["t"]], pe_.tensor_tensor, x[:, b, :], x[:, b, :], w["bo"], ALU.add)
            yield
            q0 = bk[0][:, 0:256]
            T([t_in, s.bf[0]], te.matmul, q0, s.xT[:, 0], w["wq"][:, 0], start=True, stop=False, inc=0)
            if L == 0:
                T(None, te.matmul, q0, s.xT[:, 1], w["wq"][:, 1], start=False, stop=True, inc=0)
                T(None, te.matmul, bk[0][:, 256:512], cx, w["wkv"][:, 0:256], start=True, stop=True, inc=0)
                t_p = T(s.bf[1], te.matmul, bk[1][:, 0:256], cx, w["wkv"][:, 256:512], start=True, stop=True)
                yield
                src = bk[0][:, :].rearrange("p (h f two) -> p h f two", f=4, two=2)
                co = bc(cs[:, 0, 4 * b:4 * b + 4], 1, [128, 64, 4])
                si = bc(cs[:, 1, 4 * b:4 * b + 4], 1, [128, 64, 4])
                tt = [sl.rearrange("p (h f) -> p h f", f=4) for sl in
                      (s.ar[:, 3584:3840], s.ar[:, 3840:4096], s.xn[:, :], s.ar[:, 4384:4640])]
                V([t_p, t_cs, s.done], ve.tensor_tensor, tt[0], src[:, :, :, 0], co, ALU.mult)
                V(None, ve.tensor_tensor, tt[1], src[:, :, :, 1], si, ALU.mult)
                V(None, ve.tensor_tensor, tt[2], src[:, :, :, 0], si, ALU.mult)
                t1 = V(None, ve.tensor_tensor, tt[3], src[:, :, :, 1], co, ALU.mult)
                s.bf[0] = t1
                y8 = y.rearrange("p (h f two) -> p h f two", f=4, two=2)
                V(t1, ve.tensor_tensor, y8[:, :, :, 0], tt[0], tt[1], ALU.subtract)
                t_y = V(None, ve.tensor_tensor, y8[:, :, :, 1], tt[2], tt[3], ALU.add)
                v0 = bk[1][:, 0:256].rearrange("p (h e) -> p h e", e=8)
                t_v = S([t_p, s.done], se.copy, vt[:, 0, :, 0:8], v0)
                t_v = V(t_v, ve.tensor_tensor, vt[:, 1, :, 0:8], v0, vt[:, 0, :, 0:8], ALU.subtract)
                s.bf[1] = t_v
            else:
                P([t_ctx, s.done], pe_.tensor_copy, cm[:, 0:112], cx[:, 0:112])
                t_cm = P(None, pe_.tensor_copy, cd[:, 112:128], cx[:, 112:128])
                T(None, te.matmul, q0, s.xT[:, 1], w["wq"][:, 1], start=False, stop=True, inc=0)
                for dst, wm, wd, wt in ((bk[0][:, 256:512], w["wk"], w["wd"][:, 0:256], None),
                                        (bk[1][:, 0:256], w["wv"], w["wd"][:, 256:512], s.bf[1])):
                    T([t_cm, wt], te.matmul, dst, cm, wm, start=True, stop=False, inc=0)
                    t_p = T(None, te.matmul, dst, cd, wd, start=False, stop=True)
                yield
                src = bk[0][:, :].rearrange("p (h e) -> p h e", e=16)
                y3 = y.rearrange("p (h e) -> p h e", e=16)
                sq = tmp.rearrange("p (h e) -> p h e", e=16)
                mu = s.sm[:, 64:96]
                va = s.sm[:, 96:128]
                t1 = s.bf[0] = V([t_p, s.done], ve.tensor_tensor, y, bk[0][:, :], w["bqk"], ALU.add)
                t_vb = s.bf[1] = V(t_p, ve.tensor_tensor, s.xn[:, :], bk[1][:, 0:256], w["bv"], ALU.add)
                t1 = V(t1, ve.tensor_reduce, mu, y3, AX.X, ALU.add)
                t1 = V(t1, ve.tensor_scalar, mu, mu, 1.0 / 16, None, ALU.mult)
                t1 = V(t1, ve.tensor_tensor, y3, y3, bc(mu, 2, [128, 32, 16]), ALU.subtract)
                t2 = S(t1, se.activation, sq, y3, ACT.Square)
                vs = s.xn[:, :].rearrange("p (h e) -> p h e", e=16)
                for c in range(2):
                    m = cst[:, C_MM + c:C_MM + c + 1]
                    vh = vt[:, 0, :, 17 * c:17 * c + 16]
                    t_v = V([t_vb, s.done], ve.tensor_scalar, vh, vs, m, None, ALU.mult)
                    t_v = V(t_v, ve.scalar_tensor_tensor, vt[:, 1, :, 17 * c:17 * c + 16], vs, m, vh, ALU.mult, ALU.subtract)
                yield
                t2 = V(t2, ve.tensor_reduce, va, sq, AX.X, ALU.add)
                t2 = V(t2, ve.tensor_scalar, va, va, 1.0 / 16, 1e-6, ALU.mult, ALU.add)
                t2 = P(t2, pe_.tensor_tensor, va, va, neghalf[:, 0:32], ALU.pow)
                yield
                t2 = V(t2, ve.tensor_tensor, y3, y3, bc(va, 2, [128, 32, 16]), ALU.mult)
                y4 = y.rearrange("p (a h e) -> p a h e", a=2, h=16)
                for a in range(2):
                    t3 = V([t2, w["t"]], ve.tensor_tensor, y4[:, a], y4[:, a],
                           bc(w["nw"][:, 0, a], 1, [128, 16, 16]), ALU.mult)
                for a in range(2):
                    t_y = V(t3, ve.tensor_tensor, y4[:, a], y4[:, a],
                            bc(w["nw"][:, 1, a], 1, [128, 16, 16]), ALU.add)
            y4 = y.rearrange("p (a h e) -> p a h e", a=2, h=H)
            qpa = s.ar[:, 0:1024].bitcast(F16).rearrange("p (ah e) -> p ah e", e=SW)
            t_h = S([t_y, s.done], se.copy, qpa[:, :, 0:hd], y.rearrange("p (ah e) -> p ah e", e=hd))
            V([t_h, s.done], ve.tensor_tensor, qp[:, 0, :, hd:2 * hd], y4[:, 0], qp[:, 0, :, 0:hd], ALU.subtract)
            t_q1 = V(None, ve.tensor_tensor, qp[:, 1, :, 2 * hd:3 * hd], y4[:, 1], qp[:, 1, :, 0:hd], ALU.subtract)
            nmx = 1 if L == 0 else 2
            V([t_h, s.done], ve.tensor_copy, qp[:, 0, :, 2 * hd:3 * hd], qp[:, 0, :, 0:hd])
            V(None, ve.tensor_copy, qp[:, 1, :, hd:2 * hd], qp[:, 1, :, 0:hd])
            t_q2 = V(None, ve.memset, qp[:, 0, :, 3 * hd:3 * hd + nmx], 0.0)
            yield
            bh = [bk[j][:, :].bitcast(F16) for j in range(2)]
            for j in range(2):
                for t_ in range(8):
                    t = T([t_q1, t_q2, s.bf[j]], te.transpose, bh[j][:, t_ * 128:(t_ + 1) * 128],
                          qpf[:, j, t_ * 128:(t_ + 1) * 128], idh[:, :], inc=(t_ == 7))
                if j == 0:
                    t_qe = s.bf[0] = S([t, t_q1], se.copy, qT, bh[0].rearrange("p (t n) -> p t n", n=128))
                else:
                    t_ke = s.bf[1] = V([t, t_q1], ve.tensor_copy, kT, bh[1].rearrange("p (t n) -> p t n", n=128))
            yield
            ng = H // 4
            qph = qp[:, 0].rearrange("p (t i) e -> p t i e", i=R)
            for g in range(ng):
                j = g % 2
                i = g // 2
                r = slice(SW * i, SW * i + SW)
                for c in range(4):
                    t_ = 4 * j + c
                    t = T([t_qe, t_ke, s.bf[j]], te.matmul, bk[j][:, c * 128:(c + 1) * 128], qT[r, t_, :],
                          kT[r, t_, :], start=True, stop=True, inc=(c == 3))
                bv = bk[j][:, :].rearrange("p (h n) -> p h n", h=4)
                o = qph[:, 4 * j:4 * j + 4, i, 3 * hd:3 * hd + nmx]
                if L == 0:
                    t_m = V([t, t_q2], ve.tensor_reduce, o, bv, AX.X, ALU.max, negate=True)
                else:
                    V([t, t_q2], ve.tensor_reduce, o[:, :, 0:1], bv[:, :, 0:112], AX.X, ALU.max, negate=True)
                    t_m = V(None, ve.tensor_reduce, o[:, :, 1:2], bv[:, :, 112:128], AX.X, ALU.max, negate=True)
                s.bf[j] = t_m
                if g % 2:
                    yield
            t_s = t
            for t_ in range(8):
                t = T([t_m, s.bf[0]], te.transpose, bh[0][:, t_ * 128:(t_ + 1) * 128],
                      qpf[:, 0, t_ * 128:(t_ + 1) * 128], idh[:, :], inc=(t_ == 7))
            t_qe = s.bf[0] = S([t, t_s], se.copy, qT, bh[0].rearrange("p (t n) -> p t n", n=128))
            yield
            Pm = s.ar[:, 1024:2048].rearrange("p (x n) -> p x n", x=2)
            Pq = s.PQ
            O = s.xn[:, :].rearrange("p (h e) -> p h e", h=H)
            rec = s.sm[:, 16:48]
            t_o = None
            t_l = [None, None]
            t_pp = [s.done, s.done]

            def scores(g):
                r = slice(SW * (g // 2), SW * (g // 2) + SW)
                for c in range(4):
                    t_ = 4 * (g % 2) + c
                    t = T([t_qe, s.bf[0]], te.matmul, bk[0][:, c * 128:(c + 1) * 128], kT[r, t_, :],
                          qT[r, t_, :], start=True, stop=True, inc=(c == 3))
                return t

            t_sc = scores(0)
            for g in range(ng):
                xx = g % 2
                i = g // 2
                S([t_sc, t_pp[xx], t_y], se.activation, Pm[:, xx], bk[0][:, :], ACT.Exp, scale=scale)
                t_hi = s.bf[0] = S([t_l[xx], s.done], se.activation, Pq[:, xx, 0], bk[0][:, :], ACT.Exp, scale=scale)
                f, g_ = (V, ve) if L == 0 or g % 2 else (P, pe_)
                t_pp[xx] = f([t_hi, t_l[xx]], g_.tensor_tensor, Pq[:, xx, 1], Pm[:, xx], Pq[:, xx, 0], ALU.subtract)
                yield
                if g < ng - 1:
                    t_sc = scores(g + 1)
                for c in range(4):
                    h = (4 * xx + c) * R + i
                    o = bk[1][:, (h if L == 0 else 4 * xx + c) * E:][:, 0:E]
                    ph = Pq[:, xx, 0, c * 128:(c + 1) * 128]
                    pl = Pq[:, xx, 1, c * 128:(c + 1) * 128]
                    T([t_hi, t_v, s.bf[1]], te.matmul, o, ph, vt[:, 0, h, :], start=True, stop=False, inc=0)
                    T(None, te.matmul, o, ph, vt[:, 1, h, :], start=False, stop=False, inc=0)
                    t = T(t_pp[xx], te.matmul, o, pl, vt[:, 0, h, :], start=False, stop=True, inc=(c == 3))
                t_l[xx] = t
                if L == 0 and g == 7:
                    ov = bk[1][:, 0:288].rearrange("p (h e) -> p h e", e=E)
                    t1 = V([t, t_q1], ve.reciprocal, rec[:, 0:32].unsqueeze(2), ov[:, :, 8:9])
                    t_o = s.bf[1] = V(t1, ve.tensor_tensor, O, ov[:, :, 0:8], bc(rec[:, 0:32], 2, [128, 32, 8]), ALU.mult)
                    yield
                if L == 2 and g % 2:
                    ov = bk[1][:, 0:8 * E].rearrange("p (h e) -> p h e", e=E)
                    Oi = O.rearrange("p (t i) e -> p t i e", i=R)[:, :, i]
                    tA = tmp[:, 0:128].rearrange("p (h e) -> p h e", e=16)
                    V([t, t_o], ve.reciprocal, rec[:, 0:8].unsqueeze(2), ov[:, :, 16:17])
                    t1 = V(None, ve.reciprocal, rec[:, 8:16].unsqueeze(2), ov[:, :, 33:34])
                    V(t1, ve.tensor_tensor, Oi, ov[:, :, 0:16], bc(rec[:, 0:8], 2, [128, 8, 16]), ALU.mult)
                    t2 = V(None, ve.tensor_tensor, tA, ov[:, :, 17:33], bc(rec[:, 8:16], 2, [128, 8, 16]), ALU.mult)
                    t_o = s.bf[1] = V(t2, ve.tensor_tensor, Oi, Oi, tA, ALU.add)
                    yield
            for k in range(2):
                t = T([t_o, s.bf[0]], te.transpose, bk[0][:, k * 128:(k + 1) * 128], s.xn[:, k * 128:(k + 1) * 128], ident,
                      inc=(k == 1))
            OT = s.xT
            t = S([t, t_o], se.copy, OT[:, :, :], bk[0][:, 0:256].rearrange("p (k n) -> p k n", k=2))
            s.bf[0] = t
            yield
            T([t, s.bf[1]], te.matmul, bk[1][:, 0:256], OT[:, 0], w["wo"][:, 0], start=True, stop=False, inc=0)
            t = T(None, te.matmul, bk[1][:, 0:256], OT[:, 1], w["wo"][:, 1], start=False, stop=True)
            t = add_x(s, b, bk[1][:, 0:256], [t, t_xb])
            s.bf[1] = t
            s.done = [t, t_pp]
            s.x_t[b] = t
            yield

        def big_attn(s, b, L):
            w = W[2 if L == 1 else 6]
            kv = 2 if L == 1 else 4
            scale = 1.0 / math.sqrt(128.0)
            bk = s.bk
            cx = ctxT[:, b * 128:(b + 1) * 128]
            t_ln = ln(s, b)
            yield
            t_xT = xpose(s, t_ln)
            yield
            qn = s.ar[:, 0:512]
            kn = s.ar[:, 512:1024]
            sq = s.ar[:, 3584:4608]
            Pm = s.ar[:, 0:512].rearrange("p (h n) -> p h n", n=128)
            PT = s.ar[:, 512:1024].rearrange("p (h n) -> p h n", n=128)
            qT = s.ar[:, 1024:1536].rearrange("p (h n) -> p h n", n=128)
            kT = [s.ar[:, 1536 + 128 * kv * i:1536 + 128 * kv * (i + 1)].rearrange("p (h n) -> p h n", n=128)
                  for i in range(4 // kv)]
            va = [s.ar[:, 2048 + 128 * kv * i:2048 + 128 * kv * (i + 1)].rearrange("p (h n) -> p h n", n=128)
                  for i in range(4 // kv)]
            OT = [s.ar[:, 2560 + 512 * i:3072 + 512 * i].rearrange("p (h n) -> p h n", n=128) for i in range(2)]
            mrow = s.xn[0:1, 0:64].bitcast(F16)
            ms = s.sm[:, 16:24]
            nm = s.sm[:, 24:28]
            rec = s.sm[:, 28:32]
            nb = s.sm[:, 32:36]
            den = s.sm[:, 36:40]
            rq = s.sm[:, 40:44]
            deps = [w["t"], t_xT, t_const, t_ctx]
            b0 = bk[0][:, :].rearrange("p (h n) -> p h n", h=4)
            b1 = bk[1][:, :].rearrange("p (h n) -> p h n", h=4)
            t0 = [s.done, t_xT]
            rd = [t0, t0]
            t_ot = [None, None]

            def out(c):
                for h in range(4):
                    t = T([t_ot[c % 2], s.bf[1]], te.matmul, bk[1][:, 0:256], OT[c % 2][:, h], w["wo"][:, 4 * c + h],
                          start=(h == 0), stop=(h == 3), inc=(h == 3))
                t_ot[c % 2] = t
                return t

            def q1(c):
                for h in range(4):
                    for k in range(2):
                        t = T([deps, s.bf[0]], te.matmul, bk[0][:, h * 128:(h + 1) * 128],
                              w["wq"][:, k, (4 * c + h) * 128:(4 * c + h + 1) * 128], s.xT[:, k, :],
                              start=(k == 0), stop=(k == 1), inc=(k == 1 and h == 3))
                s.bf[0] = S([t, t0], se.activation, qT, b0, ACT.Copy, scale=scale)
                return s.bf[0]

            def kv1(c):
                for h in range(2):
                    T([deps, s.bf[1]], te.matmul, bk[1][:, h * 128:(h + 1) * 128],
                      w["wk"][:, (2 * c + h) * 128:(2 * c + h + 1) * 128], cx, start=True, stop=True, inc=0)
                t = T(None, te.matmul, bk[1][:, 256:512], cx, w["wv"][:, c * 256:(c + 1) * 256], start=True, stop=True)
                V([t, rd[c % 2]], ve.tensor_copy, kT[c % 2], b1[:, 0:2])
                s.bf[1] = V([t, rd[c % 2]], ve.tensor_scalar, va[c % 2], b1[:, 2:4], mk, None, ALU.mult)
                return s.bf[1]

            def q3(c, waits):
                for k in range(2):
                    t = T([deps, s.bf[0]], te.matmul, bk[0][:, :], s.xT[:, k, :],
                          w["wq"][:, k, c * 512:(c + 1) * 512], start=(k == 0), stop=(k == 1), inc=(k == 1))
                S([t, waits], se.activation, sq[:, 0:512], bk[0][:, :], ACT.Square)
                s.bf[0] = S(None, se.copy, qn, bk[0][:, :])
                return s.bf[0]

            if L == 3:
                t_q = q3(0, t0)
            if L == 1:
                t = T([s.bf[1], t_const], te.transpose, bk[1][0:1, 0:128], mbias[:, b:b + 1], ident)
                t_mr = V([t, t0, t_ln], ve.tensor_scalar, mrow, bk[1][0:1, 0:128], -30000.0, None, ALU.max)
                s.bf[1] = t_mr
                mk = mkey[:, b:b + 1]
                t_q = q1(0)
                t_kv = kv1(0)
                yield
            for c in range(4):
                kc, vc = (kT[c % 2], va[c % 2]) if L == 1 else (kT[0], va[0])
                t_b = rd[(c + 1) % 2]
                if L == 3:
                    t1 = T([deps, s.bf[1]], te.matmul, bk[1][:, :], cx, w["wk"][:, c * 512:(c + 1) * 512], start=True, stop=True)
                    yield
                    tb = S([t1, t_q], se.activation, sq[:, 512:1024], bk[1][:, :], ACT.Square)
                    t3 = V([tb, t_b], ve.tensor_reduce, ms, sq.rearrange("p (h n) -> p h n", h=8), AX.X, ALU.add)
                    t3 = V(t3, ve.tensor_scalar, ms, ms, 1.0 / 128, 1e-5, ALU.mult, ALU.add)
                    t3 = P(t3, pe_.tensor_tensor, ms, ms, neghalf[:, 0:8], ALU.pow)
                    yield
                    for h in range(4):
                        t = T([t_q, s.bf[0]], te.transpose, b0[:, h], qn[:, h * 128:(h + 1) * 128], ident, inc=(h == 3))
                    t_q = s.bf[0] = S(t, se.copy, qT, b0)
                    t_kn = s.bf[1] = V([t3, t_b], ve.tensor_tensor, kn.rearrange("p (h n) -> p h n", h=4), b1,
                                       bc(ms[:, 4:8], 2, [128, 4, 128]), ALU.mult)
                    t_rq = V(t3, ve.tensor_scalar, rq, ms[:, 0:4], scale, None, ALU.mult)
                    yield
                    for h in range(4):
                        t1 = T([t_kn, s.bf[1]], te.transpose, b1[:, h], kn[:, h * 128:(h + 1) * 128], ident, inc=(h == 3))
                    t_kv = s.bf[1] = V([t1, t_gp], ve.tensor_scalar, kc, b1, gp[:, 0:1], None, ALU.mult)
                    yield
                if L == 1:
                    T([t_mr, s.bf[0]], te.matmul, bk[0][:, :], idh[0:1, 0:1].to_broadcast([1, 128]),
                      bc(mrow, 1, [1, 4, 128]), start=True, stop=False, inc=0)
                for h in range(4):
                    kh = h // 2 if L == 1 else h
                    t = T([t_q, t_kv, s.bf[0]], te.matmul, b0[:, h], qT[:, h], kc[:, kh],
                          start=(L == 3), stop=(L == 3 or h == 3), inc=(h == 3))
                t_m = V([t, t0], ve.tensor_reduce, nm, b0, AX.X, ALU.max, negate=True)
                if L == 3:
                    t_m = V([t_m, t_rq], ve.tensor_tensor, nb, nm, rq, ALU.mult)
                s.bf[0] = t_m
                yield
                if c > 0:
                    t = out(c - 1)
                    s.bf[1] = add_x(s, b, bk[1][:, 0:256], [t, s.bf[1]])
                if L == 1 and c < 3:
                    t_kv = kv1(c + 1)
                if L == 3:
                    t2 = T(s.bf[1], te.matmul, bk[1][:, :], cx, w["wv"][:, c * 512:(c + 1) * 512], start=True, stop=True)
                for h in range(4):
                    t = S([t_m, t_b], se.activation, Pm[:, h], b0[:, h], ACT.Exp, accum_out=den[:, h:h + 1],
                          bias=(nm if L == 1 else nb)[:, h:h + 1], **({} if L == 1 else {"scale": rq[:, h:h + 1]}))
                s.bf[0] = t
                if L == 3:
                    s.bf[1] = t_v = S([t2, t_b], se.copy, vc, b1)
                else:
                    t_v = None
                t1 = V(t, ve.reciprocal, rec, den)
                t_p = V(t1, ve.tensor_tensor, Pm, Pm, bc(rec, 2, [128, 4, 128]), ALU.mult)
                yield
                for h in range(4):
                    t = T([t_p, s.bf[0]], te.transpose, b0[:, h], Pm[:, h], ident, inc=(h == 3))
                t_pt = s.bf[0] = S([t, t_b], se.copy, PT, b0)
                yield
                if L == 1 and c < 3:
                    t_q = q1(c + 1)
                if L == 3 and c < 3:
                    t_q = q3(c + 1, t_p)
                if L == 1:
                    for h in range(2):
                        t = T([t_pt, s.bf[1]], te.matmul, bk[1][:, h * 256:(h + 1) * 256], vc[:, h],
                              s.ar[:, 512 + 256 * h:768 + 256 * h], start=True, stop=True, inc=(h == 1))
                else:
                    for h in range(4):
                        t = T([t_pt, t_v, s.bf[1]], te.matmul, b1[:, h], vc[:, h], PT[:, h], start=True, stop=True,
                              inc=(h == 3))
                rd[c % 2] = t
                t_ot[c % 2] = s.bf[1] = V([t, t_ot[c % 2], t0], ve.tensor_copy, OT[c % 2], b1)
                yield
            t = out(3)
            t = s.bf[1] = add_x(s, b, bk[1][:, 0:256], [t, s.bf[1]])
            s.done = t
            s.x_t[b] = t
            yield

        def peer(s, b):
            w = W[1]
            bk = s.bk
            t_ln = ln(s, b)
            yield
            t_xT = xpose(s, t_ln)
            yield
            G = s.ar[:, 0:2048].rearrange("p (e n) -> p e n", n=128)
            wk_ = s.ar[:, 2048:4608]
            B = wk_[:, 0:1024].bitcast(F16).rearrange("p (x g n) -> p x g n", x=2, n=128)
            Am = wk_[:, 1024:2048].bitcast(F16).rearrange("p (x a g n) -> p x a g n", x=2, a=2, n=64)
            oh = wk_[:, 2048:2560].bitcast(F16).rearrange("p (x g n) -> p x g n", x=2, n=64)
            sims = wk_[:, 0:1024].rearrange("p (a h n) -> p a h n", a=2, h=4)
            qT = wk_[:, 1024:1536].rearrange("p (h n) -> p h n", n=128)
            al = wk_[:, 1536:1792]
            e1 = wk_[:, 1792:2048]
            m0 = 2048
            s8 = wk_[:, m0:m0 + 64].rearrange("p (a h k) -> p a h k", a=2, h=4)
            i8 = wk_[:, m0 + 64:m0 + 128].bitcast(U32)
            i8f = wk_[:, m0 + 128:m0 + 192]
            f8 = wk_[:, m0 + 192:m0 + 224].rearrange("p (h k) -> p h k", h=4)
            pk = wk_[:, m0 + 224:m0 + 256].bitcast(U32)
            pk2 = wk_[:, m0 + 256:m0 + 320].bitcast(U32)
            pkf = wk_[:, m0 + 320:m0 + 384]
            isel = wk_[:, m0 + 384:m0 + 448]
            idx = wk_[:, m0 + 448:m0 + 480]
            iu = wk_[:, m0 + 480:m0 + 512].bitcast(U32)
            iv = wk_[:, 1024:1088].bitcast(U32)
            wh = wk_[:, 1088:1184]
            tr = wk_[:, 1184:1280]
            rest = wk_[:, 1280:1312]
            trh = s.ar[:, 4608:4672].bitcast(F16)
            t_b = [s.done, t_xT]
            for h in range(4):
                for k in range(2):
                    t = T([w["t"], t_xT, s.bf[0]], te.matmul, bk[0][:, h * 128:(h + 1) * 128], w["wq"][:, k, h * 128:(h + 1) * 128],
                          s.xT[:, k, :], start=(k == 0), stop=(k == 1), inc=(h == 3 and k == 1))
            t = s.bf[0] = S([t, t_b], se.copy, qT, bk[0][:, :].rearrange("p (h n) -> p h n", h=4))
            yield
            for a in range(2):
                for h in range(4):
                    tt = T([t, s.bf[a]], te.matmul, bk[a][:, h * 128:(h + 1) * 128],
                           qT[64 * a:64 * a + 64, h, :], w["keys"][64 * a:64 * a + 64, h, :],
                           start=True, stop=True, inc=(h == 3))
                ts_ = s.bf[a] = S([tt, t_b], se.copy, sims[:, a], bk[a][:, :].rearrange("p (h n) -> p h n", h=4))
            yield
            for a in range(2):
                for h in range(4):
                    t = V([ts_, t_b], ve.max, s8[:, a, h], sims[:, a, h])
            for a in range(2):
                for h in range(4):
                    t2 = V(t, ve.max_index, i8[:, (a * 4 + h) * 8:(a * 4 + h + 1) * 8], s8[:, a, h], sims[:, a, h])
            for j in range(4):
                for e in range(4):
                    for k in range(2):
                        tg = T([s.bf[j % 2]], te.matmul, bk[j % 2][:, e * 128:(e + 1) * 128],
                               w["ed"][:, k, (4 * j + e) * 128:(4 * j + e + 1) * 128], s.xT[:, k, :],
                               start=(k == 0), stop=(k == 1), inc=(k == 1 and e == 3))
                t_g = s.bf[j % 2] = S([tg, t_b], se.activation, G[:, 4 * j:4 * j + 4, :],
                                      bk[j % 2][:, :].rearrange("p (e n) -> p e n", e=4), ACT.Silu)
                if j % 2:
                    yield
            al4 = al.rearrange("p (h i j) -> p h i j", h=4, i=8)
            t = V(t, ve.tensor_tensor, al4, bc(s8[:, 0], 3, [128, 4, 8, 8]), bc(s8[:, 1], 2, [128, 4, 8, 8]), ALU.add)
            t2 = V(t2, ve.tensor_copy, i8f, i8)
            for h in range(4):
                t3 = V(t, ve.max, f8[:, h], al[:, h * 64:(h + 1) * 64])
            for h in range(4):
                t3_ = V(t3, ve.max_index, pk[:, h * 8:(h + 1) * 8], f8[:, h], al[:, h * 64:(h + 1) * 64])
            V(t3_, ve.tensor_scalar, pk2[:, 0:32], pk, 3, None, ALU.logical_shift_right)
            t4 = V(t3_, ve.tensor_scalar, pk2[:, 32:64], pk, 7, None, ALU.bitwise_and)
            t4 = V(t4, ve.tensor_copy, pkf, pk2)
            yield
            t5 = None
            for a in range(2):
                e2 = e1.rearrange("p (m j) -> p m j", j=8)
                t5 = V([t4, t5], ve.tensor_tensor, e2, bc(iota8, 1, [128, 32, 8]),
                       bc(pkf[:, 32 * a:32 * a + 32], 2, [128, 32, 8]), ALU.is_equal)
                e4 = e1.rearrange("p (h k j) -> p h k j", h=4, k=8)
                iv4 = i8f[:, 32 * a:32 * a + 32].rearrange("p (h j) -> p h j", h=4)
                t5 = V([t5, t2], ve.tensor_tensor, e4, e4, bc(iv4, 2, [128, 4, 8, 8]), ALU.mult)
                t5 = V(t5, ve.tensor_reduce, isel[:, 32 * a:32 * a + 32], e2, AX.X, ALU.add)
            t5 = V(t5, ve.scalar_tensor_tensor, idx, isel[:, 0:32], 128.0, isel[:, 32:64], ALU.mult, ALU.add)
            t5 = V(t5, ve.tensor_scalar, idx, idx, 2047.0, None, ALU.min)
            t5 = V(t5, ve.tensor_copy, iu, idx)
            V(t5, ve.tensor_scalar, iv[:, 0:32], iu, 7, None, ALU.logical_shift_right)
            t5 = V(None, ve.tensor_scalar, iv[:, 32:64], iu, 127, None, ALU.bitwise_and)
            t5 = V(t5, ve.tensor_copy, wh[:, 0:64], iv)
            t5 = V(t5, ve.tensor_scalar, wh[:, 64:96], f8.rearrange("p h k -> p (h k)"), 0.0, None, ALU.max)
            for q in range(3):
                t6 = V(t5, ve.transpose, tr[:, 32 * q:32 * q + 32], wh[:, 32 * q:32 * q + 32])
            V(t6, ve.tensor_scalar, trh[:, 0:32], tr[:, 0:32], cst[:, C_PC:C_PC + 1], None, ALU.add)
            t7 = V(None, ve.tensor_copy, trh[:, 32:96], tr[:, 32:96])
            t7 = V(t7, ve.tensor_tensor, rest, tr[:, 64:96], trh[:, 64:96], ALU.subtract)
            t7 = V(t7, ve.tensor_copy, trh[:, 96:128], rest)
            yield
            rd = [t7, t7]
            for j in range(4):
                xx = j % 2
                g8 = slice(8 * j, 8 * j + 8)
                t8 = V([t7, rd[xx]], ve.tensor_tensor, B[:, xx], bc(i128h[:, :], 1, [128, 8, 128]),
                       bc(trh[:, 32:64][:, g8], 2, [128, 8, 128]), ALU.is_equal)
                t9 = V([t7, rd[xx]], ve.tensor_tensor, oh[:, xx], bc(i64h[:, :], 1, [128, 8, 64]),
                       bc(trh[:, 0:32][:, g8], 2, [128, 8, 64]), ALU.is_equal)
                for a in range(2):
                    t10 = P(t9, pe_.tensor_tensor, Am[:, xx, a], oh[:, xx],
                            bc(trh[:, 64 + 32 * a:96 + 32 * a][:, g8], 2, [128, 8, 64]), ALU.mult)
                yield
                for g in range(8):
                    for a in range(2):
                        t = T([t8, t10, s.bf[xx]], te.matmul, bk[xx][:, g * 64:(g + 1) * 64], B[:, xx, g, :], Am[:, xx, a, g, :],
                              start=(a == 0), stop=(a == 1), inc=(g == 7 and a == 1))
                rd[xx] = [t, t10]
                src = bk[xx][:, :].rearrange("p (g c e) -> p e c g", g=8, c=4)
                dst = G.rearrange("p e (c g) -> p e c g", c=4)[:, :, :, g8]
                t_gm = s.bf[xx] = V([t, t_g], ve.tensor_tensor, dst, dst, src, ALU.mult)
            yield
            for e in range(16):
                t = T([t_gm, s.bf[0]], te.matmul, bk[0][:, 0:256], G[:, e, :], w["eu"][:, e, :],
                      start=(e == 0), stop=(e == 15), inc=(e == 15))
            t = s.bf[0] = add_x(s, b, bk[0][:, 0:256], t)
            s.done = [t, t10]
            s.x_t[b] = t
            yield

        def moe(s, b):
            w = W[3]
            bk = s.bk
            t_ln = ln(s, b)
            yield
            t_xT = xpose(s, t_ln)
            yield
            pr = s.sm[:, 16:24]
            bg = s.sm[:, 24:32]
            s8 = s.sm[:, 32:40]
            i8 = s.sm[:, 40:48].bitcast(U32)
            i8f = s.sm[:, 48:56]
            sel = s.sm[:, 56:72]
            mk = s.sm[:, 72:80]
            mm = s.sm[:, 80:82]
            pT = s.ar[0:8, 0:128]
            acc = s.ar[:, 128:384]
            uT = [s.ar[:, 384 + 256 * i:640 + 256 * i].rearrange("p (k n) -> p k n", k=2) for i in range(2)]
            gT = [s.ar[:, 896 + 256 * i:1152 + 256 * i].rearrange("p (k n) -> p k n", k=2) for i in range(2)]
            t_b = [s.done, t_xT]
            for o, extra in ((0, False), (8, True)):
                r = bk[1][:, o:o + 7]
                T([w["t"], ts, t_xT, s.bf[1], t_const], te.matmul, r, s.xT[:, 0], wr[:, 0], start=True, stop=False, inc=0)
                T(None, te.matmul, r, s.xT[:, 1], wr[:, 1], start=False, stop=False, inc=0)
                t = T(None, te.matmul, r, ones_row, rb[0:1, 0:7], start=False, stop=not extra)
                if extra:
                    t = T(None, te.matmul, r, ones_row, rb[0:1, 8:15], start=False, stop=True)
            t1 = V(t_b, ve.memset, bg, -3e38)
            t1 = V([t, t1], ve.tensor_copy, bg[:, 0:7], bk[1][:, 8:15])
            t1 = V(t1, ve.max, s8, bg)
            t1 = V(t1, ve.max_index, i8, s8, bg)
            t1 = V(t1, ve.tensor_copy, i8f, i8)
            t2 = V(t1, ve.tensor_scalar, sel[:, 0:8], iota8, i8f[:, 0:1], None, ALU.is_equal)
            t2 = V(t1, ve.tensor_scalar, sel[:, 8:16], iota8, i8f[:, 1:2], None, ALU.is_equal)
            t2 = V(t2, ve.tensor_tensor, sel[:, 0:8], sel[:, 0:8], sel[:, 8:16], ALU.add)
            t2 = V(t2, ve.tensor_scalar, mk, sel[:, 0:8], -1.0, 1e30, ALU.add, ALU.mult)
            t2 = V(t2, ve.tensor_tensor, mk[:, 0:7], mk[:, 0:7], bk[1][:, 0:7], ALU.add)
            s.bf[1] = t2
            t2 = V(t2, ve.tensor_reduce, mm[:, 0:1], mk[:, 0:7], AX.X, ALU.max)
            t2 = V(t2, ve.tensor_scalar, mk[:, 0:7], mk[:, 0:7], mm[:, 0:1], None, ALU.subtract)
            t2 = S(t2, se.activation, mk[:, 0:7], mk[:, 0:7], ACT.Exp)
            yield
            t2 = V(t2, ve.tensor_reduce, mm[:, 1:2], mk[:, 0:7], AX.X, ALU.add)
            t2 = V(t2, ve.reciprocal, mm[:, 1:2], mm[:, 1:2])
            V(None, ve.memset, pr[:, 7:8], 1.0)
            t_p = V(t2, ve.tensor_scalar, pr[:, 0:7], mk[:, 0:7], mm[:, 1:2], None, ALU.mult)
            t = T([t_p, s.bf[0]], te.transpose, bk[0][0:8, 0:128], pr, ident)
            t = s.bf[0] = V([t, t_b], ve.tensor_copy, pT, bk[0][0:8, 0:128])
            yield
            t = T([t, s.bf[1]], te.matmul, bk[1][:, 0:256], pT, bdn[:, :], start=True, stop=True)
            t_acc = s.bf[1] = V([t, t_b], ve.tensor_tensor, acc, x[:, b, :], bk[1][:, 0:256], ALU.add)
            rd_u, rd_g = [None, None], [None, None]
            b0 = bk[0][:, 0:256].rearrange("p (m n) -> p m n", m=2)
            b1 = bk[1][:, 0:256].rearrange("p (m n) -> p m n", m=2)

            def up(e):
                for m in range(2):
                    for k in range(2):
                        t = T([t_xT, s.bf[0]], te.matmul, bk[0][:, m * 128:(m + 1) * 128], w["Wup"][:, e, k, m * 128:(m + 1) * 128],
                              s.xT[:, k, :], start=(k == 0), stop=(k == 1), inc=(k == 1 and m == 1))
                s.bf[0] = V([t, t_b, rd_u[e % 2]], ve.tensor_tensor, uT[e % 2], b0,
                            bc(bu[:, 0, 2 * e:2 * e + 2], 2, [128, 2, 128]), ALU.add)
                return s.bf[0]

            t_u = up(0)
            yield
            for e in range(8):
                i = e % 2
                for m in range(2):
                    for k in range(2):
                        t = T([t_u, s.bf[1]], te.matmul, bk[1][:, m * 128:(m + 1) * 128], w["Wgate"][:, e, k, m * 128:(m + 1) * 128],
                              uT[i][:, k], start=(k == 0), stop=(k == 1), inc=(k == 1 and m == 1))
                for m in range(2):
                    t_s = S([t, t_b, rd_g[i]], se.activation, gT[i][:, m], b1[:, m], ACT.Silu, bias=bu[:, 1, 2 * e + m:2 * e + m + 1])
                s.bf[1] = t_s
                t_g = rd_u[i] = V([t_s, rd_g[i]], ve.tensor_tensor, gT[i], gT[i], uT[i], ALU.mult)
                if e < 7:
                    t_u = up(e + 1)
                yield
                for k in range(2):
                    t = T([t_g, s.bf[1]], te.matmul, bk[1][:, 0:256], gT[i][:, k, :],
                          w["Wdown"][:, e, k, :], start=(k == 0), stop=(k == 1), inc=(k == 1))
                rd_g[i] = t
                dst = acc if e < 7 else x[:, b]
                t_acc = s.bf[1] = V([t, t_acc, t_p], ve.scalar_tensor_tensor, dst, bk[1][:, 0:256],
                                    pr[:, e:e + 1], acc, ALU.mult, ALU.add)
                yield
            s.done = t_acc
            s.x_t[b] = t_acc

        def tern_prep(s):
            w = W[5]
            tmp = w["tmp"]
            sm = s.sm
            t0 = [s.done, w["t"]]
            raw = area[1]
            t = V(t0, ve.tensor_reduce, sm[:, 0:1], raw[:, 0:1364], AX.X, ALU.add, apply_absolute_value=True)
            yield
            t = V(t0, ve.tensor_reduce, sm[:, 1:2], raw[:, 1364:2728], AX.X, ALU.add, apply_absolute_value=True)
            yield
            t = V(t0, ve.tensor_reduce, sm[:, 2:3], raw[:, 2728:2728 + 1280], AX.X, ALU.add, apply_absolute_value=True)
            t = V(t0, ve.tensor_reduce, sm[0:42, 3:4], raw[0:42, 4008:4264], AX.X, ALU.add, apply_absolute_value=True)
            t = V(t, ve.tensor_tensor, sm[0:42, 2:3], sm[0:42, 2:3], sm[0:42, 3:4], ALU.add)
            t = T([t, s.bf[0]], te.matmul, s.bk[0][:, 0:3], ones_sq, sm[:, 0:3], start=True, stop=True)
            t = V(t, ve.tensor_scalar, sm[:, 4:7], s.bk[0][:, 0:3], 1.0 / (682 * 256), None, ALU.mult)
            s.bf[0] = t
            t = V(t, ve.tensor_scalar, sm[:, 8:11], sm[:, 4:7], 0.5, None, ALU.mult)
            t = V(t, ve.tensor_scalar, sm[:, 12:15], sm[:, 4:7], -0.5, None, ALU.mult)
            t = V(t, ve.tensor_scalar, sm[:, 16:19], sm[:, 4:7], -1.0, None, ALU.mult)
            for j, (lo, hi, rows) in enumerate(((0, 1364, 128), (1364, 2728, 128), (2728, 4008, 128), (4008, 4264, 42))):
                q = min(j, 2)
                r = raw[0:rows, lo:hi]
                m = tmp[0:rows, lo:hi]
                t1 = V(t, ve.tensor_scalar, m, r, sm[0:rows, 8 + q:9 + q], None, ALU.is_gt)
                yield
                t2 = V(t1, ve.scalar_tensor_tensor, m, r, sm[0:rows, 12 + q:13 + q], m, ALU.is_lt, ALU.subtract)
                yield
                t2 = V(t2, ve.scalar_tensor_tensor, m, m, sm[0:rows, 16 + q:17 + q], r, ALU.mult, ALU.subtract)
                yield
                t = V(t2, ve.tensor_tensor, r, r, m, ALU.add)
                yield
            w["tq"] = t
            s.done = [s.done, t]

        def tern(s, b):
            w = W[5]
            bk = s.bk
            t_ln = ln(s, b)
            yield
            t_xT = xpose(s, t_ln)
            yield
            a = s.ar[:, 0:512]
            g = s.ar[:, 512:1280].rearrange("p (k n) -> p k n", k=6)
            t_b = [s.done, t_xT]
            for c in range(2):
                nt = 4 if c == 0 else 2
                for q, wm in ((0, w["w1"]), (1, w["w3"])):
                    for m in range(nt):
                        mt = 4 * c + m
                        M = 42 if mt == 5 else 128
                        for k in range(2):
                            t = T([t_xT, w["tq"], s.bf[q]], te.matmul, bk[q][0:M, m * 128:(m + 1) * 128],
                                  wm[:, k, mt * 128:mt * 128 + M], s.xT[:, k, :], start=(k == 0), stop=(k == 1),
                                  inc=(k == 1 and m == nt - 1))
                for lo, hi, M in (((0, 4, 128),) if c == 0 else ((0, 1, 128), (1, 2, 42))):
                    cs_ = slice(lo * 128, hi * 128)
                    t1 = S([t, t_b], se.activation, a[0:M, cs_], bk[0][0:M, cs_], ACT.Silu)
                    t2 = V([t1, t], ve.tensor_tensor, g[0:M, 4 * c + lo:4 * c + hi, :].rearrange("p k n -> p (k n)"),
                           a[0:M, cs_], bk[1][0:M, cs_], ALU.mult)
                s.bf[0], s.bf[1] = t1, t2
                t_b = [t_b, t2]
                yield
            for k in range(6):
                M = 42 if k == 5 else 128
                t = T([t2, s.bf[0]], te.matmul, bk[0][:, 0:256], g[0:M, k, :],
                      w["w2"][0:M, k, :], start=(k == 0), stop=(k == 5), inc=(k == 5))
            t = s.bf[0] = add_x(s, b, bk[0][:, 0:256], t)
            s.done = t
            s.x_t[b] = t
            yield

        def quant(s_, src, dst, n, sc, tm, waits):
            nb = n // 32
            s3 = src.rearrange("p (b k) -> p b k", k=32)
            d3 = dst.rearrange("p (b k) -> p b k", k=32)
            am, iv = sc[:, 0:nb], sc[:, 32:32 + nb]
            t = V(waits, ve.tensor_reduce, am, s3, AX.X, ALU.max, apply_absolute_value=True)
            t = V(t, ve.tensor_scalar, am, am, 1.0 / 448.0, 1e-30, ALU.mult, ALU.max)
            t = V(t, ve.reciprocal, iv, am)
            t = V(t, ve.tensor_tensor, d3, s3, bc(iv, 2, [128, nb, 32]), ALU.mult)
            yield
            t = V(t, ve.tensor_scalar, tm.bitcast(U32), dst.bitcast(U32), 0x7f800000, None, ALU.bitwise_and)
            t = V(t, ve.tensor_scalar, tm, tm, 1572864.0, 24576.0, ALU.mult, ALU.max)
            t = V(t, ve.tensor_tensor, dst, dst, tm, ALU.add)
            t = V(t, ve.tensor_tensor, dst, dst, tm, ALU.subtract)
            yield
            t = V(t, ve.tensor_tensor, d3, d3, bc(am, 2, [128, nb, 32]), ALU.mult)
            s_.t_q = t
            return t

        def mx_prep(s, blk):
            w = W[7]
            raw = w["raw"].rearrange("p a n -> p (a n)")
            bk = s.bk
            q = s.ar[:, 0:1024]
            t = yield from quant(s, raw[:, blk * 1024:(blk + 1) * 1024], q, 1024, s.sm[:, 32:96], s.ar[:, 1024:2048],
                                 [s.done, w["t"]])
            for i in range(2):
                for c in range(4 * i, 4 * i + 4):
                    tt = T([t, s.bf[i], t_const], te.transpose, bk[i][:, (c % 4) * 128:(c % 4 + 1) * 128],
                           q[:, c * 128:(c + 1) * 128], ident, inc=(c % 4 == 3))
                src = bk[i][:, :].rearrange("p (r k n) -> p k r n", r=2, k=2)
                if blk < 4:
                    r = 4 * (blk % 2) + 2 * i
                    dst = (w["g"], w["u"])[blk // 2][:, :, r * 128:(r + 2) * 128].rearrange("p k (r n) -> p k r n", r=2)
                else:
                    src = bk[i][:, :].rearrange("p (c n) -> p c n", c=4)
                    dst = w["d"][:, 4 * i:4 * i + 4, (blk - 4) * 128:(blk - 3) * 128]
                s.bf[i] = S(tt, se.copy, dst, src)
            w.setdefault("tp", []).append(s.bf[1])
            s.done = [s.done, tt, s.t_q, s.bf[0], s.bf[1]]
            yield

        def mx(s, b):
            w = W[7]
            bk = s.bk
            t_ln = ln(s, b)
            yield
            t = yield from quant(s, s.xn[:, :], s.xn[:, :], 256, s.sm[:, 32:96], s.ar[:, 0:256], [t_ln, s.done])
            t_xT = xpose(s, t)
            yield
            g = s.ar[:, 0:1024]
            h = s.ar[:, 1024:2048]
            tm = s.ar[:, 2048:3072]
            hT = s.ar[:, 3072:4096].rearrange("p (k n) -> p k n", k=8)
            t_b = [t_xT, s.done]
            for c in range(2):
                for q, wm in ((0, w["g"]), (1, w["u"])):
                    for k in range(2):
                        t = T([t_xT, w["tp"], s.bf[q]], te.matmul, bk[q][:, :], s.xT[:, k, :],
                              wm[:, k, c * 512:(c + 1) * 512], start=(k == 0), stop=(k == 1), inc=(k == 1))
                t1 = s.bf[0] = S([t, t_b], se.activation, g[:, c * 512:(c + 1) * 512], bk[0][:, :], ACT.Silu)
                t2 = s.bf[1] = V([t1, t_b, t], ve.tensor_tensor, h[:, c * 512:(c + 1) * 512], g[:, c * 512:(c + 1) * 512],
                                 bk[1][:, :], ALU.mult)
                yield
            t = yield from quant(s, h, h, 1024, s.sm[:, 32:96], tm, t2)
            yield
            for c in range(2):
                for k in range(4):
                    tt = T([t, s.bf[c]], te.transpose, bk[c][:, k * 128:(k + 1) * 128], h[:, (4 * c + k) * 128:(4 * c + k + 1) * 128],
                           ident, inc=(k == 3))
                s.bf[c] = S([tt, t_b], se.copy, hT[:, 4 * c:4 * c + 4, :], bk[c][:, :].rearrange("p (k n) -> p k n", k=4))
            t = s.bf[1]
            yield
            for k in range(8):
                t = T([t, s.bf[0]], te.matmul, bk[0][:, 0:256], hT[:, k, :], w["d"][:, k, :], start=(k == 0), stop=(k == 7),
                      inc=(k == 7))
            t = s.bf[0] = add_x(s, b, bk[0][:, 0:256], t)
            s.done = t
            s.x_t[b] = t
            yield

        x_t = {b: [t_x0] for b in range(NB)}
        for s in slots:
            s.x_t = x_t
        load_weights(SUBS[0], None)
        ts = load_small()
        t_gp = V([ts], ve.tensor_tensor, gp[:, :], gqk[:, 0:1], gqk[:, 1:2], ALU.mult)
        if len(SUBS) > 1:
            load_weights(SUBS[1], None if SUBS[1] % 2 != SUBS[0] % 2 else [s.done for s in slots])
        todo = [list(range(NB)) for _ in SUBS]
        through = [0] * NB
        left = [NS] * len(SUBS)
        blocks = list(range(6))
        MORE = "more"

        busy = [False]

        def ahead(s, k):
            if k == 5 and "started" not in W[5]:
                W[5]["started"] = True
                yield from tern_prep(s)
            if k == 7 and blocks:
                yield from mx_prep(s, blocks.pop(0))

        def worker(s):
            for n, k in enumerate(SUBS):
                while W[k] is None:
                    yield MORE
                if k in (0, 4):
                    yield from small_init(s, 0 if k == 0 else 2)
                if k == 5:
                    yield from ahead(s, 5)
                    while "tq" not in W[5]:
                        yield MORE
                if k == 7:
                    while blocks:
                        yield from ahead(s, 7)
                    while len(W[7].get("tp", ())) < 6:
                        yield MORE
                while todo[n]:
                    b = next((b for b in todo[n] if through[b] == n), None)
                    if b is None:
                        yield MORE
                        continue
                    todo[n].remove(b)
                    if k in (0, 4):
                        yield from small_attn(s, b, 0 if k == 0 else 2)
                    if k in (2, 6):
                        yield from big_attn(s, b, 1 if k == 2 else 3)
                    if k == 1:
                        yield from peer(s, b)
                    if k == 3:
                        yield from moe(s, b)
                    if k == 5:
                        yield from tern(s, b)
                    if k == 7:
                        yield from mx(s, b)
                    through[b] = n + 1
                    if k in (4, 6) and n + 1 < len(SUBS) and W[k + 1] is not None and not busy[0]:
                        busy[0] = True
                        yield from ahead(s, k + 1)
                        busy[0] = False
                left[n] -= 1
                ends[n] = ends.get(n, []) + [s.done]
                if left[n] == 0 and n + 2 < len(SUBS):
                    load_weights(SUBS[n + 2], ends[n])

        ends = {}
        ready = [[float(s.i), worker(s)] for s in slots]
        while ready:
            r = min(ready, key=lambda e: e[0])
            clock["last"] = 0.0
            try:
                if next(r[1]) == MORE:
                    r[0] = min([e[0] for e in ready if e is not r] + [1e12]) + 1.0
                else:
                    r[0] = clock["last"]
            except StopIteration:
                ready.remove(r)

        for u in range(NB):
            t = st_o([x_t[u]], out[u], x[:, u, :])
        D([t], nc.sync.nop, inc=0)

        block = ctx.enter_context(nc.Block())

        @block.sync
        def _(eng):
            D.run(eng)

        @block.vector
        def _(eng):
            V.run(eng)

        @block.scalar
        def _(eng):
            S.run(eng)

        @block.tensor
        def _(eng):
            T.run(eng)

        @block.gpsimd
        def _(eng):
            P.run(eng)


_PLAIN = ["L0_xattn_Wq", "L0_xattn_Wkv", "L0_xattn_Wout", "L0_xattn_bout", "L0_ffn_Wq", "L0_ffn_e_up",
          "L1_xattn_Wq", "L1_xattn_Wk", "L1_xattn_Wv", "L1_xattn_Wo", "L1_ffn_Wr", "L1_ffn_br",
          "L1_ffn_gate_bias", "L1_ffn_Wup", "L1_ffn_Wgate", "L1_ffn_Wdown", "L1_ffn_Wsu", "L1_ffn_Wsg",
          "L1_ffn_Wsd", "L2_xattn_Wq", "L2_xattn_bq", "L2_xattn_Wk", "L2_xattn_bk", "L2_xattn_Wv",
          "L2_xattn_bv", "L2_xattn_Wkv_dca", "L2_xattn_bkv_dca", "L2_xattn_qn_w", "L2_xattn_qn_b",
          "L2_xattn_kn_w", "L2_xattn_kn_b", "L2_xattn_kn_dca_w", "L2_xattn_kn_dca_b", "L2_xattn_Wo",
          "L2_xattn_bo", "L3_xattn_Wq", "L3_xattn_Wk", "L3_xattn_Wv", "L3_xattn_Wo", "L3_ffn_gate_w",
          "L3_ffn_up_w", "L3_ffn_down_w"]


def _constants():
    c = np.zeros((128, C_N), np.float32)
    c[:, C_ID:C_ID + 128] = np.eye(128)
    c[:, C_I128:C_I128 + 128] = np.arange(128)
    c[:, C_I64:C_I64 + 64] = np.arange(64)
    c[:, C_I8:C_I8 + 8] = np.arange(8)
    p = np.arange(128)
    c[:, C_MM] = p < 112
    c[:, C_MD] = p >= 112
    c[:, C_PC] = 16 * (p // 32)
    c[:, C_ONE:C_ONE + 128] = 1
    return c


def kernel(**inputs):
    import concourse.bacc as _bacc
    from concourse.bass_utils import run_bass_kernel_spmd as _run

    I = {k: np.asarray(v) for k, v in inputs.items()}
    a = {n: I[n] for n in _PLAIN}
    a["x"] = I["x"]
    a["fside"] = I["fside_BxSx2_0"]
    a["ctxT"] = I["ctx_1024"].reshape(2048, 128).T
    a["maskT"] = I["mask_BxS2_bf1"].T.view(np.uint8) if I["mask_BxS2_bf1"].dtype == np.bool_ else I["mask_BxS2_bf1"].T
    a["edT"] = I["L0_ffn_e_down"].T
    a["keysT"] = I["L0_ffn_keys"].transpose(2, 3, 0, 1).reshape(128, 4, 128)
    bup = np.concatenate([I["L1_ffn_bup"], I["L1_ffn_bsu"][None]], 0)
    bga = np.concatenate([I["L1_ffn_bgate"], I["L1_ffn_bsg"][None]], 0)
    a["bugT"] = np.stack([bup.reshape(16, 128).T, bga.reshape(16, 128).T], 1)
    a["bdown"] = np.concatenate([I["L1_ffn_bdown"], I["L1_ffn_bsd"][None]], 0)
    a["w1T"], a["w3T"], a["w2T"] = I["L2_ffn_w1"].T, I["L2_ffn_w3"].T, I["L2_ffn_w2"].T
    kv = np.concatenate([I["L2_xattn_Wk"], I["L2_xattn_Wv"]], 1).reshape(128, 16, 2, 16)
    a["L2_xattn_Wk"], a["L2_xattn_Wv"] = kv[:, :, 0].reshape(128, 256), kv[:, :, 1].reshape(128, 256)
    bkv = np.concatenate([I["L2_xattn_bk"], I["L2_xattn_bv"]]).reshape(16, 2, 16)
    a["L2_xattn_bk"], a["L2_xattn_bv"] = bkv[:, 0].reshape(256), bkv[:, 1].reshape(256)
    a["gqk"] = np.stack([I["L3_xattn_gq"], I["L3_xattn_gk"]], 1)
    a["consts"] = _constants()

    nc = _bacc.Bacc("TRN2", target_bir_lowering=False, num_devices=1)
    arrays, aps = {}, {}
    for name, v in a.items():
        v = np.ascontiguousarray(v)
        arrays[f"in_{name}"] = v
        aps[name] = nc.dram_tensor(f"in_{name}", v.shape, mybir.dt.from_np(v.dtype), kind="ExternalInput").ap()
    o = nc.dram_tensor("out_0", (16, 128, 256), F32, kind="ExternalOutput").ap()
    program(nc, aps, o)
    return _run(nc, [arrays], core_ids=[0]).results[0]["out_0"]
```
